# Optimizing a Trainium2 kernel written in Bass

```python
import numpy as np
import jax
import jax.numpy as jnp

def _softmax(x, axis=-1):
    return jax.nn.softmax(x, axis=axis)

def _gelu(x):
    return jax.nn.gelu(x, approximate=True)

def _silu(x):
    return jax.nn.silu(x)

def _sigmoid(x):
    return jax.nn.sigmoid(x)

def _layernorm(x, axis=-1, eps=1e-05):
    m = jnp.mean(x, axis=axis, keepdims=True)
    v = jnp.var(x, axis=axis, keepdims=True)
    return (x - m) / jnp.sqrt(v + eps)

def _scatter_add(tgt, idx, src, axis=0):
    return tgt.at[idx].add(src)

def _segment_sum(src, seg, n):
    return jax.ops.segment_sum(src, seg, n)
kernel_name = 'mk_gnn_resnorm_d4_gnn_r32_c984d5'

def setup_inputs(seed: int=0):
    np.random.seed(seed)
    _w = jnp.asarray

    def _rec_inputs():
        import jax
        import jax.numpy as jnp
        _gk = jax.random.key(seed)
        x = -0.0009044 + 1 * jax.random.normal(jax.random.fold_in(_gk, 1), (3125, 32), jnp.float32)
        src = jax.random.randint(jax.random.fold_in(_gk, 2), (100000,), 0, 3125, jnp.int32)
        dst = jax.random.randint(jax.random.fold_in(_gk, 3), (100000,), 0, 3125, jnp.int32)
        _o = jnp.argsort(dst, stable=True)
        src = src[_o]
        dst = dst[_o]
        edge_type_86 = jax.random.randint(jax.random.fold_in(_gk, 13), (100000,), 0, 86, jnp.int32)
        return (x, src, dst, edge_type_86)
    x, src, dst, edge_type_86 = _rec_inputs()

    def _L0_gnn_setup():
        import jax, jax.numpy as jnp
        import numpy as np
        N_NODES = 50000
        N_EDGES = 25000
        INP_DIM = 32
        OUT_DIM = 32
        ATTN_DIM = 32
        NUM_RELS = 86
        NUM_BASES = 16
        GAMMA = 0.0
        key = jax.random.key(seed)
        ks = jax.random.split(key, 12)
        return {'h': jax.random.normal(ks[0], (N_NODES, INP_DIM), jnp.float32), 'weight': jax.random.normal(ks[1], (NUM_BASES, INP_DIM, OUT_DIM), jnp.float32), 'w_comp': jax.random.normal(ks[2], (NUM_RELS, NUM_BASES), jnp.float32), 'self_loop_weight': jax.random.normal(ks[3], (INP_DIM, OUT_DIM), jnp.float32), 'A1_w': jax.random.normal(ks[4], (ATTN_DIM, INP_DIM), jnp.float32), 'A1_b': jax.random.normal(ks[5], (ATTN_DIM,), jnp.float32), 'A2_w': jax.random.normal(ks[6], (ATTN_DIM, INP_DIM), jnp.float32), 'A2_b': jax.random.normal(ks[7], (ATTN_DIM,), jnp.float32), 'rel_emb': jax.random.normal(ks[8], (NUM_RELS, ATTN_DIM), jnp.float32), 'src': jax.random.randint(ks[9], (N_EDGES,), 0, N_NODES, jnp.int32), 'dst': jax.random.randint(ks[10], (N_EDGES,), 0, N_NODES, jnp.int32), 'etype': jax.random.randint(ks[11], (N_EDGES,), 0, NUM_RELS, jnp.int32)}
    _L0_gnn_all = _L0_gnn_setup()
    _L0_gnn_in = {k: v for k, v in _L0_gnn_all.items() if k in ('weight', 'w_comp', 'self_loop_weight', 'A1_w', 'A1_b', 'A2_w', 'A2_b', 'rel_emb')}
    del _L0_gnn_all

    def _L1_gnn_setup():
        import jax, jax.numpy as jnp
        import numpy as np
        N_NODES = 50000
        N_EDGES = 50000
        D_FEAT = 32
        key = jax.random.key(seed)
        kx, ke = jax.random.split(key)
        x = jax.random.normal(kx, (N_NODES, D_FEAT), dtype=jnp.float32)
        edge_index = jax.random.randint(ke, (2, N_EDGES), 0, N_NODES, dtype=jnp.int64)
        return {'x': x, 'edge_index': edge_index, 'num_nodes': N_NODES}
    _L1_gnn_all = _L1_gnn_setup()
    _L1_gnn_in = {k: v for k, v in _L1_gnn_all.items() if k in ()}
    del _L1_gnn_all

    def _L2_gnn_setup():
        import jax, jax.numpy as jnp
        import numpy as np
        N_NODES = 3125
        N_EDGES = 50000
        DIM1 = 32
        LEAKY_SLOPE = 0.01
        key = jax.random.key(seed)
        k1, k2, k3, k4 = jax.random.split(key, 4)
        h = jax.random.normal(k1, (N_NODES, DIM1), dtype=jnp.float32)
        attn_w = jax.random.normal(k2, (2 * DIM1,), dtype=jnp.float32) * (1.0 / np.sqrt(2 * DIM1))
        src = jax.random.randint(k3, (N_EDGES,), 0, N_NODES, dtype=jnp.int32)
        dst = jax.random.randint(k4, (N_EDGES,), 0, N_NODES, dtype=jnp.int32)
        return {'h': h, 'attn_w': attn_w, 'src': src, 'dst': dst}
    _L2_gnn_all = _L2_gnn_setup()
    _L2_gnn_in = {k: v for k, v in _L2_gnn_all.items() if k in ('attn_w',)}
    del _L2_gnn_all

    def _L3_gnn_setup():
        import jax, jax.numpy as jnp
        import numpy as np
        N_NODES = 3125
        N_EDGES = 50000
        D_FEAT = 32
        K = 10
        ALPHA = 0.1
        key = jax.random.key(seed)
        k1, k2, k3 = jax.random.split(key, 3)
        feat = jax.random.normal(k1, (N_NODES, D_FEAT), dtype=jnp.float32)
        src = jax.random.randint(k2, (N_EDGES,), 0, N_NODES, dtype=jnp.int64)
        dst = jax.random.randint(k3, (N_EDGES,), 0, N_NODES, dtype=jnp.int64)
        return {'feat': feat, 'src': src, 'dst': dst}
    _L3_gnn_all = _L3_gnn_setup()
    _L3_gnn_in = {k: v for k, v in _L3_gnn_all.items() if k in ()}
    del _L3_gnn_all
    return {'x': x, 'src': src, 'dst': dst, 'edge_type_86': edge_type_86, 'L0_gnn_weight': _L0_gnn_in['weight'], 'L0_gnn_w_comp': _L0_gnn_in['w_comp'], 'L0_gnn_self_loop_weight': _L0_gnn_in['self_loop_weight'], 'L0_gnn_A1_w': _L0_gnn_in['A1_w'], 'L0_gnn_A1_b': _L0_gnn_in['A1_b'], 'L0_gnn_A2_w': _L0_gnn_in['A2_w'], 'L0_gnn_A2_b': _L0_gnn_in['A2_b'], 'L0_gnn_rel_emb': _L0_gnn_in['rel_emb'], 'L2_gnn_attn_w': _L2_gnn_in['attn_w']}

def reference(x, src, dst, edge_type_86, L0_gnn_weight, L0_gnn_w_comp, L0_gnn_self_loop_weight, L0_gnn_A1_w, L0_gnn_A1_b, L0_gnn_A2_w, L0_gnn_A2_b, L0_gnn_rel_emb, L2_gnn_attn_w):
    import jax
    import jax.numpy as jnp

    def _L0_gnn_ref(h, weight, w_comp, self_loop_weight, A1_w, A1_b, A2_w, A2_b, rel_emb, src, dst, etype):
        import jax, jax.numpy as jnp
        import numpy as np
        N_NODES = 50000
        N_EDGES = 25000
        INP_DIM = 32
        OUT_DIM = 32
        ATTN_DIM = 32
        NUM_RELS = 86
        NUM_BASES = 16
        GAMMA = 0.0
        E = src.shape[0]
        N = h.shape[0]
        x = h[src]
        y = h[dst]
        c = w_comp[etype]
        xb = jnp.einsum('ei,bio->ebo', x, weight)
        msg = jnp.einsum('eb,ebo->eo', c, xb)
        x_hat = x @ A1_w.T + A1_b
        y_hat = y @ A2_w.T + A2_b + rel_emb[etype]
        scale = jnp.sqrt(jnp.asarray(INP_DIM, h.dtype))
        a = jnp.tanh(jax.nn.relu(jnp.sum(x_hat * y_hat, axis=-1) / scale))
        a = jnp.where(a > GAMMA, a, jnp.zeros_like(a))
        nei = jax.ops.segment_sum(a[:, None] * msg, dst, num_segments=N)
        last_e = jax.ops.segment_max(jnp.arange(E, dtype=jnp.int32), dst, num_segments=N)
        last_e = jnp.clip(last_e, 0, E - 1)
        curr = h[src[last_e]] @ self_loop_weight
        in_deg = jax.ops.segment_sum(jnp.ones((E,), h.dtype), dst, num_segments=N)
        h_new = jnp.where((in_deg > 0)[:, None], nei + curr, jnp.zeros_like(nei))
        return jax.nn.relu(h_new)

    def _L1_gnn_ref(x, edge_index, num_nodes):
        import jax, jax.numpy as jnp
        import numpy as np
        N_NODES = 50000
        N_EDGES = 50000
        D_FEAT = 32
        src = edge_index[0]
        dst = edge_index[1]
        msgs = x[src]
        out = jax.ops.segment_sum(msgs, dst, num_segments=num_nodes)
        return out

    def _L2_gnn_ref(h, attn_w, src, dst):
        import jax, jax.numpy as jnp
        import numpy as np
        N_NODES = 3125
        N_EDGES = 50000
        DIM1 = 32
        LEAKY_SLOPE = 0.01
        N, d = h.shape
        s_src = h @ attn_w[:d]
        s_dst = h @ attn_w[d:]
        e = s_src[src] + s_dst[dst]
        e = jnp.where(e >= 0, e, LEAKY_SLOPE * e)
        m = jax.ops.segment_max(e, dst, num_segments=N)
        ex = jnp.exp(e - m[dst])
        denom = jax.ops.segment_sum(ex, dst, num_segments=N)
        alpha = ex / denom[dst]
        out = jax.ops.segment_sum(h[src] * alpha[:, None], dst, num_segments=N)
        return out

    def _L3_gnn_ref(feat, src, dst):
        import jax, jax.numpy as jnp
        import numpy as np
        N_NODES = 3125
        N_EDGES = 50000
        D_FEAT = 32
        K = 10
        ALPHA = 0.1
        n = feat.shape[0]
        ones = jnp.ones(src.shape[0], dtype=feat.dtype)
        out_deg = jax.ops.segment_sum(ones, src, num_segments=n)
        in_deg = jax.ops.segment_sum(ones, dst, num_segments=n)
        src_norm = jnp.clip(out_deg, 1.0, None) ** (-0.5)
        dst_norm = jnp.clip(in_deg, 1.0, None) ** (-0.5)
        feat0 = feat

        def step(f, _):
            f = f * src_norm[:, None]
            agg = jax.ops.segment_sum(f[src], dst, num_segments=n)
            f = agg * dst_norm[:, None]
            f = (1.0 - ALPHA) * f + ALPHA * feat0
            return (f, None)
        feat, _ = jax.lax.scan(step, feat, None, length=K)
        return feat
    edge_index = jnp.stack([src, dst])
    x = _layernorm(x + _L0_gnn_ref(x, L0_gnn_weight, L0_gnn_w_comp, L0_gnn_self_loop_weight, L0_gnn_A1_w, L0_gnn_A1_b, L0_gnn_A2_w, L0_gnn_A2_b, L0_gnn_rel_emb, src, dst, edge_type_86), axis=-1)
    x = _layernorm(x + _L1_gnn_ref(x, edge_index, 3125), axis=-1)
    x = _layernorm(x + _L2_gnn_ref(x, L2_gnn_attn_w, src, dst), axis=-1)
    x = _layernorm(x + _L3_gnn_ref(x, src, dst), axis=-1)
    return x

_drawn_inputs = setup_inputs


def setup_inputs(seed=0):
    import zlib

    import numpy as np

    out = dict(_drawn_inputs(seed))
    spreads = {}
    factors = {}
    for name, (base, spread) in spreads.items():
        noise = np.random.default_rng([zlib.crc32(name.encode()), seed]).standard_normal(out[name].shape)
        drawn = base * np.exp(spread * noise) if base else spread * noise
        out[name] = jnp.asarray(drawn.astype(out[name].dtype))
    for name, factor in factors.items():
        out[name] = (out[name] * factor).astype(out[name].dtype)
    return out
```

```python
from contextlib import ExitStack
from math import sqrt

import concourse.bass as bass
from concourse import mybir

F32, I32 = mybir.dt.float32, mybir.dt.int32
ALU, ACT, AX = mybir.AluOpType, mybir.ActivationFunctionType, mybir.AxisListType

P = 128
NODES, FEAT = 3125, 32
BLOCKS = -(-NODES // P)
NODES_PAD = BLOCKS * P
EDGES = 100000
TILES = -(-EDGES // P)
EDGES_PAD = TILES * P
RELS, BASES = 86, 16
ROW = 64
BANK = 512
CHUNKS = [(c, min(BANK, NODES - c)) for c in range(0, NODES, BANK)]
STEPS, ALPHA = 10, 0.1
SLOPE, EPS = 0.01, 1e-5
FAR = 1e30
REL_ROW = FEAT + FEAT * FEAT

P_REL, P_SUM, P_MAX, P_SOFT, P_OUTDEG, P_PROP = range(6)
ROWS_GATHERED = {P_REL: 3, P_SUM: 1, P_MAX: 2, P_SOFT: 2, P_OUTDEG: 0, P_PROP: 1}
SUM_COLS = {P_REL: FEAT, P_SUM: FEAT + 1, P_SOFT: FEAT + 1, P_OUTDEG: 1, P_PROP: FEAT}


def rows_of(b):
    return min(P, NODES - b * P)


class Chain:

    def __init__(self, eng, sem):
        self.eng, self.sem, self.count, self.loops = eng, sem, 0, []

    def value(self):
        total = self.count
        for var, per_turn, _, _ in self.loops:
            total = var * per_turn + total
        return total

    def link(self, instruction):
        instruction.then_inc(self.sem, 1)
        self.count += 1
        self.eng.wait_ge(self.sem, self.value())

    def enter(self, var, turns, per_turn):
        self.loops.append((var, per_turn, turns, self.count))

    def leave(self):
        _, per_turn, turns, start = self.loops.pop()
        assert self.count - start == per_turn, (self.count - start, per_turn)
        self.count = start + turns * per_turn


def gnn(nc, x_pad, edges, weight, w_comp_t, self_loop, a1_t, a2_t, rel_emb, attn_w, out):
    ctx = ExitStack()
    with ctx:
        def sb(name, shape, dt=F32):
            return ctx.enter_context(nc.sbuf_tensor(name, shape, dt))

        def sem(name):
            return ctx.enter_context(nc.semaphore(name))

        feat_table = nc.dram_tensor("feat_table", [NODES_PAD, ROW], F32, kind="Internal").ap()
        dst_table = nc.dram_tensor("dst_table", [NODES_PAD, FEAT], F32, kind="Internal").ap()
        rel_table = nc.dram_tensor("rel_table", [RELS, REL_ROW], F32, kind="Internal").ap()

        x = sb("x", [P, BLOCKS, FEAT])
        x0 = sb("x0", [P, BLOCKS, FEAT])
        rows = sb("rows", [P, BLOCKS, ROW])
        dst_rows = sb("dst_rows", [P, BLOCKS, FEAT])
        agg = sb("agg", [P, BLOCKS, FEAT + 1])
        work = sb("work", [P, BLOCKS, FEAT])
        stat = sb("stat", [P, 4, BLOCKS])
        src_norm = sb("src_norm", [P, BLOCKS])
        dst_norm = sb("dst_norm", [P, BLOCKS])
        xT = sb("xT", [FEAT + 1, NODES_PAD])
        a1 = sb("a1", [FEAT + 1, FEAT])
        a2 = sb("a2", [FEAT + 1, FEAT])
        wc = sb("wc", [BASES, RELS])
        wb = sb("wb", [BASES, FEAT * FEAT])
        sl = sb("sl", [FEAT, FEAT])
        attn = sb("attn", [P, 2 * FEAT])
        rel_rows = sb("rel_rows", [RELS, REL_ROW])
        ident = sb("ident", [P, P])
        eps = sb("eps", [P, 1])
        edge = sb("edge", [P, 3], I32)
        src_row = sb("src_row", [P, ROW])
        dst_row = sb("dst_row", [P, FEAT])
        rel_row = sb("rel_row", [P, REL_ROW])
        prod = sb("prod", [P, FEAT, FEAT])
        score = sb("score", [P, 4])
        edge_no = sb("edge_no", [P, 1])
        val = sb("val", [P, FEAT + 1])
        node_no = sb("node_no", [P, NODES])
        hot = sb("hot", [P, NODES])
        top = sb("top", [P, NODES])
        aggT = sb("aggT", [FEAT + 1, NODES])
        zeros = sb("zeros", [P, BANK])
        last_no = sb("last_no", [P, BLOCKS], I32)
        last_edge = sb("last_edge", [P, BLOCKS, 3], I32)
        last_src = sb("last_src", [P, BLOCKS], I32)
        last_row = sb("last_row", [P, BLOCKS, ROW])
        lastT = sb("lastT", [FEAT, NODES_PAD])

        ps = ctx.enter_context(nc.psum_tensor("ps", [P, 8 * BANK], F32))
        per_bank = BANK // ROW

        def ps_block(b, cols, n=P, first_bank=0):
            at = first_bank * BANK + b * ROW
            return ps[0:n, at:at + cols]

        def ps_blocks(cols, b0, b1, n=P):
            return ps[0:n, b0 * ROW:b1 * ROW].rearrange("p (b c) -> p b c", c=ROW)[:, :, 0:cols]

        inputs_loaded = sem("inputs_loaded")
        constants_made = sem("constants_made")
        vector_steps = sem("vector_steps")
        turns, vector_turns = sem("turns"), sem("vector_turns")
        xT_out, xT_ready = sem("xT_out"), sem("xT_ready")
        projected, projections_copied = sem("projected"), sem("projections_copied")
        relations_out = sem("relations_out")
        table_ready = [sem(f"table_ready_{p}") for p in range(6)]
        table_stored = sem("table_stored")
        edge_in = sem("edge_in")
        rows_in = [sem(f"rows_in_{p}") for p in range(6)]
        rows_in_cleared = sem("rows_in_cleared")
        score_out, weight_out = sem("score_out"), sem("weight_out")
        tile_ready = sem("tile_ready")
        tile_done = sem("tile_done")
        sums_out, sums_copied, nodes_out = sem("sums_out"), sem("sums_copied"), sem("nodes_out")
        top_ready, top_out, top_copied = sem("top_ready"), sem("top_out"), sem("top_copied")
        last_ready, last_in = sem("last_ready"), sem("last_in")
        lastT_out, lastT_ready, current_out = sem("lastT_out"), sem("lastT_ready"), sem("current_out")
        root_in, root_out = sem("root_in"), sem("root_out")
        result_ready, stored = sem("result_ready"), sem("stored")

        LOADS = 8
        serial = {p: p * TILES for p in range(6)}
        summed = [p for p in range(6) if p != P_MAX]
        nth_sum = {p: n + 1 for n, p in enumerate(summed)}
        TABLES = {P_REL: 3, P_SUM: 4, P_MAX: 6, P_SOFT: 7, P_OUTDEG: 7, P_PROP: 8}

        block = ctx.enter_context(nc.Block())

        @block.sync
        def _(sp):
            for dst, src in ((x[:], x_pad.rearrange("(b p) f -> p b f", p=P)), (a1[:], a1_t), (a2[:], a2_t),
                             (wc[:], w_comp_t), (wb[:], weight), (sl[:], self_loop),
                             (attn[:], attn_w.to_broadcast([P, 2 * FEAT])), (rel_rows[:, 0:FEAT], rel_emb)):
                sp.dma_start(dst, src).then_inc(inputs_loaded, 16)
            table = feat_table.rearrange("(b p) c -> p b c", p=P)
            dtable = dst_table.rearrange("(b p) c -> p b c", p=P)

            def load_tiles(base):
                with sp.Fori(0, TILES) as t:
                    sp.wait_ge(tile_done, t + (base + 1))
                    sp.dma_start(edge[:], edges[bass.ds(t * P, P), :]).then_inc(edge_in, 16)

            for p in range(P_PROP):
                sp.wait_ge(table_ready[p], 1)
                if p in (P_REL, P_SUM, P_MAX):
                    sp.dma_start(table, rows[:]).then_inc(table_stored, 16)
                if p in (P_REL, P_MAX, P_SOFT):
                    sp.dma_start(dtable, dst_rows[:]).then_inc(table_stored, 16)
                if p == P_REL:
                    sp.dma_start(rel_table, rel_rows[:]).then_inc(table_stored, 16)
                load_tiles(serial[p])
            with sp.Fori(0, STEPS) as s:
                sp.wait_ge(table_ready[P_PROP], s + 1)
                sp.dma_start(table, rows[:]).then_inc(table_stored, 16)
                load_tiles(s * TILES + serial[P_PROP])
            sp.wait_ge(result_ready, 1)
            sp.dma_start(out.rearrange("(b p) f -> p b f", p=P), x[:]).then_inc(stored, 16)
            sp.wait_ge(stored, 16)

        @block.gpsimd
        def _(pool):
            pool.iota(node_no[:], pattern=[[1, NODES]], base=0, channel_multiplier=0,
                      allow_small_or_imprecise_dtypes=True).then_inc(constants_made, 1)
            pool.iota(edge_no[:], pattern=[[1, 1]], base=1 - P, channel_multiplier=1,
                      allow_small_or_imprecise_dtypes=True).then_inc(constants_made, 1)
            pool.memset(ident[:], 0.0).then_inc(constants_made, 1)
            pool.wait_ge(constants_made, 3)
            pool.affine_select(out=ident[:], in_=ident[:], compare_op=ALU.not_equal, fill=1.0, base=0,
                               pattern=[[-1, P]], channel_multiplier=1).then_inc(constants_made, 1)

            def gather(to, table, index, done):
                pool.indirect_dma_start(to, None, table, bass.IndirectOffsetOnAxis(ap=index, axis=0)).then_inc(done, 16)

            def hold():
                pool.sem_inc(turns, 1)

            def gather_tiles(p, tile, step=None):
                with pool.Fori(0, TILES) as t:
                    pool.wait_ge(edge_in, (t + tile) * 16 + 16)
                    hold()
                    gather(src_row[:], feat_table, edge[:, 0:1], rows_in[p])
                    if ROWS_GATHERED[p] >= 2:
                        gather(dst_row[:], dst_table, edge[:, 1:2], rows_in[p])
                    if ROWS_GATHERED[p] >= 3:
                        gather(rel_row[:], rel_table, edge[:, 2:3], rows_in[p])

            for p in range(P_PROP):
                if ROWS_GATHERED[p]:
                    pool.wait_ge(table_stored, 16 * TABLES[p])
                    gather_tiles(p, serial[p])
                if p == P_REL:
                    pool.wait_ge(last_ready, 1)
                    for b in range(BLOCKS):
                        gather(last_edge[:, b, :], edges, last_no[:, b:b + 1], last_in)
                    pool.wait_ge(last_ready, 2)
                    for b in range(BLOCKS):
                        gather(last_row[:, b, :], feat_table, last_src[:, b:b + 1], last_in)
            with pool.Fori(0, STEPS) as s:
                pool.wait_ge(table_stored, s * 16 + 16 * TABLES[P_PROP])
                hold()
                n = rows_in[P_PROP].num
                pool.dma_reset(range(n, n + 1))
                pool.sem_clear(rows_in[P_PROP])
                pool.sem_inc(rows_in_cleared, 1)
                gather_tiles(P_PROP, s * TILES + serial[P_PROP])

        @block.tensor
        def _(pe):
            pe.wait_ge(inputs_loaded, 16 * LOADS)
            pe.wait_ge(constants_made, 4)
            for b in range(BLOCKS):
                mm = nc.tensor.matmul(ps[0:FEAT, b * P:(b + 1) * P], x[:, b, :], ident[:], start=True, stop=True)
            mm.then_inc(xT_out, 1)
            pe.wait_ge(xT_ready, 1)
            for b in range(BLOCKS):
                blk = xT[:, b * P:(b + 1) * P]
                nc.tensor.matmul(ps_block(b, FEAT), blk, a1[:], start=True, stop=True)
                mm = nc.tensor.matmul(ps_block(b, FEAT, first_bank=4), blk, a2[:], start=True, stop=True)
            mm.then_inc(projected, 1)
            pe.wait_ge(projections_copied, 1)
            for c in range(FEAT * FEAT // BANK):
                mm = nc.tensor.matmul(ps[0:RELS, c * BANK:(c + 1) * BANK], wc[:], wb[:, c * BANK:(c + 1) * BANK],
                                      start=True, stop=True)
            mm.then_inc(relations_out, 1)
            pe.sem_inc(tile_done, 1)

            def edge_sums(p, tile):
                cols = SUM_COLS[p]
                for c, w in CHUNKS:
                    nc.tensor.matmul(ps[0:cols, c:c + w], zeros[:, 0:cols], zeros[:, 0:w], start=True, stop=False)
                with pe.Fori(0, TILES) as t:
                    pe.wait_ge(tile_ready, t + tile + 1)
                    for c, w in CHUNKS:
                        mm = nc.tensor.matmul(ps[0:cols, c:c + w], val[:, 0:cols], hot[:, c:c + w],
                                              start=False, stop=False)
                    mm.then_inc(tile_done, 1)
                for c, w in CHUNKS:
                    mm = nc.tensor.matmul(ps[0:cols, c:c + w], zeros[:, 0:cols], zeros[:, 0:w], start=False, stop=True)
                mm.then_inc(sums_out, 1)

            def to_nodes(p, nth):
                pe.wait_ge(sums_copied, nth)
                cols = SUM_COLS[p]
                for b in range(BLOCKS):
                    mm = nc.tensor.matmul(ps_block(b, cols, rows_of(b)), aggT[0:cols, b * P:b * P + rows_of(b)],
                                          ident[0:cols, 0:cols], start=True, stop=True)
                mm.then_inc(nodes_out, 1)

            def top_to_nodes(nth):
                pe.wait_ge(top_ready, nth)
                for b in range(BLOCKS):
                    n = rows_of(b)
                    mm = nc.tensor.matmul(ps[0:n, b * P:(b + 1) * P], top[:, b * P:b * P + n], ident[:],
                                          start=True, stop=True)
                mm.then_inc(top_out, 1)

            for p in range(P_PROP):
                pe.wait_ge(table_ready[p], 1)
                if p != P_MAX:
                    edge_sums(p, (nth_sum[p] - 1) * TILES)
                    to_nodes(p, nth_sum[p])
                if p == P_REL:
                    top_to_nodes(1)
                    pe.wait_ge(last_in, 16 * 2 * BLOCKS)
                    pe.wait_ge(top_copied, 1)
                    for b in range(BLOCKS):
                        mm = nc.tensor.matmul(ps[0:FEAT, b * P:(b + 1) * P], last_row[:, b, 0:FEAT], ident[:],
                                              start=True, stop=True)
                    mm.then_inc(lastT_out, 1)
                    pe.wait_ge(lastT_ready, 1)
                    for b in range(BLOCKS):
                        mm = nc.tensor.matmul(ps_block(b, FEAT), lastT[:, b * P:(b + 1) * P], sl[:],
                                              start=True, stop=True)
                    mm.then_inc(current_out, 1)
                if p == P_MAX:
                    top_to_nodes(2)
            with pe.Fori(0, STEPS) as s:
                pe.wait_ge(table_ready[P_PROP], s + 1)
                edge_sums(P_PROP, s * TILES + (nth_sum[P_PROP] - 1) * TILES)
                to_nodes(P_PROP, s + nth_sum[P_PROP])

        @block.scalar
        def _(act):
            with act.Fori(0, TILES) as t:
                act.wait_ge(score_out, t + 1)
                nc.scalar.activation(score[:, 1:2], score[:, 0:1], ACT.Tanh, scale=1.0 / sqrt(FEAT))\
                   .then_inc(weight_out, 1)
            for n in (1, 2):
                act.wait_ge(root_in, n)
                nc.scalar.activation(stat[:, 2, :], stat[:, 1, :], ACT.Sqrt, bias=eps[:], scale=1.0 / FEAT)\
                   .then_inc(root_out, 1)
            with act.Fori(0, TILES) as t:
                act.wait_ge(score_out, t + (TILES + 1))
                nc.scalar.activation(score[:, 1:2], score[:, 0:1], ACT.Exp).then_inc(weight_out, 1)
            act.wait_ge(root_in, 3)
            nc.scalar.activation(stat[:, 2, :], stat[:, 1, :], ACT.Sqrt, bias=eps[:], scale=1.0 / FEAT)\
               .then_inc(root_out, 1)
            act.wait_ge(root_in, 4)
            nc.scalar.activation(src_norm[:], src_norm[:], ACT.Sqrt).then_inc(root_out, 1)
            nc.scalar.activation(dst_norm[:], dst_norm[:], ACT.Sqrt).then_inc(root_out, 1)
            act.wait_ge(root_in, 5)
            nc.scalar.activation(stat[:, 2, :], stat[:, 1, :], ACT.Sqrt, bias=eps[:], scale=1.0 / FEAT)\
               .then_inc(root_out, 1)

        @block.vector
        def _(dve):
            v = nc.vector
            chain = Chain(dve, vector_steps)
            link = chain.link

            def spread(per_node, cols):
                return per_node.unsqueeze(2).to_broadcast([P, BLOCKS, cols])

            def layer_norm(root_nth, roots):
                link(v.tensor_reduce(stat[:, 0, :], x[:], AX.X, ALU.add))
                link(v.tensor_scalar(stat[:, 0, :], stat[:, 0, :], -1.0 / FEAT, None, ALU.mult))
                link(v.tensor_tensor(x[:], x[:], spread(stat[:, 0, :], FEAT), ALU.add))
                link(v.tensor_tensor(work[:], x[:], x[:], ALU.mult))
                link(v.tensor_reduce(stat[:, 1, :], work[:], AX.X, ALU.add))
                dve.sem_inc(root_in, 1)
                dve.wait_ge(root_out, roots)
                link(v.reciprocal(stat[:, 3, :], stat[:, 2, :]))
                link(v.tensor_tensor(x[:], x[:], spread(stat[:, 3, :], FEAT), ALU.mult))

            def sums_to_nodes(p, nth):
                cols = SUM_COLS[p]
                dve.wait_ge(sums_out, nth)
                for c, w in CHUNKS:
                    link(v.tensor_copy(aggT[0:cols, c:c + w], ps[0:cols, c:c + w]))
                dve.sem_inc(sums_copied, 1)
                dve.wait_ge(nodes_out, nth)
                for b in range(0, BLOCKS, per_bank):
                    e = min(b + per_bank, BLOCKS - 1)
                    if e > b:
                        link(v.tensor_copy(agg[:, b:e, 0:cols], ps_blocks(cols, b, e)))
                n = rows_of(BLOCKS - 1)
                link(v.tensor_copy(agg[0:n, BLOCKS - 1:BLOCKS, 0:cols], ps_blocks(cols, BLOCKS - 1, BLOCKS, n)))

            def top_to_nodes(nth):
                dve.sem_inc(top_ready, 1)
                dve.wait_ge(top_out, nth)
                for b in range(BLOCKS):
                    n = rows_of(b)
                    link(v.tensor_reduce(stat[0:n, 3, b:b + 1], ps[0:n, b * P:(b + 1) * P], AX.X, ALU.max))
                dve.sem_inc(top_copied, 1)

            def one_hot():
                link(v.tensor_copy(score[:, 2:3], edge[:, 1:2]))
                link(v.tensor_scalar(hot[:], node_no[:], score[:, 2:3], None, ALU.is_equal))

            link(v.memset(zeros[:], 0.0))
            link(v.memset(agg[:], 0.0))
            link(v.memset(eps[:], EPS))
            link(v.memset(xT[FEAT:FEAT + 1, :], 1.0))
            link(v.memset(val[:], 1.0))
            link(v.memset(top[:], 0.0))
            link(v.memset(stat[:], 0.0))
            link(v.memset(dst_rows[:], 0.0))
            dve.wait_ge(inputs_loaded, 16 * LOADS)
            dve.wait_ge(constants_made, 4)
            dve.wait_ge(xT_out, 1)
            for c in range(0, NODES_PAD, BANK):
                w = min(BANK, NODES_PAD - c)
                link(v.tensor_copy(xT[0:FEAT, c:c + w], ps[0:FEAT, c:c + w]))
            dve.sem_inc(xT_ready, 1)
            link(v.tensor_copy(rows[:, :, 0:FEAT], x[:]))
            dve.wait_ge(projected, 1)
            for b in range(0, BLOCKS, per_bank):
                e = min(b + per_bank, BLOCKS)
                link(v.tensor_copy(rows[:, b:e, FEAT:ROW], ps_blocks(FEAT, b, e)))
                at = 4 * per_bank
                link(v.tensor_copy(dst_rows[:, b:e, :], ps_blocks(FEAT, at + b, at + e)))
            dve.sem_inc(projections_copied, 1)
            dve.wait_ge(relations_out, 1)
            for c in range(0, FEAT * FEAT, BANK):
                link(v.tensor_copy(rel_rows[:, FEAT + c:FEAT + c + BANK], ps[0:RELS, c:c + BANK]))
            dve.sem_inc(table_ready[P_REL], 1)

            with dve.Fori(0, TILES) as t:
                chain.enter(t, TILES, 12)
                dve.wait_ge(rows_in[P_REL], t * 48 + 48)
                link(v.tensor_tensor(prod[:, 0, :], dst_row[:], rel_row[:, 0:FEAT], ALU.add))
                link(v.tensor_tensor(prod[:, 0, :], prod[:, 0, :], src_row[:, FEAT:ROW], ALU.mult))
                link(v.tensor_reduce(score[:, 3:4], prod[:, 0, :], AX.X, ALU.add))
                link(v.tensor_scalar(score[:, 0:1], score[:, 3:4], 0.0, None, ALU.max))
                dve.sem_inc(score_out, 1)
                link(v.tensor_tensor(prod[:], rel_row[:, FEAT:].rearrange("p (i o) -> p o i", o=FEAT),
                                     src_row[:, 0:FEAT].unsqueeze(1).to_broadcast([P, FEAT, FEAT]), ALU.mult))
                link(v.tensor_reduce(val[:, 0:FEAT], prod[:], AX.X, ALU.add))
                link(v.tensor_scalar(edge_no[:], edge_no[:], float(P), None, ALU.add))
                one_hot()
                link(v.scalar_tensor_tensor(out=top[:], in0=hot[:], scalar=edge_no[:], in1=top[:],
                                            op0=ALU.mult, op1=ALU.max))
                dve.wait_ge(weight_out, t + 1)
                link(v.tensor_scalar(val[:, 0:FEAT], val[:, 0:FEAT], score[:, 1:2], None, ALU.mult))
                link(v.tensor_copy(score[:, 3:4], score[:, 1:2]))
                dve.sem_inc(tile_ready, 1)
                chain.leave()
            sums_to_nodes(P_REL, nth_sum[P_REL])
            top_to_nodes(1)
            link(v.tensor_scalar(stat[:, 0, :], stat[:, 3, :], 0.0, None, ALU.is_gt))
            link(v.tensor_scalar(stat[:, 3, :], stat[:, 3, :], -1.0, 0.0, ALU.add, ALU.max))
            link(v.tensor_copy(last_no[:], stat[:, 3, :]))
            dve.sem_inc(last_ready, 1)
            dve.wait_ge(last_in, 16 * BLOCKS)
            link(v.tensor_copy(last_src[:].unsqueeze(2), last_edge[:, :, 0:1]))
            dve.sem_inc(last_ready, 1)
            dve.wait_ge(lastT_out, 1)
            for c in range(0, NODES_PAD, BANK):
                w = min(BANK, NODES_PAD - c)
                link(v.tensor_copy(lastT[:, c:c + w], ps[0:FEAT, c:c + w]))
            dve.sem_inc(lastT_ready, 1)
            dve.wait_ge(current_out, 1)
            for b in range(0, BLOCKS, per_bank):
                e = min(b + per_bank, BLOCKS)
                link(v.tensor_tensor(work[:, b:e, :], agg[:, b:e, 0:FEAT], ps_blocks(FEAT, b, e), ALU.add))
            link(v.tensor_scalar(work[:], work[:], 0.0, None, ALU.max))
            link(v.tensor_tensor(work[:], work[:], spread(stat[:, 0, :], FEAT), ALU.mult))
            link(v.tensor_tensor(x[:], x[:], work[:], ALU.add))
            layer_norm(1, 1)
            link(v.tensor_copy(rows[:, :, 0:FEAT], x[:]))
            dve.sem_inc(table_ready[P_SUM], 1)

            def value_tiles(p):
                with dve.Fori(0, TILES) as t:
                    chain.enter(t, TILES, 3)
                    dve.wait_ge(rows_in[p], t * 16 + 16)
                    link(v.tensor_copy(val[:, 0:FEAT], src_row[:, 0:FEAT]))
                    one_hot()
                    dve.sem_inc(tile_ready, 1)
                    chain.leave()

            value_tiles(P_SUM)
            sums_to_nodes(P_SUM, nth_sum[P_SUM])
            link(v.tensor_scalar(dst_norm[:], agg[:, :, FEAT:FEAT + 1].rearrange("p b c -> p (b c)"), 1.0, None,
                                 ALU.max))
            link(v.tensor_tensor(x[:], x[:], agg[:, :, 0:FEAT], ALU.add))
            layer_norm(2, 2)

            link(v.tensor_copy(rows[:, :, 0:FEAT], x[:]))
            for half, to in ((0, rows[:, :, FEAT:FEAT + 1]), (1, dst_rows[:, :, 0:1])):
                w = attn[:, half * FEAT:(half + 1) * FEAT].unsqueeze(1).to_broadcast([P, BLOCKS, FEAT])
                link(v.tensor_tensor(work[:], x[:], w, ALU.mult))
                link(v.tensor_reduce(to.rearrange("p b c -> p (b c)"), work[:], AX.X, ALU.add))
            link(v.memset(top[:], -FAR))
            dve.sem_inc(table_ready[P_MAX], 1)

            def edge_score():
                link(v.tensor_tensor(score[:, 0:1], src_row[:, FEAT:FEAT + 1], dst_row[:, 0:1], ALU.add))
                link(v.scalar_tensor_tensor(out=score[:, 3:4], in0=score[:, 0:1], scalar=SLOPE,
                                            in1=score[:, 0:1], op0=ALU.mult, op1=ALU.max))

            with dve.Fori(0, TILES) as t:
                chain.enter(t, TILES, 6)
                dve.wait_ge(rows_in[P_MAX], t * 32 + 32)
                edge_score()
                one_hot()
                link(v.tensor_scalar(hot[:], hot[:], FAR, -FAR, ALU.mult, ALU.add))
                link(v.scalar_tensor_tensor(out=top[:], in0=hot[:], scalar=score[:, 3:4], in1=top[:],
                                            op0=ALU.add, op1=ALU.max))
                dve.sem_inc(tile_done, 1)
                chain.leave()
            top_to_nodes(2)
            link(v.tensor_copy(dst_rows[:, :, 1:2], stat[:, 3, :].unsqueeze(2)))
            dve.sem_inc(table_ready[P_SOFT], 1)
            with dve.Fori(0, TILES) as t:
                chain.enter(t, TILES, 7)
                dve.wait_ge(rows_in[P_SOFT], t * 32 + 32)
                edge_score()
                link(v.tensor_tensor(score[:, 0:1], score[:, 3:4], dst_row[:, 1:2], ALU.subtract))
                dve.sem_inc(score_out, 1)
                one_hot()
                dve.wait_ge(weight_out, t + (TILES + 1))
                link(v.tensor_scalar(val[:, 0:FEAT], src_row[:, 0:FEAT], score[:, 1:2], None, ALU.mult))
                link(v.tensor_copy(val[:, FEAT:FEAT + 1], score[:, 1:2]))
                dve.sem_inc(tile_ready, 1)
                chain.leave()
            sums_to_nodes(P_SOFT, nth_sum[P_SOFT])
            link(v.tensor_scalar(stat[:, 0, :], agg[:, :, FEAT:FEAT + 1].rearrange("p b c -> p (b c)"), 1e-30, None,
                                 ALU.max))
            link(v.reciprocal(stat[:, 1, :], stat[:, 0, :]))
            link(v.tensor_tensor(work[:], agg[:, :, 0:FEAT], spread(stat[:, 1, :], FEAT), ALU.mult))
            link(v.tensor_tensor(x[:], x[:], work[:], ALU.add))
            layer_norm(3, 3)
            link(v.memset(val[:], 1.0))
            dve.sem_inc(table_ready[P_OUTDEG], 1)

            with dve.Fori(0, TILES) as t:
                chain.enter(t, TILES, 2)
                dve.wait_ge(edge_in, t * 16 + (16 * serial[P_OUTDEG] + 16))
                link(v.tensor_copy(score[:, 2:3], edge[:, 0:1]))
                link(v.tensor_scalar(hot[:], node_no[:], score[:, 2:3], None, ALU.is_equal))
                dve.sem_inc(tile_ready, 1)
                chain.leave()
            sums_to_nodes(P_OUTDEG, nth_sum[P_OUTDEG])
            link(v.tensor_scalar(src_norm[:], agg[:, :, 0:1].rearrange("p b c -> p (b c)"), 1.0, None, ALU.max))
            dve.sem_inc(root_in, 1)
            dve.wait_ge(root_out, 5)
            link(v.reciprocal(stat[:, 0, :], src_norm[:]))
            link(v.tensor_copy(src_norm[:], stat[:, 0, :]))
            link(v.reciprocal(stat[:, 0, :], dst_norm[:]))
            link(v.tensor_scalar(dst_norm[:], stat[:, 0, :], 1.0 - ALPHA, None, ALU.mult))
            link(v.tensor_scalar(x0[:], x[:], ALPHA, None, ALU.mult))
            link(v.tensor_copy(work[:], x[:]))
            link(v.tensor_tensor(rows[:, :, 0:FEAT], work[:], spread(src_norm[:], FEAT), ALU.mult))
            dve.sem_inc(table_ready[P_PROP], 1)
            PER_STEP = 3 * TILES + len(CHUNKS) + 4 + 3
            with dve.Fori(0, STEPS) as s:
                chain.enter(s, STEPS, PER_STEP)
                dve.wait_ge(rows_in_cleared, s + 1)
                dve.sem_inc(vector_turns, 1)
                value_tiles(P_PROP)
                sums_to_nodes(P_PROP, s + nth_sum[P_PROP])
                link(v.tensor_tensor(work[:], agg[:, :, 0:FEAT], spread(dst_norm[:], FEAT), ALU.mult))
                link(v.tensor_tensor(work[:], work[:], x0[:], ALU.add))
                link(v.tensor_tensor(rows[:, :, 0:FEAT], work[:], spread(src_norm[:], FEAT), ALU.mult))
                dve.sem_inc(table_ready[P_PROP], 1)
                chain.leave()
            link(v.tensor_tensor(x[:], x[:], work[:], ALU.add))
            layer_norm(5, 6)
            dve.sem_inc(result_ready, 1)


def kernel(**inputs):
    import numpy as np
    import concourse.bacc as bacc
    from concourse.bass_utils import run_bass_kernel_spmd

    x = np.asarray(inputs["x"])
    x_pad = np.zeros((NODES_PAD, FEAT), x.dtype)
    x_pad[:NODES] = x
    edges = np.zeros((EDGES_PAD, 3), np.int32)
    edges[EDGES:, 1] = NODES
    for c, name in enumerate(("src", "dst", "edge_type_86")):
        edges[:EDGES, c] = np.asarray(inputs[name])

    def with_bias(w, b):
        return np.concatenate([np.asarray(inputs[w]).T, np.asarray(inputs[b])[None]], 0)

    arrays = {
        "x_pad": x_pad, "edges": edges,
        "weight": np.asarray(inputs["L0_gnn_weight"]).reshape(BASES, FEAT * FEAT),
        "w_comp_t": np.asarray(inputs["L0_gnn_w_comp"]).T,
        "self_loop": np.asarray(inputs["L0_gnn_self_loop_weight"]),
        "a1_t": with_bias("L0_gnn_A1_w", "L0_gnn_A1_b"), "a2_t": with_bias("L0_gnn_A2_w", "L0_gnn_A2_b"),
        "rel_emb": np.asarray(inputs["L0_gnn_rel_emb"]),
        "attn_w": np.asarray(inputs["L2_gnn_attn_w"])[None],
    }
    arrays = {k: np.ascontiguousarray(a) for k, a in arrays.items()}
    nc = bacc.Bacc("TRN2", target_bir_lowering=False, num_devices=1)
    aps = {k: nc.dram_tensor(k, a.shape, mybir.dt.from_np(a.dtype), kind="ExternalInput").ap()
           for k, a in arrays.items()}
    out = nc.dram_tensor("out", [NODES_PAD, FEAT], F32, kind="ExternalOutput").ap()
    gnn(nc, out=out, **aps)
    r = run_bass_kernel_spmd(nc, [arrays], core_ids=[0])
    return r.results[0]["out"][:NODES]
```

```python
from contextlib import ExitStack
from math import sqrt

import concourse.bass as bass
from concourse import mybir

F32, I32 = mybir.dt.float32, mybir.dt.int32
BF16, F16, FP8, U8 = mybir.dt.bfloat16, mybir.dt.float16, mybir.dt.float8e4, mybir.dt.uint8
ALU, ACT, AX = mybir.AluOpType, mybir.ActivationFunctionType, mybir.AxisListType

P = 128
NODES, FEAT = 3125, 32
BLOCKS = -(-NODES // P)
NODES_PAD = BLOCKS * P
EDGES = 100000
TILES = -(-EDGES // P)
RELS, BASES = 86, 16
ROW = 64
BANK = 512
CHUNKS = [(c, min(BANK, NODES - c)) for c in range(0, NODES, BANK)]
PER_BANK = BANK // ROW
STEPS, ALPHA = 10, 0.1
SLOPE, EPS = 0.01, 1e-5
FAR = 1e30
REL_ROW = FEAT + FEAT * FEAT
EDGE_COLS = 4

GROUP = 25
GROUPS = NODES // GROUP
SLOTS = 8
WINDOW = SLOTS * P
HALF = SLOTS // 2
UNROLL = 5
TURNS = GROUPS // UNROLL
SPAN = UNROLL * GROUP
RUN = 32
ROWS_CHECKED = 125
PER_ROW = EDGES // ROWS_CHECKED
RUNS = PER_ROW // RUN
EDGES_PAD = -(-(EDGES + WINDOW) // P) * P
PAIRS = BLOCKS * GROUP
BANK0 = 13
MIXES = BASES + 1
REL_COLS = FEAT + BASES
DST_AT = 96
SIDE = DST_AT + GROUP
ADJ_MAX = 16

P_REL, P_SUM, P_MAX, P_SOFT, P_OUTDEG, P_PROP = range(6)
ROWS_GATHERED = {P_REL: 3, P_SUM: 1, P_MAX: 2, P_SOFT: 2, P_OUTDEG: 0, P_PROP: 1}
SUM_COLS = {P_REL: FEAT, P_SUM: FEAT + 1, P_SOFT: FEAT + 1, P_OUTDEG: 1, P_PROP: FEAT}


def rows_of(b):
    return min(P, NODES - b * P)


class Chain:

    def __init__(self, eng, sem):
        self.eng, self.sem, self.count, self.loops = eng, sem, 0, []

    def value(self):
        total = self.count
        for var, per_turn, _, _ in self.loops:
            total = var * per_turn + total
        return total

    def link(self, instruction):
        self.step(instruction)
        self.wait()

    def step(self, instruction):
        instruction.then_inc(self.sem, 1)
        self.count += 1

    def wait(self):
        self.eng.wait_ge(self.sem, self.value())

    def enter(self, var, turns, per_turn):
        self.loops.append((var, per_turn, turns, self.count))

    def leave(self):
        _, per_turn, turns, start = self.loops.pop()
        assert self.count - start == per_turn, (self.count - start, per_turn)
        self.count = start + turns * per_turn


class Carver:

    def __init__(self, whole, words):
        self.whole, self.words, self.at = whole, words, 0

    def cut(self, cols, dt=F32, n=P, n0=0):
        size = {F32: 4, I32: 4, BF16: 2, F16: 2, FP8: 1}[dt]
        words = -(-cols * size // 4)
        ap = self.whole[n0:n0 + n, self.at:self.at + words]
        self.at += words
        assert self.at <= self.words, (self.at, self.words)
        return (ap if dt == F32 else ap.bitcast(dt))[:, 0:cols]


def gnn(nc, x_pad, edges, weight, w_comp, w_comp_t, self_loop, a1_t, a2_t, rel_emb, attn_w, out):
    ctx = ExitStack()
    with ctx:
        def sb(name, shape, dt=F32):
            return ctx.enter_context(nc.sbuf_tensor(name, shape, dt))

        def sem(name):
            return ctx.enter_context(nc.semaphore(name))

        feat_table = nc.dram_tensor("feat_table", [NODES_PAD, ROW], F32, kind="Internal").ap()
        dst_table = nc.dram_tensor("dst_table", [NODES_PAD, FEAT], F32, kind="Internal").ap()
        dst_parts = nc.dram_tensor("dst_parts", [NODES_PAD, 3 * FEAT], BF16, kind="Internal").ap()
        rel_table = nc.dram_tensor("rel_table", [RELS, REL_ROW], F32, kind="Internal").ap()

        x = sb("x", [P, BLOCKS, FEAT])
        x0 = sb("x0", [P, BLOCKS, FEAT])
        rows = sb("rows", [P, BLOCKS, ROW])
        dst_rows = sb("dst_rows", [P, BLOCKS, FEAT])
        agg = sb("agg", [P, BLOCKS, FEAT + 1])
        work = sb("work", [P, BLOCKS, FEAT])
        stat = sb("stat", [P, 4, BLOCKS])
        src_norm = sb("src_norm", [P, BLOCKS])
        dst_norm = sb("dst_norm", [P, BLOCKS])
        aggT = sb("aggT", [FEAT + 1, NODES])
        a1 = sb("a1", [FEAT + 1, FEAT])
        a2 = sb("a2", [FEAT + 1, FEAT])
        wc = sb("wc", [BASES, RELS])
        wb = sb("wb", [BASES, FEAT * FEAT])
        sl = sb("sl", [FEAT, FEAT])
        attn = sb("attn", [P, 2 * FEAT])
        mix = sb("mix", [P, MIXES, FEAT])
        rel_side = sb("rel_side", [DST_AT, REL_COLS])
        ident = sb("ident", [P, P])
        ident_bf = sb("ident_bf", [P, P], BF16)
        ones = sb("ones", [P, P])
        eps = sb("eps", [P, 1])
        pair_no = sb("pair_no", [P, PAIRS], F16)
        row_no = sb("row_no", [P, P], BF16)
        dst_no = sb("dst_no", [P, GROUP])
        dst_no_bf = sb("dst_no_bf", [P, GROUP], BF16)
        first_dst = sb("first_dst", [P, GROUPS + 1])
        flags = sb("flags", [1, 2], I32)
        window_at = sb("window_at", [1, P], I32)
        flag_parts = sb("flag_parts", [P, 4])
        found = sb("found", [1, P])

        ADJ_WORDS = -(-BLOCKS * NODES // 4)
        adj_words = sb("adj_words", [P, ADJ_WORDS])
        adj = adj_words[:, :].bitcast(FP8)[:, 0:BLOCKS * NODES].rearrange("p (b n) -> p b n", b=BLOCKS)
        adj_bytes = adj_words[:, :].bitcast(U8)[:, 0:BLOCKS * NODES].rearrange("p (b n) -> p b n", b=BLOCKS)
        old = Carver(adj_words, ADJ_WORDS)
        node_no, hot, top_g = old.cut(NODES), old.cut(NODES), old.cut(NODES)
        rel_row, prod_g = old.cut(REL_ROW), old.cut(FEAT * FEAT).rearrange("p (o i) -> p o i", o=FEAT)
        last_row = old.cut(BLOCKS * ROW).rearrange("p (b c) -> p b c", b=BLOCKS)
        lastT = old.cut(NODES_PAD, n=FEAT)
        last_edge = old.cut(BLOCKS * EDGE_COLS, I32).rearrange("p (b c) -> p b c", b=BLOCKS)
        rel_rows = old.cut(REL_ROW, n=RELS)
        last_no, last_src = old.cut(BLOCKS, I32), old.cut(BLOCKS, I32)
        zeros = old.cut(BANK)
        edge, src_row, dst_row = old.cut(EDGE_COLS, I32), old.cut(ROW), old.cut(FEAT)
        score_g, edge_no, val = old.cut(4), old.cut(1), old.cut(FEAT + 1)

        ARENA = 21500
        arena = sb("arena", [P, ARENA])
        prep = Carver(arena, ARENA)
        xT = prep.cut(NODES_PAD, n=FEAT + 1)
        checked = prep.cut(PER_ROW * EDGE_COLS, I32, n=ROWS_CHECKED).rearrange("p (e c) -> p e c", c=EDGE_COLS)
        unsorted = prep.cut(PER_ROW, n=ROWS_CHECKED)
        run_last = prep.cut(RUNS, n=ROWS_CHECKED)
        below = prep.cut((GROUPS + 1) * RUNS, n=ROWS_CHECKED).rearrange("p (g r) -> p g r", r=RUNS)
        runs_below = prep.cut(GROUPS + 2, n=ROWS_CHECKED)
        q_parts = prep.cut(BLOCKS * 3 * FEAT, BF16).rearrange("p (b j f) -> p b j f", b=BLOCKS, j=3)
        rel_parts = prep.cut(3 * REL_COLS, BF16, n=DST_AT).rearrange("p (j c) -> p j c", j=3)
        split_rest = prep.cut(BLOCKS * FEAT)

        sweep = Carver(arena, ARENA)
        side = sweep.cut(UNROLL * 3 * REL_COLS, BF16, n=SIDE).rearrange("p (u j c) -> p u j c", u=UNROLL, j=3)
        window = sweep.cut(UNROLL * SLOTS * EDGE_COLS, I32).rearrange("p (u k c) -> p u k c", u=UNROLL, k=SLOTS)

        def per_slot(dt=F32):
            return sweep.cut(UNROLL * SLOTS, dt).rearrange("p (u k) -> p u k", u=UNROLL)

        block_of, row_of = per_slot(I32), per_slot(I32)
        dst_off, inside, pair_of, row_f, rel_f, score, weight_e = [per_slot() for _ in range(7)]
        coeff = sweep.cut(UNROLL * SLOTS * MIXES).rearrange("p (u k m) -> p u k m", u=UNROLL, k=SLOTS)
        xp = sweep.cut(UNROLL * SLOTS * ROW).rearrange("p (u k c) -> p u k c", u=UNROLL, k=SLOTS)
        side_hot = sweep.cut(UNROLL * SLOTS * SIDE, BF16).rearrange("p (u k s) -> p u k s", u=UNROLL, k=SLOTS)
        side_hotT = sweep.cut(UNROLL * WINDOW, BF16, n=SIDE).rearrange("p (u w) -> p u w", u=UNROLL)
        per_edge = sweep.cut(UNROLL * SLOTS * REL_COLS).rearrange("p (u k c) -> p u k c", u=UNROLL, k=SLOTS)
        product = sweep.cut(SLOTS * FEAT).rearrange("p (k f) -> p k f", k=SLOTS)
        pair_hot = sweep.cut(2 * HALF * PAIRS, BF16).rearrange("p (h k v) -> p h k v", h=2, k=HALF)
        row_hot = sweep.cut(2 * HALF * P, BF16).rearrange("p (h k v) -> p h k v", h=2, k=HALF)
        mixed = sweep.cut(2 * HALF * GROUP * MIXES).rearrange("p (h k d m) -> p h k d m", h=2, k=HALF, d=GROUP)
        sumsT = sweep.cut(UNROLL * GROUP * MIXES).rearrange("p (d m) -> p d m", m=MIXES)
        squares = sweep.cut(2 * BANK0 * GROUP, BF16).rearrange("p (h v) -> p h v", h=2)
        turn_fp8 = sweep.cut(BLOCKS * SPAN, FP8)
        turn_adj = turn_fp8.rearrange("p (b n) -> p b n", b=BLOCKS)
        turn_bytes = turn_fp8.bitcast(U8).rearrange("p (b n) -> p b n", b=BLOCKS)
        square_sums = sweep.cut(2 * GROUPS).rearrange("p (h g) -> p h g", h=2)

        dense = Carver(arena, ARENA)
        parts = dense.cut(2 * BLOCKS * P, BF16).rearrange("p (s b c) -> p s b c", s=2, b=BLOCKS)
        fold = dense.cut(FEAT + 1, n=3 * FEAT + 1)
        chunkT = dense.cut(2 * BANK, n=3 * FEAT + 1).rearrange("p (s c) -> p s c", s=2)
        fresh = dense.cut(2 * 4 * FEAT).rearrange("p (s b f) -> p s b f", s=2, b=4)
        counted = dense.cut(NODES, BF16)
        src_count = dense.cut(BLOCKS)
        s_src, s_src_small, s_dst, s_max, level = [dense.cut(BLOCKS) for _ in range(5)]
        spread_of = dense.cut(4)
        keep_at = dense.at
        row1, row2 = dense.cut(NODES), dense.cut(NODES)
        shared_at = dense.at
        diag1, diag2 = dense.cut(NODES_PAD), dense.cut(NODES_PAD)
        dense.at = keep_at
        top = dense.cut(NODES)
        dense.at = shared_at
        HALVES = [(0, 3 * BANK), (3 * BANK, NODES - 3 * BANK)]
        exps = dense.cut(2 * 2 * HALVES[1][1]).rearrange("p (s e c) -> p s e c", s=2, e=2)

        ps = ctx.enter_context(nc.psum_tensor("ps", [P, 8 * BANK], F32))

        def ps_block(b, cols, n=P, first_bank=0):
            at = first_bank * BANK + b * ROW
            return ps[0:n, at:at + cols]

        def ps_blocks(cols, b0, b1, n=P):
            return ps[0:n, b0 * ROW:b1 * ROW].rearrange("p (b c) -> p b c", c=ROW)[:, :, 0:cols]

        inputs_loaded = sem("inputs_loaded")
        constants_made = sem("constants_made")
        cleared = sem("cleared")
        side_loaded = sem("side_loaded")
        vector_steps = sem("vector_steps")
        xT_out, xT_ready = sem("xT_out"), sem("xT_ready")
        projected = sem("projected")
        parts_split, parts_stored = sem("parts_split"), sem("parts_stored")
        rows_made, rows_stored = sem("rows_made"), sem("rows_stored")
        runs_counted, runs_summed = sem("runs_counted"), sem("runs_summed")
        flag_ready = sem("flag_ready")
        window_in = [sem(f"window_in_{u}") for u in range(UNROLL)]
        gathered = [sem(f"gathered_{u}") for u in range(UNROLL)]
        side_in = sem("side_in")
        decoded = sem("decoded")
        side_hot_ready, side_hotT_out, side_hotT_copied = sem("side_hot_ready"), sem("side_hotT_out"), sem("side_hotT_copied")
        pairs_ready, pairs_used, adj_copied = sem("pairs_ready"), sem("pairs_used"), sem("adj_copied")
        per_edge_out, per_edge_copied = sem("per_edge_out"), sem("per_edge_copied")
        score_ready, weight_ready = sem("score_ready"), sem("weight_ready")
        mixed_ready, mixed_used, sumsT_copied = sem("mixed_ready"), sem("mixed_used"), sem("sumsT_copied")
        turn_out, turn_copied, turn_moved = sem("turn_out"), sem("turn_copied"), sem("turn_moved")
        sync_turns, tensor_turns = sem("sync_turns"), sem("tensor_turns")
        sweep_steps, scalar_turns = sem("sweep_steps"), sem("scalar_turns")
        flags_counted, flags_summed = sem("flags_counted"), sem("flags_summed")
        dense_steps = sem("dense_steps")
        layer_sums, layer_nodes, layer_copied = sem("layer_sums"), sem("layer_nodes"), sem("layer_copied")
        d_root_in, d_root_out = sem("d_root_in"), sem("d_root_out")
        parts_ready, chunk_out, chunk_copied = sem("parts_ready"), sem("chunk_out"), sem("chunk_copied")
        fold_out, fold_taken = sem("fold_out"), sem("fold_taken")
        degree_out = sem("degree_out")
        range_in, range_out = sem("range_in"), sem("range_out")
        d_top_ready, d_top_out = sem("d_top_ready"), sem("d_top_out")
        level_ready, diag1_ready, diag2_ready = sem("level_ready"), sem("diag1_ready"), sem("diag2_ready")
        row1_out, row2_out, row1_copied, row2_copied = sem("row1_out"), sem("row2_out"), sem("row1_copied"), sem("row2_copied")
        exps_ready, soft_ready, soft_used = sem("exps_ready"), sem("soft_ready"), sem("soft_used")
        general_steps = sem("general_steps")
        turns, vector_turns = sem("turns"), sem("vector_turns")
        general_made = sem("general_made")
        embedding_in = sem("embedding_in")
        relations_out = sem("relations_out")
        table_ready = [sem(f"table_ready_{p}") for p in range(6)]
        table_stored = sem("table_stored")
        edge_in = sem("edge_in")
        rows_in = [sem(f"rows_in_{p}") for p in range(6)]
        rows_in_cleared = sem("rows_in_cleared")
        score_out, weight_out = sem("score_out"), sem("weight_out")
        tile_ready = sem("tile_ready")
        tile_done = sem("tile_done")
        sums_out, sums_copied, nodes_out = sem("sums_out"), sem("sums_copied"), sem("nodes_out")
        top_ready, top_out, top_copied = sem("top_ready"), sem("top_out"), sem("top_copied")
        last_ready, last_in = sem("last_ready"), sem("last_in")
        lastT_out, lastT_ready, current_out = sem("lastT_out"), sem("lastT_ready"), sem("current_out")
        root_in, root_out = sem("root_in"), sem("root_out")
        result_ready, stored = sem("result_ready"), sem("stored")

        LOADS = 16
        CONSTANTS = 9
        serial = {p: p * TILES for p in range(6)}
        summed = [p for p in range(6) if p != P_MAX]
        nth_sum = {p: n + 1 for n, p in enumerate(summed)}
        TABLES = {P_REL: 2, P_SUM: 3, P_MAX: 5, P_SOFT: 6, P_OUTDEG: 6, P_PROP: 7}

        def either(eng, if_sorted, if_counted, otherwise):
            eng.wait_ge(flag_ready, 1)
            with eng.If(eng.value_load(flags[0:1, 0:1], min_val=0, max_val=1) == 0):
                if_sorted()
            eng.wait_ge(flag_ready, 2)
            with eng.If(eng.value_load(flags[0:1, 1:2], min_val=0, max_val=1) == 0):
                if_counted()
            with eng.Else():
                otherwise()

        block = ctx.enter_context(nc.Block())

        @block.sync
        def _(sp):
            loads = [(x[:], x_pad.rearrange("(b p) f -> p b f", p=P)), (a1[:], a1_t), (a2[:], a2_t),
                     (checked, edges[0:EDGES, :].rearrange("(p e) c -> p e c", p=ROWS_CHECKED)),
                     (wc[:], w_comp_t), (wb[:], weight), (sl[:], self_loop),
                     (attn[:], attn_w.to_broadcast([P, 2 * FEAT]))]
            for q in range(0, P, FEAT):
                loads.append((mix[q:q + FEAT, 0:BASES, :], weight.rearrange("m (i o) -> i m o", i=FEAT)))
                loads.append((mix[q:q + FEAT, BASES, :], self_loop))
            assert len(loads) == LOADS
            for dst, src in loads:
                sp.dma_start(dst, src).then_inc(inputs_loaded, 16)
            sp.wait_ge(cleared, 1)
            sp.dma_start(rel_side[0:RELS, 0:FEAT], rel_emb).then_inc(side_loaded, 16)
            sp.dma_start(rel_side[0:RELS, FEAT:REL_COLS], w_comp).then_inc(side_loaded, 16)
            sp.wait_ge(parts_split, 1)
            sp.dma_start(dst_parts.rearrange("(b p) (j f) -> p b j f", p=P, j=3), q_parts).then_inc(parts_stored, 16)
            sp.wait_ge(rows_made, 1)
            sp.dma_start(feat_table.rearrange("(b p) c -> p b c", p=P), rows[:]).then_inc(rows_stored, 16)

            def run_sweep():
                sp.wait_ge(parts_stored, 16)
                with sp.Fori(0, TURNS) as i:
                    for u in range(UNROLL):
                        sp.wait_ge(score_ready, i * UNROLL + (u + 1))
                        sp.sem_inc(sync_turns, 1)
                        sp.wait_ge(decoded, i + 1)
                        sp.sem_inc(sync_turns, 1)
                        at = sp.value_load(window_at[0:1, bass.ds(i * UNROLL + u, 1)], min_val=0, max_val=EDGES)
                        sp.dma_start(window[:, u].rearrange("p k c -> p (k c)"),
                                     edges[bass.ds(at, WINDOW), :].rearrange("(p k) c -> p (k c)", p=P))\
                          .then_inc(window_in[u], 16)
                    sp.wait_ge(per_edge_out, i * UNROLL + 1)
                    sp.sem_inc(sync_turns, 1)
                    for u in range(UNROLL):
                        sp.dma_start(side[DST_AT:SIDE, u, :, 0:FEAT],
                                     dst_parts[bass.ds(i * SPAN + u * GROUP, GROUP), :]
                                     .rearrange("d (j f) -> d j f", j=3)).then_inc(side_in, 16)

            def run_dense():
                sp.wait_ge(result_ready, 1)
                sp.dma_start(out.rearrange("(b p) f -> p b f", p=P), x[:]).then_inc(stored, 16)
                sp.wait_ge(stored, 16)

            def run_general():
                sp.dma_start(rel_rows[:, 0:FEAT], rel_emb).then_inc(embedding_in, 16)
                table = feat_table.rearrange("(b p) c -> p b c", p=P)
                dtable = dst_table.rearrange("(b p) c -> p b c", p=P)

                def load_tiles(base):
                    with sp.Fori(0, TILES) as t:
                        sp.wait_ge(tile_done, t + (base + 1))
                        sp.dma_start(edge[:], edges[bass.ds(t * P, P), :]).then_inc(edge_in, 16)

                for p in range(P_PROP):
                    sp.wait_ge(table_ready[p], 1)
                    if p in (P_SUM, P_MAX):
                        sp.dma_start(table, rows[:]).then_inc(table_stored, 16)
                    if p in (P_REL, P_MAX, P_SOFT):
                        sp.dma_start(dtable, dst_rows[:]).then_inc(table_stored, 16)
                    if p == P_REL:
                        sp.dma_start(rel_table, rel_rows[:]).then_inc(table_stored, 16)
                    load_tiles(serial[p])
                with sp.Fori(0, STEPS) as s:
                    sp.wait_ge(table_ready[P_PROP], s + 1)
                    sp.dma_start(table, rows[:]).then_inc(table_stored, 16)
                    load_tiles(s * TILES + serial[P_PROP])
                sp.wait_ge(result_ready, 1)
                sp.dma_start(out.rearrange("(b p) f -> p b f", p=P), x[:]).then_inc(stored, 16)
                sp.wait_ge(stored, 16)

            either(sp, run_sweep, run_dense, run_general)

        @block.gpsimd
        def _(pool):
            def numbers(to, pattern, base, step):
                pool.iota(to, pattern=pattern, base=base, channel_multiplier=step,
                          allow_small_or_imprecise_dtypes=True).then_inc(constants_made, 1)

            numbers(first_dst[:], [[GROUP, GROUPS + 1]], 0, 0)
            numbers(pair_no[:], [[1, PAIRS]], 1, 0)
            numbers(row_no[:], [[1, P]], 0, 0)
            numbers(dst_no[:], [[1, GROUP]], 1, 0)
            numbers(dst_no_bf[:], [[1, GROUP]], 1, 0)
            for m in (ident, ident_bf):
                pool.memset(m[:], 0.0).then_inc(constants_made, 1)
            pool.wait_ge(constants_made, CONSTANTS - 2)
            for m in (ident, ident_bf):
                pool.affine_select(out=m[:], in_=m[:], compare_op=ALU.not_equal, fill=1.0, base=0,
                                   pattern=[[-1, P]], channel_multiplier=1).then_inc(constants_made, 1)

            def gather(to, table, index, done):
                pool.indirect_dma_start(to, None, table, bass.IndirectOffsetOnAxis(ap=index, axis=0)).then_inc(done, 16)

            def hold():
                pool.sem_inc(turns, 1)

            def run_sweep():
                pool.wait_ge(rows_stored, 16)
                pool.sem_inc(turns, 1)
                with pool.Fori(0, TURNS) as i:
                    for u in range(UNROLL):
                        pool.wait_ge(window_in[u], i * 16 + 16)
                        pool.wait_ge(mixed_used, (i * UNROLL + u) * 2 + 2)
                        hold()
                        for k in range(SLOTS):
                            gather(xp[:, u, k, :], feat_table, window[:, u, k, 0:1], gathered[u])

            def run_dense():
                pool.wait_ge(range_in, 1)
                pool.partition_all_reduce(spread_of[:, 1:2], spread_of[:, 0:1], P, bass.bass_isa.ReduceOp.max)\
                    .then_inc(range_out, 1)

            def run_general():
                pool.iota(node_no, pattern=[[1, NODES]], base=0, channel_multiplier=0,
                          allow_small_or_imprecise_dtypes=True).then_inc(general_made, 1)
                pool.iota(edge_no, pattern=[[1, 1]], base=1 - P, channel_multiplier=1,
                          allow_small_or_imprecise_dtypes=True).then_inc(general_made, 1)

                def gather_tiles(p, tile, step=None):
                    with pool.Fori(0, TILES) as t:
                        pool.wait_ge(edge_in, (t + tile) * 16 + 16)
                        hold()
                        gather(src_row[:], feat_table, edge[:, 0:1], rows_in[p])
                        if ROWS_GATHERED[p] >= 2:
                            gather(dst_row[:], dst_table, edge[:, 1:2], rows_in[p])
                        if ROWS_GATHERED[p] >= 3:
                            gather(rel_row[:], rel_table, edge[:, 2:3], rows_in[p])

                for p in range(P_PROP):
                    if ROWS_GATHERED[p]:
                        pool.wait_ge(table_stored, 16 * TABLES[p])
                        gather_tiles(p, serial[p])
                    if p == P_REL:
                        pool.wait_ge(last_ready, 1)
                        for b in range(BLOCKS):
                            gather(last_edge[:, b, :], edges, last_no[:, b:b + 1], last_in)
                        pool.wait_ge(last_ready, 2)
                        for b in range(BLOCKS):
                            gather(last_row[:, b, :], feat_table, last_src[:, b:b + 1], last_in)
                with pool.Fori(0, STEPS) as s:
                    pool.wait_ge(table_stored, s * 16 + 16 * TABLES[P_PROP])
                    hold()
                    n = rows_in[P_PROP].num
                    pool.dma_reset(range(n, n + 1))
                    pool.sem_clear(rows_in[P_PROP])
                    pool.sem_inc(rows_in_cleared, 1)
                    gather_tiles(P_PROP, s * TILES + serial[P_PROP])

            either(pool, run_sweep, run_dense, run_general)

        @block.tensor
        def _(pe):
            pe.wait_ge(inputs_loaded, 16 * LOADS)
            pe.wait_ge(constants_made, CONSTANTS)
            for b in range(BLOCKS):
                mm = nc.tensor.matmul(ps[0:FEAT, b * P:(b + 1) * P], x[:, b, :], ident[:], start=True, stop=True)
            mm.then_inc(xT_out, 1)
            pe.wait_ge(xT_ready, 1)
            for b in range(BLOCKS):
                blk = xT[:, b * P:(b + 1) * P]
                nc.tensor.matmul(ps_block(b, FEAT), blk, a1[:], start=True, stop=True)
                mm = nc.tensor.matmul(ps_block(b, FEAT, first_bank=4), blk, a2[:], start=True, stop=True)
            mm.then_inc(projected, 1)
            pe.wait_ge(runs_counted, 1)
            nc.tensor.matmul(ps[:, 0:GROUPS + 2], ones[0:ROWS_CHECKED, :], runs_below, start=True, stop=True)\
              .then_inc(runs_summed, 1)

            def run_sweep():
                for s, n in ((pairs_used, 2), (mixed_used, 2 * UNROLL), (per_edge_out, 1), (turn_out, 1)):
                    pe.sem_inc(s, n)

                def transpose_side(i, u):
                    pe.wait_ge(side_hot_ready, i * UNROLL + (u + 1))
                    pe.wait_ge(side_hotT_copied, i * UNROLL + (u + 1))
                    for k in range(SLOTS):
                        mm = nc.tensor.matmul(ps[0:SIDE, 2 * BANK + k * P:2 * BANK + (k + 1) * P],
                                              side_hot[:, u, k, :], ident_bf[:], start=True, stop=True)
                    mm.then_inc(side_hotT_out, 1)

                def count_pairs(i, u):
                    pe.wait_ge(adj_copied, i * UNROLL + (u + 1))
                    for h in range(2):
                        pe.wait_ge(pairs_ready, (i * UNROLL + u) * 2 + (h + 1))
                        for k in range(HALF):
                            first, last = h + k == 0, h * HALF + k == SLOTS - 1
                            nc.tensor.matmul(ps[:, 0:BANK0 * GROUP], row_hot[:, h, k, :],
                                             pair_hot[:, h, k, 0:BANK0 * GROUP], start=first, stop=last)
                            mm = nc.tensor.matmul(ps[:, BANK:BANK + PAIRS - BANK0 * GROUP], row_hot[:, h, k, :],
                                                  pair_hot[:, h, k, BANK0 * GROUP:PAIRS], start=first, stop=last)
                        mm.then_inc(pairs_used, 1)

                def fetch_per_edge(i, u):
                    pe.wait_ge(side_hotT_copied, i * UNROLL + (u + 2))
                    pe.wait_ge(side_in, i * (16 * UNROLL) + 16 * UNROLL)
                    pe.wait_ge(per_edge_copied, i * UNROLL + (u + 1))
                    for k in range(SLOTS):
                        for j in range(3):
                            mm = nc.tensor.matmul(ps[:, 4 * BANK + k * REL_COLS:4 * BANK + (k + 1) * REL_COLS],
                                                  side_hotT[:, u, k * P:(k + 1) * P], side[:, u, j, :],
                                                  start=(j == 0), stop=(j == 2))
                    mm.then_inc(per_edge_out, 1)

                def sum_mixed(i, u):
                    pe.wait_ge(sumsT_copied, i * UNROLL + (u + 1))
                    for h in range(2):
                        pe.wait_ge(mixed_ready, (i * UNROLL + u) * 2 + (h + 2))
                        for k in range(HALF):
                            mm = nc.tensor.matmul(
                                ps[k * FEAT:(k + 1) * FEAT, 5 * BANK:5 * BANK + GROUP * MIXES],
                                xp[:, u, h * HALF + k, 0:FEAT], mixed[:, h, k].rearrange("p d m -> p (d m)"),
                                start=(h == 0), stop=(h == 1), tile_position=(0, k * FEAT))
                        mm.then_inc(mixed_used, 1)

                with pe.Fori(0, TURNS) as i:
                    transpose_side(i, 0)
                    for u in range(UNROLL):
                        count_pairs(i, u)
                        if u + 1 < UNROLL:
                            transpose_side(i, u + 1)
                        fetch_per_edge(i, u)
                        if u:
                            sum_mixed(i, u - 1)
                    sum_mixed(i, UNROLL - 1)
                    pe.wait_ge(sumsT_copied, i * UNROLL + (UNROLL + 1))
                    pe.wait_ge(turn_copied, i + 1)
                    for m in range(MIXES):
                        mm = nc.tensor.matmul(ps[0:FEAT, 6 * BANK:6 * BANK + SPAN], mix[:, m, :], sumsT[:, :, m],
                                              start=(m == 0), stop=(m == MIXES - 1))
                    mm.then_inc(turn_out, 1)
                pe.wait_ge(flags_counted, 1)
                nc.tensor.matmul(ps[:, 0:1], ones[:], flag_parts[:, 0:1], start=True, stop=True)\
                  .then_inc(flags_summed, 1)

            def run_dense():
                def to_nodes(cols, nth):
                    pe.wait_ge(layer_copied, nth)
                    for b in range(BLOCKS):
                        mm = nc.tensor.matmul(ps_block(b, cols, rows_of(b)), aggT[0:cols, b * P:b * P + rows_of(b)],
                                              ident[0:cols, 0:cols], start=True, stop=True)
                    mm.then_inc(layer_nodes, 1)

                def fold_chunk(c, before, parity):
                    pe.wait_ge(chunk_copied, before + (c + 1))
                    pe.wait_ge(fold_taken, before + (c + 1))
                    at = CHUNKS[c][0]
                    for b in range(at // P, min(at // P + 4, BLOCKS)):
                        n = rows_of(b)
                        col = (4 + parity) * BANK + (b * P - at) // P * ROW
                        mm = nc.tensor.matmul(ps[0:n, col:col + FEAT + 1],
                                              chunkT[:, parity, b * P - at:b * P - at + n], fold,
                                              start=True, stop=True)
                    mm.then_inc(fold_out, 1)

                def neighbour_sum(before, half):
                    for c, (at, w) in enumerate(CHUNKS):
                        for b in range(BLOCKS):
                            if c == 0 and b % 4 == 0:
                                pe.wait_ge(parts_ready, before + (b // 4 + 1))
                                pe.sem_inc(tensor_turns, 1)
                            bank = c % 4 * BANK
                            mm = nc.tensor.matmul(ps[:, bank:bank + w], parts[:, half, b, :], adj[:, b, at:at + w],
                                                  start=(b == 0), stop=(b == BLOCKS - 1))
                        mm.then_inc(chunk_out, 1)
                        if c:
                            fold_chunk(c - 1, before, (c - 1 + half * len(CHUNKS)) % 2)
                    c = len(CHUNKS) - 1
                    fold_chunk(c, before, (c + half * len(CHUNKS)) % 2)

                pe.sem_inc(fold_taken, 2)
                to_nodes(FEAT, 1)
                neighbour_sum(0, 1)
                pe.wait_ge(d_top_ready, 1)
                for b in range(BLOCKS):
                    n = rows_of(b)
                    mm = nc.tensor.matmul(ps[0:n, b * P:(b + 1) * P], top[:, b * P:b * P + n], ident[:],
                                          start=True, stop=True)
                mm.then_inc(d_top_out, 1)
                pe.wait_ge(diag1_ready, 1)
                for at, w in CHUNKS:
                    mm = nc.tensor.matmul(ps[:, at:at + w], ones[:], diag1[:, at:at + w], start=True, stop=True)
                mm.then_inc(row1_out, 1)
                pe.wait_ge(row1_copied, 1)
                pe.wait_ge(diag2_ready, 1)
                for at, w in CHUNKS:
                    mm = nc.tensor.matmul(ps[:, at:at + w], ones[:], diag2[:, at:at + w], start=True, stop=True)
                mm.then_inc(row2_out, 1)
                pe.wait_ge(row2_copied, 1)
                for b in range(BLOCKS):
                    for h, (at, w) in enumerate(HALVES):
                        pe.wait_ge(soft_ready, 2 * b + h + 1)
                        for c in range(0, w, BANK):
                            cw = min(BANK, w - c)
                            mm = nc.tensor.matmul(ps[0:FEAT + 1, at + c:at + c + cw], agg[:, b, :],
                                                  exps[:, h, 1, c:c + cw], start=(b == 0), stop=(b == BLOCKS - 1))
                        mm.then_inc(soft_used, 1)
                to_nodes(FEAT + 1, 2)
                with pe.Fori(0, STEPS // 2) as s:
                    neighbour_sum(s * (2 * len(CHUNKS)) + len(CHUNKS), 0)
                    neighbour_sum(s * (2 * len(CHUNKS)) + 2 * len(CHUNKS), 1)

            def run_general():
                for c in range(FEAT * FEAT // BANK):
                    mm = nc.tensor.matmul(ps[0:RELS, c * BANK:(c + 1) * BANK], wc[:], wb[:, c * BANK:(c + 1) * BANK],
                                          start=True, stop=True)
                mm.then_inc(relations_out, 1)
                pe.sem_inc(tile_done, 1)

                def edge_sums(p, tile):
                    cols = SUM_COLS[p]
                    for c, w in CHUNKS:
                        nc.tensor.matmul(ps[0:cols, c:c + w], zeros[:, 0:cols], zeros[:, 0:w], start=True, stop=False)
                    with pe.Fori(0, TILES) as t:
                        pe.wait_ge(tile_ready, t + tile + 1)
                        for c, w in CHUNKS:
                            mm = nc.tensor.matmul(ps[0:cols, c:c + w], val[:, 0:cols], hot[:, c:c + w],
                                                  start=False, stop=False)
                        mm.then_inc(tile_done, 1)
                    for c, w in CHUNKS:
                        mm = nc.tensor.matmul(ps[0:cols, c:c + w], zeros[:, 0:cols], zeros[:, 0:w], start=False, stop=True)
                    mm.then_inc(sums_out, 1)

                def to_nodes(p, nth):
                    pe.wait_ge(sums_copied, nth)
                    cols = SUM_COLS[p]
                    for b in range(BLOCKS):
                        mm = nc.tensor.matmul(ps_block(b, cols, rows_of(b)), aggT[0:cols, b * P:b * P + rows_of(b)],
                                              ident[0:cols, 0:cols], start=True, stop=True)
                    mm.then_inc(nodes_out, 1)

                def top_to_nodes(nth):
                    pe.wait_ge(top_ready, nth)
                    for b in range(BLOCKS):
                        n = rows_of(b)
                        mm = nc.tensor.matmul(ps[0:n, b * P:(b + 1) * P], top_g[:, b * P:b * P + n], ident[:],
                                              start=True, stop=True)
                    mm.then_inc(top_out, 1)

                for p in range(P_PROP):
                    pe.wait_ge(table_ready[p], 1)
                    if p != P_MAX:
                        edge_sums(p, (nth_sum[p] - 1) * TILES)
                        to_nodes(p, nth_sum[p])
                    if p == P_REL:
                        top_to_nodes(1)
                        pe.wait_ge(last_in, 16 * 2 * BLOCKS)
                        pe.wait_ge(top_copied, 1)
                        for b in range(BLOCKS):
                            mm = nc.tensor.matmul(ps[0:FEAT, b * P:(b + 1) * P], last_row[:, b, 0:FEAT], ident[:],
                                                  start=True, stop=True)
                        mm.then_inc(lastT_out, 1)
                        pe.wait_ge(lastT_ready, 1)
                        for b in range(BLOCKS):
                            mm = nc.tensor.matmul(ps_block(b, FEAT), lastT[:, b * P:(b + 1) * P], sl[:],
                                                  start=True, stop=True)
                        mm.then_inc(current_out, 1)
                    if p == P_MAX:
                        top_to_nodes(2)
                with pe.Fori(0, STEPS) as s:
                    pe.wait_ge(table_ready[P_PROP], s + 1)
                    edge_sums(P_PROP, s * TILES + (nth_sum[P_PROP] - 1) * TILES)
                    to_nodes(P_PROP, s + nth_sum[P_PROP])

            either(pe, run_sweep, run_dense, run_general)

        @block.scalar
        def _(act):
            a = nc.scalar

            def run_sweep():
                for s, n in ((side_hotT_copied, 1), (adj_copied, 1), (per_edge_copied, 1), (sumsT_copied, 1),
                             (turn_copied, 1), (turn_moved, 1)):
                    act.sem_inc(s, n)

                def copy_side(i, u):
                    act.wait_ge(side_hotT_out, i * UNROLL + (u + 1))
                    a.copy(side_hotT[:, u, :], ps[0:SIDE, 2 * BANK:2 * BANK + WINDOW]).then_inc(side_hotT_copied, 1)

                def copy_adj(i, u):
                    if u == 0:
                        act.wait_ge(turn_moved, i + 1)
                    act.wait_ge(adj_copied, i * UNROLL + (u + 1))
                    act.wait_ge(pairs_used, (i * UNROLL + u) * 2 + 4)
                    act.sem_inc(scalar_turns, 1)
                    at = slice(u * GROUP, (u + 1) * GROUP)
                    banks = ((0, 0, BANK0), (BANK, BANK0, BLOCKS))
                    for h, (p0, b0, b1) in enumerate(banks):
                        n = (b1 - b0) * GROUP
                        a.activation(squares[:, h, 0:n], ps[:, p0:p0 + n], ACT.Square,
                                     accum_out=square_sums[:, h, bass.ds(i * UNROLL + u, 1)])
                    for p0, b0, b1 in banks:
                        last = a.activation(turn_adj[:, b0:b1, at], ps[:, p0:p0 + (b1 - b0) * GROUP]
                                            .rearrange("p (b d) -> p b d", d=GROUP), ACT.Copy, saturate=False)
                    last.then_inc(adj_copied, 1)

                def copy_sums(i, u):
                    act.wait_ge(mixed_used, (i * UNROLL + u) * 2 + (2 * UNROLL + 2))
                    if u == 0:
                        act.wait_ge(turn_out, i + 1)
                    a.copy(sumsT[:, u * GROUP:(u + 1) * GROUP, :].rearrange("p d m -> p (d m)"),
                           ps[:, 5 * BANK:5 * BANK + GROUP * MIXES]).then_inc(sumsT_copied, 1)

                with act.Fori(0, TURNS) as i:
                    copy_side(i, 0)
                    for u in range(UNROLL):
                        copy_adj(i, u)
                        if u + 1 < UNROLL:
                            copy_side(i, u + 1)
                        act.wait_ge(per_edge_out, i * UNROLL + (u + 2))
                        a.copy(per_edge[:, u].rearrange("p k c -> p (k c)"),
                               ps[:, 4 * BANK:4 * BANK + SLOTS * REL_COLS]).then_inc(per_edge_copied, 1)
                        act.wait_ge(score_ready, i * UNROLL + (UNROLL + u + 1))
                        a.activation(weight_e[:, u, :], score[:, u, :], ACT.Tanh, scale=1.0 / sqrt(FEAT))\
                         .then_inc(weight_ready, 1)
                        if u:
                            copy_sums(i, u - 1)
                    copy_sums(i, UNROLL - 1)
                    act.wait_ge(adj_copied, i * UNROLL + (UNROLL + 1))
                    act.sem_inc(scalar_turns, 1)
                    a.activation(adj_bytes[:, :, bass.ds(i * SPAN, SPAN)], turn_bytes, ACT.Copy)\
                       .then_inc(turn_moved, 1)
                    act.wait_ge(turn_out, i + 2)
                    act.sem_inc(scalar_turns, 1)
                    a.copy(aggT[0:FEAT, bass.ds(i * SPAN, SPAN)], ps[0:FEAT, 6 * BANK:6 * BANK + SPAN])\
                     .then_inc(turn_copied, 1)

            def run_dense():
                def root(nth):
                    act.wait_ge(d_root_in, nth)
                    a.activation(stat[:, 2, :], stat[:, 1, :], ACT.Sqrt, bias=eps[:], scale=1.0 / FEAT)\
                     .then_inc(d_root_out, 1)

                def copy_chunks(before, first=False, half=0):
                    for c, (at, w) in enumerate(CHUNKS):
                        act.wait_ge(chunk_out, before + (c + 1))
                        if not (first and c < 2):
                            act.wait_ge(fold_out, before + (c - 1))
                        a.copy(chunkT[:, (c + half * len(CHUNKS)) % 2, 0:w],
                               ps[0:3 * FEAT + 1, c % 4 * BANK:c % 4 * BANK + w]).then_inc(chunk_copied, 1)

                root(1)
                copy_chunks(0, True, 1)
                root(2)
                for b in range(BLOCKS):
                    a.activation(counted, adj[:, b, :], ACT.Copy, accum_out=src_count[:, b:b + 1])\
                     .then_inc(degree_out, 1)
                    act.wait_ge(degree_out, b + 1)
                act.wait_ge(level_ready, 1)
                for b in range(BLOCKS):
                    last = a.activation(diag1[:, b * P:(b + 1) * P], ident[:], ACT.Copy, scale=level[:, b:b + 1])
                last.then_inc(diag1_ready, 1)
                act.wait_ge(row1_out, 1)
                for at, w in CHUNKS:
                    last = a.copy(row1[:, at:at + w], ps[:, at:at + w])
                last.then_inc(row1_copied, 1)
                act.wait_ge(row2_copied, 1)
                for b in range(BLOCKS):
                    for h, (at, w) in enumerate(HALVES):
                        if b:
                            act.wait_ge(soft_used, 2 * (b - 1) + h + 1)
                        a.activation(exps[:, h, 0, 0:w], row1[:, at:at + w], ACT.Exp, bias=s_src[:, b:b + 1])
                        a.activation(exps[:, h, 1, 0:w], row2[:, at:at + w], ACT.Exp, bias=s_src_small[:, b:b + 1])\
                         .then_inc(exps_ready, 1)
                root(3)
                act.wait_ge(d_root_in, 4)
                a.activation(src_norm[:], src_norm[:], ACT.Sqrt)
                a.activation(dst_norm[:], dst_norm[:], ACT.Sqrt).then_inc(d_root_out, 1)
                with act.Fori(0, STEPS // 2) as s:
                    copy_chunks(s * (2 * len(CHUNKS)) + len(CHUNKS), half=0)
                    copy_chunks(s * (2 * len(CHUNKS)) + 2 * len(CHUNKS), half=1)
                root(5)

            def run_general():
                with act.Fori(0, TILES) as t:
                    act.wait_ge(score_out, t + 1)
                    nc.scalar.activation(score_g[:, 1:2], score_g[:, 0:1], ACT.Tanh, scale=1.0 / sqrt(FEAT))\
                       .then_inc(weight_out, 1)
                for n in (1, 2):
                    act.wait_ge(root_in, n)
                    nc.scalar.activation(stat[:, 2, :], stat[:, 1, :], ACT.Sqrt, bias=eps[:], scale=1.0 / FEAT)\
                       .then_inc(root_out, 1)
                with act.Fori(0, TILES) as t:
                    act.wait_ge(score_out, t + (TILES + 1))
                    nc.scalar.activation(score_g[:, 1:2], score_g[:, 0:1], ACT.Exp).then_inc(weight_out, 1)
                act.wait_ge(root_in, 3)
                nc.scalar.activation(stat[:, 2, :], stat[:, 1, :], ACT.Sqrt, bias=eps[:], scale=1.0 / FEAT)\
                   .then_inc(root_out, 1)
                act.wait_ge(root_in, 4)
                nc.scalar.activation(src_norm[:], src_norm[:], ACT.Sqrt).then_inc(root_out, 1)
                nc.scalar.activation(dst_norm[:], dst_norm[:], ACT.Sqrt).then_inc(root_out, 1)
                act.wait_ge(root_in, 5)
                nc.scalar.activation(stat[:, 2, :], stat[:, 1, :], ACT.Sqrt, bias=eps[:], scale=1.0 / FEAT)\
                   .then_inc(root_out, 1)

            either(act, run_sweep, run_dense, run_general)

        @block.vector
        def _(dve):
            v = nc.vector
            chain = Chain(dve, vector_steps)
            link = chain.link

            def spread(per_node, cols):
                return per_node.unsqueeze(2).to_broadcast([P, BLOCKS, cols])

            def norm_start(link):
                link(v.tensor_reduce(stat[:, 0, :], x[:], AX.X, ALU.add))
                link(v.tensor_scalar(stat[:, 0, :], stat[:, 0, :], -1.0 / FEAT, None, ALU.mult))
                link(v.tensor_tensor(x[:], x[:], spread(stat[:, 0, :], FEAT), ALU.add))
                link(v.tensor_tensor(work[:], x[:], x[:], ALU.mult))
                link(v.tensor_reduce(stat[:, 1, :], work[:], AX.X, ALU.add))

            def norm_end(link):
                link(v.reciprocal(stat[:, 3, :], stat[:, 2, :]))
                link(v.tensor_tensor(x[:], x[:], spread(stat[:, 3, :], FEAT), ALU.mult))

            def split(link, whole, rest, to):
                link(v.tensor_copy(to[0], whole))
                link(v.tensor_tensor(rest, whole, to[0], ALU.subtract))
                link(v.tensor_copy(to[1], rest))
                link(v.tensor_tensor(to[2], rest, to[1], ALU.subtract))

            v.memset(rel_side[:], 0.0).then_inc(cleared, 1)
            for tile, value in ((agg, 0.0), (eps, EPS), (stat, 0.0), (ones, 1.0), (flag_parts, 0.0)):
                link(v.memset(tile[:], value))
            link(v.memset(xT[FEAT:FEAT + 1, :], 1.0))
            dve.wait_ge(inputs_loaded, 16 * LOADS)
            dve.wait_ge(constants_made, CONSTANTS)
            dve.wait_ge(xT_out, 1)
            for c in range(0, NODES_PAD, BANK):
                w = min(BANK, NODES_PAD - c)
                link(v.tensor_copy(xT[0:FEAT, c:c + w], ps[0:FEAT, c:c + w]))
            dve.sem_inc(xT_ready, 1)
            link(v.tensor_copy(rows[:, :, 0:FEAT], x[:]))
            link(v.tensor_tensor(unsorted, checked[:, :, 1], checked[:, :, 3], ALU.is_gt))
            link(v.tensor_reduce(runs_below[:, GROUPS + 1:GROUPS + 2], unsorted, AX.X, ALU.add))
            link(v.tensor_copy(run_last, checked.rearrange("p (r e) c -> p r (e c)", e=RUN)
                               [:, :, (RUN - 1) * EDGE_COLS + 1]))
            n = [ROWS_CHECKED, GROUPS + 1, RUNS]
            link(v.tensor_tensor(below, run_last.unsqueeze(1).to_broadcast(n),
                                 first_dst[0:ROWS_CHECKED, :].unsqueeze(2).to_broadcast(n), ALU.is_lt))
            link(v.tensor_reduce(runs_below[:, 0:GROUPS + 1], below, AX.X, ALU.add))
            dve.wait_ge(projected, 1)
            for b in range(0, BLOCKS, PER_BANK):
                e = min(b + PER_BANK, BLOCKS)
                link(v.tensor_copy(rows[:, b:e, FEAT:ROW], ps_blocks(FEAT, b, e)))
                at = 4 * PER_BANK
                link(v.tensor_copy(dst_rows[:, b:e, :], ps_blocks(FEAT, at + b, at + e)))
            dve.sem_inc(rows_made, 1)
            dve.sem_inc(runs_counted, 1)
            rest = split_rest.rearrange("p (b f) -> p b f", b=BLOCKS)
            split(link, dst_rows[:], rest, [q_parts[:, :, j, :] for j in range(3)])
            dve.sem_inc(parts_split, 1)
            dve.wait_ge(side_loaded, 32)
            split(link, rel_side[:], split_rest[0:DST_AT, 0:REL_COLS], [rel_parts[:, j, :] for j in range(3)])
            dve.wait_ge(runs_summed, 1)
            link(v.tensor_copy(found[:, 0:GROUPS + 2], ps[0:1, 0:GROUPS + 2]))
            link(v.tensor_scalar(window_at[0:1, 0:GROUPS], found[:, 0:GROUPS], float(RUN), None, ALU.mult))
            link(v.tensor_tensor(flag_parts[0:1, 1:2], found[:, 1:2], found[:, 0:1], ALU.subtract))
            span = unsorted[0:1, 0:GROUPS]
            link(v.tensor_tensor(span, found[:, 1:GROUPS + 1], found[:, 0:GROUPS], ALU.subtract))
            link(v.tensor_reduce(flag_parts[0:1, 1:2], span, AX.X, ALU.max))
            link(v.tensor_scalar(flag_parts[0:1, 1:2], flag_parts[0:1, 1:2], WINDOW / RUN - 1.0, None, ALU.is_gt))
            link(v.tensor_tensor(flag_parts[0:1, 2:3], flag_parts[0:1, 1:2], found[:, GROUPS + 1:GROUPS + 2], ALU.max))
            link(v.tensor_scalar(flag_parts[0:1, 2:3], flag_parts[0:1, 2:3], 1.0, None, ALU.min))
            link(v.tensor_copy(flags[0:1, 0:1], flag_parts[0:1, 2:3]))
            link(v.tensor_copy(flags[0:1, 1:2], flag_parts[0:1, 2:3]))
            dve.wait_ge(parts_stored, 16)
            dve.wait_ge(rows_stored, 16)
            dve.sem_inc(flag_ready, 1)

            def run_sweep():
                chain = Chain(dve, sweep_steps)
                link, step = chain.link, chain.step
                link(v.memset(side, 0.0))
                link(v.tensor_copy(side[0:DST_AT], rel_parts.unsqueeze(1).to_broadcast([DST_AT, UNROLL, 3, REL_COLS])))
                link(v.memset(square_sums, 0.0))
                dve.sem_inc(decoded, 1)
                dve.sem_inc(score_ready, UNROLL)
                dve.sem_inc(mixed_ready, 1)

                def decode(i):
                    dve.wait_ge(mixed_ready, i * (2 * UNROLL) + 1)
                    for u in range(UNROLL):
                        dve.wait_ge(window_in[u], i * 16 + 16)
                    src, dst, rel, after = [window[:, :, :, c] for c in range(EDGE_COLS)]
                    step(v.tensor_scalar(block_of, src, 7, None, ALU.logical_shift_right))
                    step(v.tensor_scalar(row_of, src, P - 1, None, ALU.bitwise_and))
                    step(v.tensor_copy(rel_f, rel))
                    step(v.tensor_tensor(coeff[:, :, :, BASES], dst, after, ALU.not_equal))
                    step(v.tensor_tensor(dst_off, dst, first_dst[:, bass.ds(i * UNROLL, UNROLL)].unsqueeze(2)
                                         .to_broadcast([P, UNROLL, SLOTS]), ALU.subtract))
                    chain.wait()
                    step(v.tensor_copy(row_f, row_of))
                    step(v.tensor_scalar(inside, dst_off, 0.0, None, ALU.is_ge))
                    chain.wait()
                    link(v.scalar_tensor_tensor(out=inside, in0=dst_off, scalar=float(GROUP), in1=inside,
                                                op0=ALU.is_lt, op1=ALU.mult))
                    link(v.scalar_tensor_tensor(out=pair_of, in0=block_of, scalar=float(GROUP), in1=dst_off,
                                                op0=ALU.mult, op1=ALU.add))
                    step(v.scalar_tensor_tensor(out=pair_of, in0=pair_of, scalar=1.0, in1=inside,
                                                op0=ALU.add, op1=ALU.mult))
                    step(v.scalar_tensor_tensor(out=dst_off, in0=dst_off, scalar=1.0, in1=inside,
                                                op0=ALU.add, op1=ALU.mult))
                    chain.wait()
                    dve.sem_inc(decoded, 1)

                def make_side(i, u):
                    n = [P, SLOTS, DST_AT]
                    v.tensor_tensor(side_hot[:, u, :, 0:DST_AT], row_no[:, 0:DST_AT].unsqueeze(1).to_broadcast(n),
                                    rel_f[:, u, :].unsqueeze(2).to_broadcast(n), ALU.is_equal)
                    n = [P, SLOTS, GROUP]
                    v.tensor_tensor(side_hot[:, u, :, DST_AT:SIDE], dst_no_bf[:].unsqueeze(1).to_broadcast(n),
                                    dst_off[:, u, :].unsqueeze(2).to_broadcast(n), ALU.is_equal)\
                     .then_inc(side_hot_ready, 1)

                def make_pairs(i, u):
                    for h in range(2):
                        dve.wait_ge(pairs_used, (i * UNROLL + u) * 2 + (h + 1))
                        for k in range(HALF):
                            e = h * HALF + k
                            v.tensor_scalar(row_hot[:, h, k, :], row_no[:], row_f[:, u, e:e + 1], None, ALU.is_equal)
                            last = v.tensor_scalar(pair_hot[:, h, k, :], pair_no[:], pair_of[:, u, e:e + 1], None,
                                                   ALU.is_equal)
                        last.then_inc(pairs_ready, 1)

                def score_edges(i, u):
                    dve.wait_ge(per_edge_copied, i * UNROLL + (u + 2))
                    dve.wait_ge(gathered[u], i * (16 * SLOTS) + 16 * SLOTS)
                    link(v.tensor_tensor(product, per_edge[:, u, :, 0:FEAT], xp[:, u, :, FEAT:ROW], ALU.mult))
                    link(v.tensor_reduce(score[:, u, :], product, AX.X, ALU.add))
                    v.tensor_scalar(score[:, u, :], score[:, u, :], 0.0, None, ALU.max).then_inc(score_ready, 1)

                def make_mixed(i, u):
                    dve.wait_ge(weight_ready, i * UNROLL + (u + 1))
                    link(v.tensor_tensor(coeff[:, u, :, 0:BASES], per_edge[:, u, :, FEAT:REL_COLS],
                                         weight_e[:, u, :].unsqueeze(2).to_broadcast([P, SLOTS, BASES]), ALU.mult))
                    for h in range(2):
                        dve.wait_ge(mixed_used, (i * UNROLL + u) * 2 + (2 * UNROLL - 2 + h + 1))
                        for k in range(HALF):
                            e = h * HALF + k
                            n = [P, GROUP, MIXES]
                            last = v.scalar_tensor_tensor(
                                out=mixed[:, h, k], in0=dst_no[:].unsqueeze(2).to_broadcast(n),
                                scalar=dst_off[:, u, e:e + 1], in1=coeff[:, u, e, :].unsqueeze(1).to_broadcast(n),
                                op0=ALU.is_equal, op1=ALU.mult)
                        last.then_inc(mixed_ready, 1)

                with dve.Fori(0, TURNS) as i:
                    chain.enter(i, TURNS, 11 + 3 * UNROLL)
                    decode(i)
                    make_side(i, 0)
                    for u in range(UNROLL):
                        make_pairs(i, u)
                        if u + 1 < UNROLL:
                            make_side(i, u + 1)
                        score_edges(i, u)
                        if u:
                            make_mixed(i, u - 1)
                    make_mixed(i, UNROLL - 1)
                    chain.leave()
                dve.wait_ge(turn_copied, TURNS + 1)
                link(v.tensor_reduce(flag_parts[:, 1:2], square_sums.rearrange("p h g -> p (h g)"), AX.X, ALU.max))
                link(v.tensor_scalar(flag_parts[:, 0:1], flag_parts[:, 1:2], float(ADJ_MAX ** 2), None, ALU.is_gt))
                dve.sem_inc(flags_counted, 1)
                dve.wait_ge(flags_summed, 1)
                link(v.tensor_scalar(flag_parts[0:1, 3:4], ps[0:1, 0:1], 1.0, None, ALU.min))
                link(v.tensor_copy(flags[0:1, 1:2], flag_parts[0:1, 3:4]))

            def run_dense():
                chain = Chain(dve, dense_steps)
                link = chain.link

                def layer_norm(nth):
                    norm_start(link)
                    dve.sem_inc(d_root_in, 1)
                    dve.wait_ge(d_root_out, nth)
                    norm_end(link)

                def to_agg(cols, nth):
                    dve.sem_inc(layer_copied, 1)
                    dve.wait_ge(layer_nodes, nth)
                    for b in range(0, BLOCKS - 1, PER_BANK):
                        link(v.tensor_copy(agg[:, b:b + PER_BANK, 0:cols], ps_blocks(cols, b, b + PER_BANK)))
                    n = rows_of(BLOCKS - 1)
                    link(v.tensor_copy(agg[0:n, BLOCKS - 1:BLOCKS, 0:cols], ps_blocks(cols, BLOCKS - 1, BLOCKS, n)))

                def chunk_blocks(c):
                    b0 = CHUNKS[c][0] // P
                    return b0, min(b0 + 4, BLOCKS), P if c + 1 < len(CHUNKS) else rows_of(BLOCKS - 1)

                def folded(c, parity, cols):
                    b0, b1, n = chunk_blocks(c)
                    at = (4 + parity) * BANK
                    return ps[0:n, at:at + (b1 - b0) * ROW].rearrange("p (b c) -> p b c", c=ROW)[:, :, 0:cols]

                def split_nodes(half, b0, b1, n, whole, rest):
                    split(link, whole, rest, [parts[0:n, half, b0:b1, j * FEAT:(j + 1) * FEAT] for j in range(3)])
                    dve.sem_inc(parts_ready, 1)

                link(v.memset(parts, 0.0))
                link(v.memset(parts[:, :, :, 3 * FEAT:3 * FEAT + 1], 1.0))
                link(v.memset(fold, 0.0))
                for q in range(0, 3 * FEAT, FEAT):
                    link(v.tensor_copy(fold[q:q + FEAT, 0:FEAT], ident[q:q + FEAT, q:q + FEAT]))
                link(v.memset(fold[3 * FEAT:3 * FEAT + 1, FEAT:FEAT + 1], 1.0))

                to_agg(FEAT, 1)
                link(v.tensor_scalar(work[:], agg[:, :, 0:FEAT], 0.0, None, ALU.max))
                link(v.tensor_tensor(x[:], x[:], work[:], ALU.add))
                layer_norm(1)

                for c in range(len(CHUNKS)):
                    b0, b1, _ = chunk_blocks(c)
                    split_nodes(1, b0, b1, P, x[:, b0:b1, :], work[:, b0:b1, :])
                for c in range(len(CHUNKS)):
                    b0, b1, n = chunk_blocks(c)
                    dve.wait_ge(fold_out, c + 1)
                    link(v.tensor_copy(agg[0:n, b0:b1, :], folded(c, (c + len(CHUNKS)) % 2, FEAT + 1)))
                    dve.sem_inc(fold_taken, 1)
                link(v.tensor_scalar(dst_norm[:], agg[:, :, FEAT], 1.0, None, ALU.max))
                link(v.tensor_tensor(x[:], x[:], agg[:, :, 0:FEAT], ALU.add))
                layer_norm(2)

                for half, to in ((0, s_src), (1, s_dst)):
                    w = attn[:, half * FEAT:(half + 1) * FEAT].unsqueeze(1).to_broadcast([P, BLOCKS, FEAT])
                    link(v.tensor_tensor(work[:], x[:], w, ALU.mult))
                    link(v.tensor_reduce(to, work[:], AX.X, ALU.add))
                link(v.tensor_reduce(spread_of[:, 0:1], s_src, AX.X, ALU.max, apply_absolute_value=True))
                dve.sem_inc(range_in, 1)
                link(v.tensor_scalar(s_src_small, s_src, SLOPE, None, ALU.mult))
                link(v.memset(top, 0.0))
                link(v.tensor_copy(agg[:, :, 0:FEAT], x[:]))
                link(v.memset(agg[:, :, FEAT:FEAT + 1], 1.0))
                dve.wait_ge(range_out, 1)
                link(v.tensor_scalar(spread_of[:, 2:3], spread_of[:, 1:2], 1e-30, 4.0, ALU.max, ALU.mult))
                link(v.reciprocal(spread_of[:, 3:4], spread_of[:, 2:3]))
                link(v.tensor_scalar(s_max, s_src, spread_of[:, 3:4], 0.75, ALU.mult, ALU.add))
                for b in range(BLOCKS):
                    link(v.scalar_tensor_tensor(out=top, in0=adj[:, b, :], scalar=s_max[:, b:b + 1], in1=top,
                                                op0=ALU.min, op1=ALU.max))
                dve.sem_inc(d_top_ready, 1)
                dve.wait_ge(d_top_out, 1)
                n = rows_of(BLOCKS - 1)
                full = (BLOCKS - 1) * P
                link(v.tensor_reduce(s_max[:, 0:BLOCKS - 1], ps[:, 0:full].rearrange("p (b c) -> p b c", c=P),
                                     AX.X, ALU.max))
                link(v.tensor_reduce(s_max[0:n, BLOCKS - 1:BLOCKS], ps[0:n, full:full + P], AX.X, ALU.max))
                link(v.tensor_scalar(s_max, s_max, -0.75, spread_of[:, 2:3], ALU.add, ALU.mult))
                link(v.tensor_tensor(s_max, s_max, s_dst, ALU.add))
                link(v.scalar_tensor_tensor(out=s_max, in0=s_max, scalar=SLOPE, in1=s_max, op0=ALU.mult, op1=ALU.max))
                link(v.tensor_tensor(level, s_dst, s_max, ALU.subtract))
                dve.sem_inc(level_ready, 1)
                link(v.scalar_tensor_tensor(out=s_dst, in0=s_dst, scalar=SLOPE, in1=s_max, op0=ALU.mult,
                                            op1=ALU.subtract))
                for b in range(BLOCKS):
                    last = v.tensor_scalar(diag2[:, b * P:(b + 1) * P], ident[:], s_dst[:, b:b + 1], None, ALU.mult)
                last.then_inc(diag2_ready, 1)
                dve.wait_ge(row2_out, 1)
                for at, w in CHUNKS:
                    link(v.tensor_copy(row2[:, at:at + w], ps[:, at:at + w]))
                dve.sem_inc(row2_copied, 1)
                for b in range(BLOCKS):
                    for h, (at, w) in enumerate(HALVES):
                        dve.wait_ge(exps_ready, 2 * b + h + 1)
                        link(v.tensor_tensor(exps[:, h, 0, 0:w], exps[:, h, 0, 0:w], exps[:, h, 1, 0:w], ALU.max))
                        v.scalar_tensor_tensor(out=exps[:, h, 1, 0:w], in0=exps[:, h, 0, 0:w], scalar=1.0,
                                               in1=adj[:, b, at:at + w], op0=ALU.min, op1=ALU.mult)\
                         .then_inc(soft_ready, 1)
                dve.wait_ge(soft_used, 2 * BLOCKS)
                for c, w in CHUNKS:
                    link(v.tensor_copy(aggT[:, c:c + w], ps[0:FEAT + 1, c:c + w]))
                to_agg(FEAT + 1, 2)
                link(v.tensor_scalar(stat[:, 0, :], agg[:, :, FEAT], 1e-30, None, ALU.max))
                link(v.reciprocal(stat[:, 1, :], stat[:, 0, :]))
                link(v.tensor_tensor(work[:], agg[:, :, 0:FEAT], spread(stat[:, 1, :], FEAT), ALU.mult))
                link(v.tensor_tensor(x[:], x[:], work[:], ALU.add))
                layer_norm(3)

                dve.wait_ge(degree_out, BLOCKS)
                link(v.tensor_scalar(src_norm[:], src_count, 1.0, None, ALU.max))
                dve.sem_inc(d_root_in, 1)
                dve.wait_ge(d_root_out, 4)
                link(v.reciprocal(stat[:, 0, :], src_norm[:]))
                link(v.tensor_copy(src_norm[:], stat[:, 0, :]))
                link(v.reciprocal(stat[:, 0, :], dst_norm[:]))
                link(v.tensor_scalar(dst_norm[:], stat[:, 0, :], 1.0 - ALPHA, None, ALU.mult))
                link(v.tensor_scalar(x0[:], x[:], ALPHA, None, ALU.mult))
                link(v.tensor_tensor(work[:], x[:], spread(src_norm[:], FEAT), ALU.mult))
                for c in range(len(CHUNKS)):
                    b0, b1, _ = chunk_blocks(c)
                    split_nodes(0, b0, b1, P, work[:, b0:b1, :], fresh[:, 0, 0:b1 - b0, :])

                def propagate(before, half):
                    for c in range(len(CHUNKS)):
                        b0, b1, n = chunk_blocks(c)
                        per_node = [n, b1 - b0, FEAT]
                        new, scaled, rest = work[0:n, b0:b1, :], fresh[0:n, 0, 0:b1 - b0, :], fresh[0:n, 1, 0:b1 - b0, :]
                        dve.wait_ge(fold_out, before + (c + 1))
                        link(v.tensor_tensor(new, folded(c, (c + half * len(CHUNKS)) % 2, FEAT),
                                             dst_norm[0:n, b0:b1].unsqueeze(2).to_broadcast(per_node), ALU.mult))
                        dve.sem_inc(fold_taken, 1)
                        link(v.tensor_tensor(new, new, x0[0:n, b0:b1, :], ALU.add))
                        link(v.tensor_tensor(scaled, new, src_norm[0:n, b0:b1].unsqueeze(2).to_broadcast(per_node),
                                             ALU.mult))
                        split_nodes(1 - half, b0, b1, n, scaled, rest)

                with dve.Fori(0, STEPS // 2) as s:
                    chain.enter(s, STEPS // 2, 2 * 7 * len(CHUNKS))
                    propagate(s * (2 * len(CHUNKS)) + len(CHUNKS), 0)
                    propagate(s * (2 * len(CHUNKS)) + 2 * len(CHUNKS), 1)
                    chain.leave()
                link(v.tensor_tensor(x[:], x[:], work[:], ALU.add))
                layer_norm(5)
                dve.sem_inc(result_ready, 1)

            def run_general():
                chain = Chain(dve, general_steps)
                link = chain.link

                def layer_norm(_, roots):
                    norm_start(link)
                    dve.sem_inc(root_in, 1)
                    dve.wait_ge(root_out, roots)
                    norm_end(link)

                def sums_to_nodes(p, nth):
                    cols = SUM_COLS[p]
                    dve.wait_ge(sums_out, nth)
                    for c, w in CHUNKS:
                        link(v.tensor_copy(aggT[0:cols, c:c + w], ps[0:cols, c:c + w]))
                    dve.sem_inc(sums_copied, 1)
                    dve.wait_ge(nodes_out, nth)
                    for b in range(0, BLOCKS, PER_BANK):
                        e = min(b + PER_BANK, BLOCKS - 1)
                        if e > b:
                            link(v.tensor_copy(agg[:, b:e, 0:cols], ps_blocks(cols, b, e)))
                    n = rows_of(BLOCKS - 1)
                    link(v.tensor_copy(agg[0:n, BLOCKS - 1:BLOCKS, 0:cols], ps_blocks(cols, BLOCKS - 1, BLOCKS, n)))

                def top_to_nodes(nth):
                    dve.sem_inc(top_ready, 1)
                    dve.wait_ge(top_out, nth)
                    for b in range(BLOCKS):
                        n = rows_of(b)
                        link(v.tensor_reduce(stat[0:n, 3, b:b + 1], ps[0:n, b * P:(b + 1) * P], AX.X, ALU.max))
                    dve.sem_inc(top_copied, 1)

                def one_hot():
                    link(v.tensor_copy(score_g[:, 2:3], edge[:, 1:2]))
                    link(v.tensor_scalar(hot[:], node_no[:], score_g[:, 2:3], None, ALU.is_equal))

                link(v.memset(zeros, 0.0))
                link(v.memset(val, 1.0))
                link(v.memset(top_g, 0.0))
                link(v.memset(stat[:], 0.0))
                link(v.memset(agg[:], 0.0))
                dve.wait_ge(general_made, 2)
                dve.wait_ge(embedding_in, 16)
                dve.wait_ge(relations_out, 1)
                for c in range(0, FEAT * FEAT, BANK):
                    link(v.tensor_copy(rel_rows[:, FEAT + c:FEAT + c + BANK], ps[0:RELS, c:c + BANK]))
                dve.sem_inc(table_ready[P_REL], 1)

                with dve.Fori(0, TILES) as t:
                    chain.enter(t, TILES, 12)
                    dve.wait_ge(rows_in[P_REL], t * 48 + 48)
                    link(v.tensor_tensor(prod_g[:, 0, :], dst_row[:], rel_row[:, 0:FEAT], ALU.add))
                    link(v.tensor_tensor(prod_g[:, 0, :], prod_g[:, 0, :], src_row[:, FEAT:ROW], ALU.mult))
                    link(v.tensor_reduce(score_g[:, 3:4], prod_g[:, 0, :], AX.X, ALU.add))
                    link(v.tensor_scalar(score_g[:, 0:1], score_g[:, 3:4], 0.0, None, ALU.max))
                    dve.sem_inc(score_out, 1)
                    link(v.tensor_tensor(prod_g[:], rel_row[:, FEAT:].rearrange("p (i o) -> p o i", o=FEAT),
                                         src_row[:, 0:FEAT].unsqueeze(1).to_broadcast([P, FEAT, FEAT]), ALU.mult))
                    link(v.tensor_reduce(val[:, 0:FEAT], prod_g[:], AX.X, ALU.add))
                    link(v.tensor_scalar(edge_no[:], edge_no[:], float(P), None, ALU.add))
                    one_hot()
                    link(v.scalar_tensor_tensor(out=top_g[:], in0=hot[:], scalar=edge_no[:], in1=top_g[:],
                                                op0=ALU.mult, op1=ALU.max))
                    dve.wait_ge(weight_out, t + 1)
                    link(v.tensor_scalar(val[:, 0:FEAT], val[:, 0:FEAT], score_g[:, 1:2], None, ALU.mult))
                    link(v.tensor_copy(score_g[:, 3:4], score_g[:, 1:2]))
                    dve.sem_inc(tile_ready, 1)
                    chain.leave()
                sums_to_nodes(P_REL, nth_sum[P_REL])
                top_to_nodes(1)
                link(v.tensor_scalar(stat[:, 0, :], stat[:, 3, :], 0.0, None, ALU.is_gt))
                link(v.tensor_scalar(stat[:, 3, :], stat[:, 3, :], -1.0, 0.0, ALU.add, ALU.max))
                link(v.tensor_copy(last_no[:], stat[:, 3, :]))
                dve.sem_inc(last_ready, 1)
                dve.wait_ge(last_in, 16 * BLOCKS)
                link(v.tensor_copy(last_src[:].unsqueeze(2), last_edge[:, :, 0:1]))
                dve.sem_inc(last_ready, 1)
                dve.wait_ge(lastT_out, 1)
                for c in range(0, NODES_PAD, BANK):
                    w = min(BANK, NODES_PAD - c)
                    link(v.tensor_copy(lastT[:, c:c + w], ps[0:FEAT, c:c + w]))
                dve.sem_inc(lastT_ready, 1)
                dve.wait_ge(current_out, 1)
                for b in range(0, BLOCKS, PER_BANK):
                    e = min(b + PER_BANK, BLOCKS)
                    link(v.tensor_tensor(work[:, b:e, :], agg[:, b:e, 0:FEAT], ps_blocks(FEAT, b, e), ALU.add))
                link(v.tensor_scalar(work[:], work[:], 0.0, None, ALU.max))
                link(v.tensor_tensor(work[:], work[:], spread(stat[:, 0, :], FEAT), ALU.mult))
                link(v.tensor_tensor(x[:], x[:], work[:], ALU.add))
                layer_norm(1, 1)
                link(v.tensor_copy(rows[:, :, 0:FEAT], x[:]))
                dve.sem_inc(table_ready[P_SUM], 1)

                def value_tiles(p):
                    with dve.Fori(0, TILES) as t:
                        chain.enter(t, TILES, 3)
                        dve.wait_ge(rows_in[p], t * 16 + 16)
                        link(v.tensor_copy(val[:, 0:FEAT], src_row[:, 0:FEAT]))
                        one_hot()
                        dve.sem_inc(tile_ready, 1)
                        chain.leave()

                value_tiles(P_SUM)
                sums_to_nodes(P_SUM, nth_sum[P_SUM])
                link(v.tensor_scalar(dst_norm[:], agg[:, :, FEAT:FEAT + 1].rearrange("p b c -> p (b c)"), 1.0, None,
                                     ALU.max))
                link(v.tensor_tensor(x[:], x[:], agg[:, :, 0:FEAT], ALU.add))
                layer_norm(2, 2)

                link(v.tensor_copy(rows[:, :, 0:FEAT], x[:]))
                for half, to in ((0, rows[:, :, FEAT:FEAT + 1]), (1, dst_rows[:, :, 0:1])):
                    w = attn[:, half * FEAT:(half + 1) * FEAT].unsqueeze(1).to_broadcast([P, BLOCKS, FEAT])
                    link(v.tensor_tensor(work[:], x[:], w, ALU.mult))
                    link(v.tensor_reduce(to.rearrange("p b c -> p (b c)"), work[:], AX.X, ALU.add))
                link(v.memset(top_g[:], -FAR))
                dve.sem_inc(table_ready[P_MAX], 1)

                def edge_score():
                    link(v.tensor_tensor(score_g[:, 0:1], src_row[:, FEAT:FEAT + 1], dst_row[:, 0:1], ALU.add))
                    link(v.scalar_tensor_tensor(out=score_g[:, 3:4], in0=score_g[:, 0:1], scalar=SLOPE,
                                                in1=score_g[:, 0:1], op0=ALU.mult, op1=ALU.max))

                with dve.Fori(0, TILES) as t:
                    chain.enter(t, TILES, 6)
                    dve.wait_ge(rows_in[P_MAX], t * 32 + 32)
                    edge_score()
                    one_hot()
                    link(v.tensor_scalar(hot[:], hot[:], FAR, -FAR, ALU.mult, ALU.add))
                    link(v.scalar_tensor_tensor(out=top_g[:], in0=hot[:], scalar=score_g[:, 3:4], in1=top_g[:],
                                                op0=ALU.add, op1=ALU.max))
                    dve.sem_inc(tile_done, 1)
                    chain.leave()
                top_to_nodes(2)
                link(v.tensor_copy(dst_rows[:, :, 1:2], stat[:, 3, :].unsqueeze(2)))
                dve.sem_inc(table_ready[P_SOFT], 1)
                with dve.Fori(0, TILES) as t:
                    chain.enter(t, TILES, 7)
                    dve.wait_ge(rows_in[P_SOFT], t * 32 + 32)
                    edge_score()
                    link(v.tensor_tensor(score_g[:, 0:1], score_g[:, 3:4], dst_row[:, 1:2], ALU.subtract))
                    dve.sem_inc(score_out, 1)
                    one_hot()
                    dve.wait_ge(weight_out, t + (TILES + 1))
                    link(v.tensor_scalar(val[:, 0:FEAT], src_row[:, 0:FEAT], score_g[:, 1:2], None, ALU.mult))
                    link(v.tensor_copy(val[:, FEAT:FEAT + 1], score_g[:, 1:2]))
                    dve.sem_inc(tile_ready, 1)
                    chain.leave()
                sums_to_nodes(P_SOFT, nth_sum[P_SOFT])
                link(v.tensor_scalar(stat[:, 0, :], agg[:, :, FEAT:FEAT + 1].rearrange("p b c -> p (b c)"), 1e-30, None,
                                     ALU.max))
                link(v.reciprocal(stat[:, 1, :], stat[:, 0, :]))
                link(v.tensor_tensor(work[:], agg[:, :, 0:FEAT], spread(stat[:, 1, :], FEAT), ALU.mult))
                link(v.tensor_tensor(x[:], x[:], work[:], ALU.add))
                layer_norm(3, 3)
                link(v.memset(val[:], 1.0))
                dve.sem_inc(table_ready[P_OUTDEG], 1)

                with dve.Fori(0, TILES) as t:
                    chain.enter(t, TILES, 2)
                    dve.wait_ge(edge_in, t * 16 + (16 * serial[P_OUTDEG] + 16))
                    link(v.tensor_copy(score_g[:, 2:3], edge[:, 0:1]))
                    link(v.tensor_scalar(hot[:], node_no[:], score_g[:, 2:3], None, ALU.is_equal))
                    dve.sem_inc(tile_ready, 1)
                    chain.leave()
                sums_to_nodes(P_OUTDEG, nth_sum[P_OUTDEG])
                link(v.tensor_scalar(src_norm[:], agg[:, :, 0:1].rearrange("p b c -> p (b c)"), 1.0, None, ALU.max))
                dve.sem_inc(root_in, 1)
                dve.wait_ge(root_out, 5)
                link(v.reciprocal(stat[:, 0, :], src_norm[:]))
                link(v.tensor_copy(src_norm[:], stat[:, 0, :]))
                link(v.reciprocal(stat[:, 0, :], dst_norm[:]))
                link(v.tensor_scalar(dst_norm[:], stat[:, 0, :], 1.0 - ALPHA, None, ALU.mult))
                link(v.tensor_scalar(x0[:], x[:], ALPHA, None, ALU.mult))
                link(v.tensor_copy(work[:], x[:]))
                link(v.tensor_tensor(rows[:, :, 0:FEAT], work[:], spread(src_norm[:], FEAT), ALU.mult))
                dve.sem_inc(table_ready[P_PROP], 1)
                PER_STEP = 3 * TILES + len(CHUNKS) + 4 + 3
                with dve.Fori(0, STEPS) as s:
                    chain.enter(s, STEPS, PER_STEP)
                    dve.wait_ge(rows_in_cleared, s + 1)
                    dve.sem_inc(vector_turns, 1)
                    value_tiles(P_PROP)
                    sums_to_nodes(P_PROP, s + nth_sum[P_PROP])
                    link(v.tensor_tensor(work[:], agg[:, :, 0:FEAT], spread(dst_norm[:], FEAT), ALU.mult))
                    link(v.tensor_tensor(work[:], work[:], x0[:], ALU.add))
                    link(v.tensor_tensor(rows[:, :, 0:FEAT], work[:], spread(src_norm[:], FEAT), ALU.mult))
                    dve.sem_inc(table_ready[P_PROP], 1)
                    chain.leave()
                link(v.tensor_tensor(x[:], x[:], work[:], ALU.add))
                layer_norm(5, 6)
                dve.sem_inc(result_ready, 1)
            with dve.If(dve.value_load(flags[0:1, 0:1], min_val=0, max_val=1) == 0):
                run_sweep()
            dve.sem_inc(flag_ready, 1)
            with dve.If(dve.value_load(flags[0:1, 1:2], min_val=0, max_val=1) == 0):
                run_dense()
            with dve.Else():
                run_general()


def kernel(**inputs):
    import numpy as np
    import concourse.bacc as bacc
    from concourse.bass_utils import run_bass_kernel_spmd

    x = np.asarray(inputs["x"])
    x_pad = np.zeros((NODES_PAD, FEAT), x.dtype)
    x_pad[:NODES] = x
    edges = np.zeros((EDGES_PAD, EDGE_COLS), np.int32)
    edges[EDGES:, 1] = NODES
    for c, name in enumerate(("src", "dst", "edge_type_86")):
        edges[:EDGES, c] = np.asarray(inputs[name])
    edges[:-1, 3] = edges[1:, 1]
    edges[-1, 3] = NODES

    def with_bias(w, b):
        return np.concatenate([np.asarray(inputs[w]).T, np.asarray(inputs[b])[None]], 0)

    arrays = {
        "x_pad": x_pad, "edges": edges,
        "weight": np.asarray(inputs["L0_gnn_weight"]).reshape(BASES, FEAT * FEAT),
        "w_comp": np.asarray(inputs["L0_gnn_w_comp"]),
        "w_comp_t": np.asarray(inputs["L0_gnn_w_comp"]).T,
        "self_loop": np.asarray(inputs["L0_gnn_self_loop_weight"]),
        "a1_t": with_bias("L0_gnn_A1_w", "L0_gnn_A1_b"), "a2_t": with_bias("L0_gnn_A2_w", "L0_gnn_A2_b"),
        "rel_emb": np.asarray(inputs["L0_gnn_rel_emb"]),
        "attn_w": np.asarray(inputs["L2_gnn_attn_w"])[None],
    }
    arrays = {k: np.ascontiguousarray(a) for k, a in arrays.items()}
    nc = bacc.Bacc("TRN2", target_bir_lowering=False, num_devices=1)
    aps = {k: nc.dram_tensor(k, a.shape, mybir.dt.from_np(a.dtype), kind="ExternalInput").ap()
           for k, a in arrays.items()}
    out = nc.dram_tensor("out", [NODES_PAD, FEAT], F32, kind="ExternalOutput").ap()
    gnn(nc, out=out, **aps)
    r = run_bass_kernel_spmd(nc, [arrays], core_ids=[0])
    return r.results[0]["out"][:NODES]
```

```python
from contextlib import ExitStack
from math import sqrt

import concourse.bass as bass
from concourse import mybir

F32, I32 = mybir.dt.float32, mybir.dt.int32
BF16, F16, FP8, U8 = mybir.dt.bfloat16, mybir.dt.float16, mybir.dt.float8e4, mybir.dt.uint8
ALU, ACT, AX = mybir.AluOpType, mybir.ActivationFunctionType, mybir.AxisListType

P = 128
NODES, FEAT = 3125, 32
BLOCKS = -(-NODES // P)
NODES_PAD = BLOCKS * P
EDGES = 100000
TILES = -(-EDGES // P)
RELS, BASES = 86, 16
ROW = 64
BANK = 512
CHUNKS = [(c, min(BANK, NODES - c)) for c in range(0, NODES, BANK)]
PER_BANK = BANK // ROW
STEPS, ALPHA = 10, 0.1
SLOPE, EPS = 0.01, 1e-5
FAR = 1e30
REL_ROW = FEAT + FEAT * FEAT
EDGE_COLS = 4

GROUP = 16
GROUPS = -(-NODES // GROUP)
SLOTS = 5
WINDOW = SLOTS * P
PART = 7
UNROLL = 2 * PART
TURNS = GROUPS // UNROLL
AHEAD = 2
SPAN = PART * GROUP
COLS = GROUPS * GROUP
WINDOWS = GROUPS + PART
RUN = 20
ROWS_CHECKED = 125
PER_ROW = EDGES // ROWS_CHECKED
RUNS = PER_ROW // RUN
EDGES_PAD = -(-(EDGES + WINDOW) // P) * P
NOWHERE = NODES_PAD - 1
assert NOWHERE >= (GROUPS + AHEAD) * GROUP
ROWS_BY_SCALAR = 3
PAIRS = BLOCKS * GROUP
assert TURNS * UNROLL == GROUPS and PAIRS <= BANK and WINDOW % RUN == 0
MIXES = BASES + 1
REL_COLS = FEAT + BASES
MIXES_AT_ONCE = 4
MIX_STEPS = -(-MIXES // MIXES_AT_ONCE)
DST_AT = 96
SIDE = DST_AT + GROUP
ADJ_MAX = 16

P_REL, P_SUM, P_MAX, P_SOFT, P_OUTDEG, P_PROP = range(6)
ROWS_GATHERED = {P_REL: 3, P_SUM: 1, P_MAX: 2, P_SOFT: 2, P_OUTDEG: 0, P_PROP: 1}
SUM_COLS = {P_REL: FEAT, P_SUM: FEAT + 1, P_SOFT: FEAT + 1, P_OUTDEG: 1, P_PROP: FEAT}


def rows_of(b):
    return min(P, NODES - b * P)


class Chain:

    def __init__(self, eng, sem):
        self.eng, self.sem, self.count, self.loops = eng, sem, 0, []

    def value(self):
        total = self.count
        for var, per_turn, _, _ in self.loops:
            total = var * per_turn + total
        return total

    def link(self, instruction):
        self.step(instruction)
        self.wait()

    def step(self, instruction):
        instruction.then_inc(self.sem, 1)
        self.count += 1

    def wait(self):
        self.eng.wait_ge(self.sem, self.value())

    def enter(self, var, turns, per_turn):
        self.loops.append((var, per_turn, turns, self.count))

    def leave(self):
        _, per_turn, turns, start = self.loops.pop()
        assert self.count - start == per_turn, (self.count - start, per_turn)
        self.count = start + turns * per_turn


class Carver:

    def __init__(self, whole, words):
        self.whole, self.words, self.at = whole, words, 0

    def cut(self, cols, dt=F32, n=P, n0=0):
        size = {F32: 4, I32: 4, BF16: 2, F16: 2, FP8: 1}[dt]
        words = -(-cols * size // 4)
        ap = self.whole[n0:n0 + n, self.at:self.at + words]
        self.at += words
        assert self.at <= self.words, (self.at, self.words)
        return (ap if dt == F32 else ap.bitcast(dt))[:, 0:cols]


def gnn(nc, x_pad, edges, weight, w_comp, w_comp_t, self_loop, a1_t, a2_t, rel_emb, attn_w, out):
    ctx = ExitStack()
    with ctx:
        def sb(name, shape, dt=F32):
            return ctx.enter_context(nc.sbuf_tensor(name, shape, dt))

        def sem(name):
            return ctx.enter_context(nc.semaphore(name))

        feat_table = nc.dram_tensor("feat_table", [NODES_PAD, ROW], F32, kind="Internal").ap()
        dst_table = nc.dram_tensor("dst_table", [NODES_PAD, FEAT], F32, kind="Internal").ap()
        dst_parts = nc.dram_tensor("dst_parts", [NODES_PAD + P, 3 * FEAT], BF16, kind="Internal").ap()
        rel_table = nc.dram_tensor("rel_table", [RELS, REL_ROW], F32, kind="Internal").ap()

        x = sb("x", [P, BLOCKS, FEAT])
        x0 = sb("x0", [P, BLOCKS, FEAT])
        rows = sb("rows", [P, BLOCKS, ROW])
        dst_rows = sb("dst_rows", [P, BLOCKS, FEAT])
        agg = sb("agg", [P, BLOCKS, FEAT + 1])
        work = sb("work", [P, BLOCKS, FEAT])
        stat = sb("stat", [P, 4, BLOCKS])
        src_norm = sb("src_norm", [P, BLOCKS])
        dst_norm = sb("dst_norm", [P, BLOCKS])
        aggT_parts = sb("aggT", [FEAT + 1, SPAN + COLS])
        aggT = aggT_parts[:, SPAN:SPAN + COLS]
        a12 = sb("a12", [FEAT + 1, 2 * FEAT])
        wc = sb("wc", [BASES, RELS])
        wb = sb("wb", [BASES, FEAT * FEAT])
        sl = sb("sl", [FEAT, FEAT])
        attn = sb("attn", [P, 2 * FEAT])
        mix = sb("mix", [P, MIXES, FEAT])
        rel_side = sb("rel_side", [DST_AT, REL_COLS])
        ident = sb("ident", [P, P])
        ident_bf = sb("ident_bf", [P, P], BF16)
        ones = sb("ones", [P, P])
        eps = sb("eps", [P, 1])
        pair_no = sb("pair_no", [P, PAIRS], F16)
        row_no = sb("row_no", [P, P], BF16)
        dst_no = sb("dst_no", [P, GROUP], BF16)
        first_dst = sb("first_dst", [P, WINDOWS])
        flags = sb("flags", [1, 2], I32)
        window_at = sb("window_at", [1, WINDOWS], I32)
        flag_parts = sb("flag_parts", [P, 4])

        ADJ_WORDS = -(-BLOCKS * COLS // 4)
        adj_words = sb("adj_words", [P, ADJ_WORDS])
        adj = adj_words[:, :].bitcast(FP8)[:, 0:BLOCKS * COLS].rearrange("p (b n) -> p b n", b=BLOCKS)
        adj_bytes = adj_words[:, :].bitcast(U8)[:, 0:BLOCKS * COLS].rearrange("p (b n) -> p b n", b=BLOCKS)
        old = Carver(adj_words, ADJ_WORDS)
        node_no, hot, top_g = old.cut(NODES), old.cut(NODES), old.cut(NODES)
        rel_row, prod_g = old.cut(REL_ROW), old.cut(FEAT * FEAT).rearrange("p (o i) -> p o i", o=FEAT)
        last_row = old.cut(BLOCKS * ROW).rearrange("p (b c) -> p b c", b=BLOCKS)
        lastT = old.cut(NODES_PAD, n=FEAT)
        last_edge = old.cut(BLOCKS * EDGE_COLS, I32).rearrange("p (b c) -> p b c", b=BLOCKS)
        rel_rows = old.cut(REL_ROW, n=RELS)
        last_no, last_src = old.cut(BLOCKS, I32), old.cut(BLOCKS, I32)
        zeros = old.cut(BANK)
        edge, src_row, dst_row = old.cut(EDGE_COLS, I32), old.cut(ROW), old.cut(FEAT)
        score_g, edge_no, val = old.cut(4), old.cut(1), old.cut(FEAT + 1)

        ARENA = 21650
        arena = sb("arena", [P, ARENA])
        prep = Carver(arena, ARENA)
        xT = prep.cut(NODES_PAD, n=FEAT + 1)
        checked = prep.cut(PER_ROW * EDGE_COLS, I32, n=ROWS_CHECKED).rearrange("p (e c) -> p e c", c=EDGE_COLS)
        unsorted = prep.cut(PER_ROW, n=ROWS_CHECKED)
        run_last = prep.cut(RUNS, n=ROWS_CHECKED)
        below = prep.cut(WINDOWS * RUNS, n=ROWS_CHECKED).rearrange("p (g r) -> p g r", r=RUNS)
        runs_below = prep.cut(WINDOWS + 1, n=ROWS_CHECKED)
        q_parts = prep.cut(BLOCKS * 3 * FEAT, BF16).rearrange("p (b j f) -> p b j f", b=BLOCKS, j=3)
        rel_parts = prep.cut(3 * REL_COLS, BF16, n=DST_AT).rearrange("p (j c) -> p j c", j=3)
        split_rest = prep.cut(BLOCKS * FEAT)
        found = prep.cut(WINDOWS + 1, n=1)

        sweep = Carver(arena, ARENA)
        side = sweep.cut(UNROLL * 3 * REL_COLS, BF16, n=SIDE).rearrange("p (u j c) -> p u j c", u=UNROLL, j=3)
        window = sweep.cut(UNROLL * SLOTS * EDGE_COLS, I32).rearrange("p (u k c) -> p u k c", u=UNROLL, k=SLOTS)

        def per_slot(groups=UNROLL, dt=F32):
            return sweep.cut(groups * SLOTS, dt).rearrange("p (u k) -> p u k", u=groups)

        block_of, row_of, inside = per_slot(PART, I32), per_slot(PART, I32), per_slot(PART)
        dst_off, pair_of, row_f, rel_f, score, weight_e = [per_slot() for _ in range(6)]
        coeff = sweep.cut(UNROLL * SLOTS * MIXES).rearrange("p (u k m) -> p u k m", u=UNROLL, k=SLOTS)
        xp = sweep.cut(PART * SLOTS * ROW).rearrange("p (u k c) -> p u k c", u=PART, k=SLOTS)
        side_hot = sweep.cut(UNROLL * SLOTS * SIDE, BF16).rearrange("p (u k s) -> p u k s", u=UNROLL, k=SLOTS)
        side_hotT = sweep.cut(2 * WINDOW, BF16, n=SIDE).rearrange("p (h w) -> p h w", h=2)
        per_edge = sweep.cut(2 * SLOTS * REL_COLS).rearrange("p (h k c) -> p h k c", h=2, k=SLOTS)
        product = sweep.cut(SLOTS * FEAT).rearrange("p (k f) -> p k f", k=SLOTS)
        pair_hot = sweep.cut(2 * SLOTS * PAIRS, BF16).rearrange("p (h k v) -> p h k v", h=2, k=SLOTS)
        row_hot = sweep.cut(2 * SLOTS * P, BF16).rearrange("p (h k v) -> p h k v", h=2, k=SLOTS)
        mixed = sweep.cut(2 * SLOTS * GROUP * MIXES).rearrange("p (h k d m) -> p h k d m", h=2, k=SLOTS, d=GROUP)
        sumsT = sweep.cut(UNROLL * GROUP * MIXES).rearrange("p (d m) -> p d m", m=MIXES)
        squares = sweep.cut(2 * PAIRS, BF16).rearrange("p (h v) -> p h v", h=2)
        turn_fp8 = sweep.cut(2 * BLOCKS * SPAN, FP8)
        turn_adj = turn_fp8.rearrange("p (h b n) -> p h b n", h=2, b=BLOCKS)
        turn_bytes = turn_fp8.bitcast(U8).rearrange("p (h b n) -> p h b n", h=2, b=BLOCKS)
        square_sums = sweep.cut(GROUPS + 1)
        COUNTS, TURNED, FETCHED, MIXED, MOVED = [bank * BANK for bank in (0, 2, 4, 5, 7)]

        dense = Carver(arena, ARENA)
        parts = dense.cut(2 * BLOCKS * P, BF16).rearrange("p (s b c) -> p s b c", s=2, b=BLOCKS)
        fold = dense.cut(FEAT + 1, n=3 * FEAT + 1)
        chunkT = dense.cut(2 * BANK, n=3 * FEAT + 1).rearrange("p (s c) -> p s c", s=2)
        fresh = dense.cut(2 * 4 * FEAT).rearrange("p (s b f) -> p s b f", s=2, b=4)
        counted = dense.cut(NODES, BF16)
        src_count = dense.cut(BLOCKS)
        s_src, s_src_small, s_dst, s_max, level = [dense.cut(BLOCKS) for _ in range(5)]
        spread_of = dense.cut(4)
        keep_at = dense.at
        row1, row2 = dense.cut(NODES), dense.cut(NODES)
        shared_at = dense.at
        diag1, diag2 = dense.cut(NODES_PAD), dense.cut(NODES_PAD)
        dense.at = keep_at
        top = dense.cut(NODES)
        dense.at = shared_at
        PIECES = [(0, 2 * BANK), (2 * BANK, 2 * BANK), (4 * BANK, NODES - 4 * BANK)]
        EXP_BUFFERS = 4
        exps = dense.cut(EXP_BUFFERS * 2 * PIECES[-1][1]).rearrange("p (s e c) -> p s e c", s=EXP_BUFFERS, e=2)

        def exp_pieces():
            for n in range(BLOCKS * len(PIECES)):
                yield (n, n % EXP_BUFFERS, n // len(PIECES)) + PIECES[n % len(PIECES)]

        ps = ctx.enter_context(nc.psum_tensor("ps", [P, 8 * BANK], F32))

        def ps_block(b, cols, n=P, first_bank=0):
            at = first_bank * BANK + b * ROW
            return ps[0:n, at:at + cols]

        def ps_blocks(cols, b0, b1, n=P):
            return ps[0:n, b0 * ROW:b1 * ROW].rearrange("p (b c) -> p b c", c=ROW)[:, :, 0:cols]

        RUNS_AT = 7 * BANK

        inputs_loaded = sem("inputs_loaded")
        constants_made = sem("constants_made")
        cleared = sem("cleared")
        side_loaded = sem("side_loaded")
        vector_steps = sem("vector_steps")
        xT_out, xT_ready = sem("xT_out"), sem("xT_ready")
        projected = sem("projected")
        parts_split, parts_stored = sem("parts_split"), sem("parts_stored")
        dst_rows_made = sem("dst_rows_made")
        rows_made, rows_stored = sem("rows_made"), sem("rows_stored")
        runs_counted, runs_summed = sem("runs_counted"), sem("runs_summed")
        flag_ready = sem("flag_ready")
        window_in = [sem(f"window_in_{u}") for u in range(UNROLL)]
        gathered = [sem(f"gathered_{u}") for u in range(UNROLL)]
        side_in = [sem(f"side_in_{h}") for h in range(2)]
        side_hot_ready, side_hotT_out = sem("side_hot_ready"), sem("side_hotT_out")
        side_hotT_copied = sem("side_hotT_copied")
        decoded = sem("decoded")
        row_distances, row_hot_ready = sem("row_distances"), sem("row_hot_ready")
        pairs_ready, pairs_used, adj_copied = sem("pairs_ready"), sem("pairs_used"), sem("adj_copied")
        per_edge_out, per_edge_copied = sem("per_edge_out"), sem("per_edge_copied")
        score_ready, weight_ready = sem("score_ready"), sem("weight_ready")
        mixed_ready, mixed_used, sumsT_copied = sem("mixed_ready"), sem("mixed_used"), sem("sumsT_copied")
        moved_out, moved_copied, adj_moved = sem("moved_out"), sem("moved_copied"), sem("adj_moved")
        sync_turns, tensor_turns = sem("sync_turns"), sem("tensor_turns")
        sweep_steps, scalar_turns = sem("sweep_steps"), sem("scalar_turns")
        flags_counted, flags_summed = sem("flags_counted"), sem("flags_summed")
        dense_steps = sem("dense_steps")
        layer_sums, layer_nodes, layer_copied = sem("layer_sums"), sem("layer_nodes"), sem("layer_copied")
        d_root_in, d_root_out = sem("d_root_in"), sem("d_root_out")
        parts_ready, chunk_out, chunk_copied = sem("parts_ready"), sem("chunk_out"), sem("chunk_copied")
        fold_out, fold_taken = sem("fold_out"), sem("fold_taken")
        degree_out = sem("degree_out")
        range_in, range_out = sem("range_in"), sem("range_out")
        d_top_ready, d_top_out = sem("d_top_ready"), sem("d_top_out")
        level_ready, diag1_ready, diag2_ready = sem("level_ready"), sem("diag1_ready"), sem("diag2_ready")
        row1_out, row2_out = sem("row1_out"), sem("row2_out")
        row1_copied, row2_copied = sem("row1_copied"), sem("row2_copied")
        larger_ready = sem("larger_ready")
        exps_ready, soft_ready, soft_used = sem("exps_ready"), sem("soft_ready"), sem("soft_used")
        general_steps = sem("general_steps")
        turns, vector_turns = sem("turns"), sem("vector_turns")
        general_made = sem("general_made")
        embedding_in = sem("embedding_in")
        relations_out = sem("relations_out")
        table_ready = [sem(f"table_ready_{p}") for p in range(6)]
        table_stored = sem("table_stored")
        edge_in = sem("edge_in")
        rows_in = [sem(f"rows_in_{p}") for p in range(6)]
        rows_in_cleared = sem("rows_in_cleared")
        score_out, weight_out = sem("score_out"), sem("weight_out")
        tile_ready = sem("tile_ready")
        tile_done = sem("tile_done")
        sums_out, sums_copied, nodes_out = sem("sums_out"), sem("sums_copied"), sem("nodes_out")
        top_ready, top_out, top_copied = sem("top_ready"), sem("top_out"), sem("top_copied")
        last_ready, last_in = sem("last_ready"), sem("last_in")
        lastT_out, lastT_ready, current_out = sem("lastT_out"), sem("lastT_ready"), sem("current_out")
        root_in, root_out = sem("root_in"), sem("root_out")
        result_ready, stored = sem("result_ready"), sem("stored")

        LOADS = 16
        CONSTANTS = 8
        serial = {p: p * TILES for p in range(6)}
        summed = [p for p in range(6) if p != P_MAX]
        nth_sum = {p: n + 1 for n, p in enumerate(summed)}
        TABLES = {P_REL: 2, P_SUM: 3, P_MAX: 5, P_SOFT: 6, P_OUTDEG: 6, P_PROP: 7}

        def either(eng, if_sorted, if_counted, otherwise):
            eng.wait_ge(flag_ready, 1)
            with eng.If(eng.value_load(flags[0:1, 0:1], min_val=0, max_val=1) == 0):
                if_sorted()
            eng.wait_ge(flag_ready, 2)
            with eng.If(eng.value_load(flags[0:1, 1:2], min_val=0, max_val=1) == 0):
                if_counted()
            with eng.Else():
                otherwise()

        block = ctx.enter_context(nc.Block())

        @block.sync
        def _(sp):
            loads = [(x[:], x_pad.rearrange("(b p) f -> p b f", p=P)), (a12[:, 0:FEAT], a1_t), (a12[:, FEAT:2 * FEAT], a2_t),
                     (checked, edges[0:EDGES, :].rearrange("(p e) c -> p e c", p=ROWS_CHECKED)),
                     (wc[:], w_comp_t), (wb[:], weight), (sl[:], self_loop),
                     (attn[:], attn_w.to_broadcast([P, 2 * FEAT]))]
            for q in range(0, P, FEAT):
                loads.append((mix[q:q + FEAT, 0:BASES, :], weight.rearrange("m (i o) -> i m o", i=FEAT)))
                loads.append((mix[q:q + FEAT, BASES, :], self_loop))
            assert len(loads) == LOADS
            for dst, src in loads:
                sp.dma_start(dst, src).then_inc(inputs_loaded, 16)
            sp.wait_ge(cleared, 1)
            sp.dma_start(rel_side[0:RELS, 0:FEAT], rel_emb).then_inc(side_loaded, 16)
            sp.dma_start(rel_side[0:RELS, FEAT:REL_COLS], w_comp).then_inc(side_loaded, 16)
            sp.wait_ge(rows_made, 1)
            sp.dma_start(feat_table.rearrange("(b p) c -> p b c", p=P), rows[:]).then_inc(rows_stored, 16)
            sp.wait_ge(parts_split, 1)
            sp.dma_start(dst_parts[0:NODES_PAD, :].rearrange("(b p) (j f) -> p b j f", p=P, j=3), q_parts)\
              .then_inc(parts_stored, 16)
            sp.dma_start(dst_parts[NODES_PAD:NODES_PAD + P, :].rearrange("p (j f) -> p j f", j=3), q_parts[:, 0])\
              .then_inc(parts_stored, 16)

            def run_sweep():
                sp.wait_ge(parts_stored, 32)

                def load_part(first, h, turn):
                    for n in range(PART):
                        at = sp.value_load(window_at[0:1, bass.ds(first + n, 1)], min_val=0, max_val=EDGES)
                        if turn is not None:
                            sp.wait_ge(score_ready, turn * UNROLL + (h * PART + n + 1))
                            sp.sem_inc(sync_turns, 1)
                        sp.dma_start(window[:, h * PART + n].rearrange("p k c -> p (k c)"),
                                     edges[bass.ds(at, WINDOW), :].rearrange("(p k) c -> p (k c)", p=P))\
                          .then_inc(window_in[h * PART + n], 16)
                    if turn is not None:
                        sp.wait_ge(per_edge_out, turn * UNROLL + (h * PART + PART))
                        sp.sem_inc(sync_turns, 1)
                    else:
                        sp.wait_ge(cleared, 3)
                    for n in range(PART):
                        sp.dma_start(side[DST_AT:SIDE, h * PART + n, :, 0:FEAT],
                                     dst_parts[bass.ds((first + n) * GROUP, GROUP), :]
                                     .rearrange("d (j f) -> d j f", j=3)).then_inc(side_in[h], 16)

                load_part(0, 0, None)
                with sp.Fori(0, TURNS) as i:
                    load_part(i * UNROLL + PART, 1, i)
                    load_part(i * UNROLL + UNROLL, 0, i + 1)

            def run_dense():
                sp.wait_ge(result_ready, 1)
                sp.dma_start(out.rearrange("(b p) f -> p b f", p=P), x[:]).then_inc(stored, 16)
                sp.wait_ge(stored, 16)

            def run_general():
                sp.dma_start(rel_rows[:, 0:FEAT], rel_emb).then_inc(embedding_in, 16)
                table = feat_table.rearrange("(b p) c -> p b c", p=P)
                dtable = dst_table.rearrange("(b p) c -> p b c", p=P)

                def load_tiles(base):
                    with sp.Fori(0, TILES) as t:
                        sp.wait_ge(tile_done, t + (base + 1))
                        sp.dma_start(edge[:], edges[bass.ds(t * P, P), :]).then_inc(edge_in, 16)

                for p in range(P_PROP):
                    sp.wait_ge(table_ready[p], 1)
                    if p in (P_SUM, P_MAX):
                        sp.dma_start(table, rows[:]).then_inc(table_stored, 16)
                    if p in (P_REL, P_MAX, P_SOFT):
                        sp.dma_start(dtable, dst_rows[:]).then_inc(table_stored, 16)
                    if p == P_REL:
                        sp.dma_start(rel_table, rel_rows[:]).then_inc(table_stored, 16)
                    load_tiles(serial[p])
                with sp.Fori(0, STEPS) as s:
                    sp.wait_ge(table_ready[P_PROP], s + 1)
                    sp.dma_start(table, rows[:]).then_inc(table_stored, 16)
                    load_tiles(s * TILES + serial[P_PROP])
                sp.wait_ge(result_ready, 1)
                sp.dma_start(out.rearrange("(b p) f -> p b f", p=P), x[:]).then_inc(stored, 16)
                sp.wait_ge(stored, 16)

            either(sp, run_sweep, run_dense, run_general)

        @block.gpsimd
        def _(pool):
            def numbers(to, pattern, base, step):
                pool.iota(to, pattern=pattern, base=base, channel_multiplier=step,
                          allow_small_or_imprecise_dtypes=True).then_inc(constants_made, 1)

            numbers(first_dst[:], [[GROUP, WINDOWS]], 0, 0)
            numbers(pair_no[:], [[1, PAIRS]], 1, 0)
            numbers(row_no[:], [[1, P]], 0, 0)
            numbers(dst_no[:], [[1, GROUP]], 1, 0)
            for m in (ident, ident_bf):
                pool.memset(m[:], 0.0).then_inc(constants_made, 1)
            pool.wait_ge(constants_made, CONSTANTS - 2)
            for m in (ident, ident_bf):
                pool.affine_select(out=m[:], in_=m[:], compare_op=ALU.not_equal, fill=1.0, base=0,
                                   pattern=[[-1, P]], channel_multiplier=1).then_inc(constants_made, 1)

            def gather(to, table, index, done):
                pool.indirect_dma_start(to, None, table, bass.IndirectOffsetOnAxis(ap=index, axis=0)).then_inc(done, 16)

            def hold():
                pool.sem_inc(turns, 1)

            def run_sweep():
                pool.wait_ge(rows_stored, 16)
                pool.sem_inc(turns, 1)
                with pool.Fori(0, TURNS) as i:
                    for u in range(UNROLL):
                        pool.wait_ge(window_in[u], i * 16 + 16)
                        pool.wait_ge(mixed_used, i * UNROLL + (u + PART + 1))
                        hold()
                        for k in range(SLOTS):
                            gather(xp[:, u % PART, k, :], feat_table, window[:, u, k, 0:1], gathered[u])

            def run_dense():
                pool.wait_ge(range_in, 1)
                pool.partition_all_reduce(spread_of[:, 1:2], spread_of[:, 0:1], P, bass.bass_isa.ReduceOp.max)\
                    .then_inc(range_out, 1)

            def run_general():
                pool.iota(node_no, pattern=[[1, NODES]], base=0, channel_multiplier=0,
                          allow_small_or_imprecise_dtypes=True).then_inc(general_made, 1)
                pool.iota(edge_no, pattern=[[1, 1]], base=1 - P, channel_multiplier=1,
                          allow_small_or_imprecise_dtypes=True).then_inc(general_made, 1)

                def gather_tiles(p, tile, step=None):
                    with pool.Fori(0, TILES) as t:
                        pool.wait_ge(edge_in, (t + tile) * 16 + 16)
                        hold()
                        gather(src_row[:], feat_table, edge[:, 0:1], rows_in[p])
                        if ROWS_GATHERED[p] >= 2:
                            gather(dst_row[:], dst_table, edge[:, 1:2], rows_in[p])
                        if ROWS_GATHERED[p] >= 3:
                            gather(rel_row[:], rel_table, edge[:, 2:3], rows_in[p])

                for p in range(P_PROP):
                    if ROWS_GATHERED[p]:
                        pool.wait_ge(table_stored, 16 * TABLES[p])
                        gather_tiles(p, serial[p])
                    if p == P_REL:
                        pool.wait_ge(last_ready, 1)
                        for b in range(BLOCKS):
                            gather(last_edge[:, b, :], edges, last_no[:, b:b + 1], last_in)
                        pool.wait_ge(last_ready, 2)
                        for b in range(BLOCKS):
                            gather(last_row[:, b, :], feat_table, last_src[:, b:b + 1], last_in)
                with pool.Fori(0, STEPS) as s:
                    pool.wait_ge(table_stored, s * 16 + 16 * TABLES[P_PROP])
                    hold()
                    n = rows_in[P_PROP].num
                    pool.dma_reset(range(n, n + 1))
                    pool.sem_clear(rows_in[P_PROP])
                    pool.sem_inc(rows_in_cleared, 1)
                    gather_tiles(P_PROP, s * TILES + serial[P_PROP])

            either(pool, run_sweep, run_dense, run_general)

        @block.tensor
        def _(pe):
            pe.wait_ge(inputs_loaded, 16 * LOADS)
            pe.wait_ge(constants_made, CONSTANTS)
            for b in range(BLOCKS):
                mm = nc.tensor.matmul(ps[0:FEAT, b * P:(b + 1) * P], x[:, b, :], ident[:], start=True, stop=True)
                if b % 4 == 3 or b == BLOCKS - 1:
                    mm.then_inc(xT_out, 1)
            pe.wait_ge(cleared, 2)
            for b in range(BLOCKS):
                if b % 4 == 0:
                    pe.wait_ge(xT_ready, b // 4 + 1)
                mm = nc.tensor.matmul(ps_block(b, 2 * FEAT), xT[:, b * P:(b + 1) * P], a12[:], start=True, stop=True)
                if b % PER_BANK == PER_BANK - 1 or b == BLOCKS - 1:
                    mm.then_inc(projected, 1)
            pe.wait_ge(runs_counted, 1)
            nc.tensor.matmul(ps[:, RUNS_AT:RUNS_AT + WINDOWS + 1], ones[0:ROWS_CHECKED, :], runs_below,
                             start=True, stop=True).then_inc(runs_summed, 1)

            def run_sweep():
                for s, n in ((pairs_used, 2), (mixed_used, UNROLL), (per_edge_out, UNROLL), (moved_out, 1)):
                    pe.sem_inc(s, n)

                def transpose_side(i, u):
                    pe.wait_ge(side_hot_ready, i * UNROLL + (u + 1))
                    pe.wait_ge(side_hotT_copied, i * UNROLL + (u + 1))
                    for k in range(SLOTS):
                        mm = nc.tensor.matmul(ps[0:SIDE, TURNED + k * P:TURNED + (k + 1) * P],
                                              side_hot[:, u % UNROLL, k, :], ident_bf[:], start=True, stop=True)
                    mm.then_inc(side_hotT_out, 1)

                def fetch_per_edge(i, u):
                    pe.wait_ge(side_hotT_copied, i * UNROLL + (u + 2))
                    s, turn = u % UNROLL, i + u // UNROLL
                    if s % PART == 0:
                        pe.wait_ge(side_in[s // PART], turn * (16 * PART) + 16 * PART)
                    pe.wait_ge(per_edge_copied, i * UNROLL + (u + 1))
                    for k in range(SLOTS):
                        for j in range(3):
                            mm = nc.tensor.matmul(ps[:, FETCHED + k * REL_COLS:FETCHED + (k + 1) * REL_COLS],
                                                  side_hotT[:, u % 2, k * P:(k + 1) * P], side[:, s, j, :],
                                                  start=(j == 0), stop=(j == 2))
                    mm.then_inc(per_edge_out, 1)

                def count_pairs(i, u):
                    pe.wait_ge(adj_copied, i * UNROLL + (u + 1))
                    pe.wait_ge(pairs_ready, i * UNROLL + (u + 1))
                    pe.wait_ge(row_hot_ready, i * UNROLL + (u + 2))
                    at = COUNTS + u % 2 * BANK
                    for k in range(SLOTS):
                        mm = nc.tensor.matmul(ps[:, at:at + PAIRS], row_hot[:, u % 2, k, :], pair_hot[:, u % 2, k, :],
                                              start=(k == 0), stop=(k == SLOTS - 1))
                    mm.then_inc(pairs_used, 1)

                def sum_mixed(i, u):
                    pe.wait_ge(sumsT_copied, i * UNROLL + (u + 1))
                    pe.wait_ge(mixed_ready, i * UNROLL + (u + 2))
                    at = MIXED + u % 2 * BANK
                    for k in range(SLOTS):
                        q = k % 4
                        mm = nc.tensor.matmul(ps[q * FEAT:(q + 1) * FEAT, at:at + GROUP * MIXES],
                                              xp[:, u % PART, k, 0:FEAT], mixed[:, u % 2, k].rearrange("p d m -> p (d m)"),
                                              start=(k < 4), stop=(k + 4 >= SLOTS), tile_position=(0, q * FEAT))
                    mm.then_inc(mixed_used, 1)

                def times_bases(i, h, mixes):
                    pe.wait_ge(sumsT_copied, i * UNROLL + (h * PART + PART + 2))
                    pe.wait_ge(moved_copied, i * 2 + (h + 2))
                    at = h % 2 * SPAN
                    for m in mixes:
                        mm = nc.tensor.matmul(ps[0:FEAT, MOVED:MOVED + SPAN], mix[:, m, :], sumsT[:, at:at + SPAN, m],
                                              start=(m == 0), stop=(m == MIXES - 1))
                    if m == MIXES - 1:
                        mm.then_inc(moved_out, 1)

                pe.wait_ge(mixed_ready, 1)
                transpose_side(0, 0)
                transpose_side(0, 1)
                fetch_per_edge(0, 0)
                count_pairs(0, 0)
                with pe.Fori(0, TURNS) as i:
                    for u in range(UNROLL):
                        fetch_per_edge(i, u + 1)
                        transpose_side(i, u + 2)
                        if 1 <= u % PART <= MIX_STEPS:
                            first = (u % PART - 1) * MIXES_AT_ONCE
                            times_bases(i, u // PART - 1, range(first, min(first + MIXES_AT_ONCE, MIXES)))
                        count_pairs(i, u + 1)
                        sum_mixed(i, u)
                times_bases(TURNS, -1, range(MIXES))
                pe.wait_ge(flags_counted, 1)
                nc.tensor.matmul(ps[:, 0:1], ones[:], flag_parts[:, 0:1], start=True, stop=True)\
                  .then_inc(flags_summed, 1)

            def run_dense():
                def to_nodes(cols, nth):
                    for b in range(BLOCKS):
                        if b % 4 == 0:
                            pe.wait_ge(layer_copied, (nth - 1) * len(CHUNKS) + b // 4 + 1)
                        mm = nc.tensor.matmul(ps_block(b, cols, rows_of(b)), aggT[0:cols, b * P:b * P + rows_of(b)],
                                              ident[0:cols, 0:cols], start=True, stop=True)
                    mm.then_inc(layer_nodes, 1)

                def fold_chunk(c, before, parity):
                    pe.wait_ge(chunk_copied, before + (c + 1))
                    pe.wait_ge(fold_taken, before + (c + 1))
                    at = CHUNKS[c][0]
                    for b in range(at // P, min(at // P + 4, BLOCKS)):
                        n = rows_of(b)
                        col = (4 + parity) * BANK + (b * P - at) // P * ROW
                        mm = nc.tensor.matmul(ps[0:n, col:col + FEAT + 1],
                                              chunkT[:, parity, b * P - at:b * P - at + n], fold,
                                              start=True, stop=True)
                    mm.then_inc(fold_out, 1)

                def neighbour_sum(before, half):
                    early = 5 * 4
                    order = [(0, 0, early), (1, 0, early), (0, early, BLOCKS), (1, early, BLOCKS)]
                    order += [(c, 0, BLOCKS) for c in range(2, len(CHUNKS))]
                    for step, (c, b0, b1) in enumerate(order):
                        at, w = CHUNKS[c]
                        for b in range(b0, b1):
                            if c == 0 and b % 4 == 0:
                                pe.wait_ge(parts_ready, before + (b // 4 + 1))
                                pe.sem_inc(tensor_turns, 1)
                            bank = c % 4 * BANK
                            mm = nc.tensor.matmul(ps[:, bank:bank + w], parts[:, half, b, :], adj[:, b, at:at + w],
                                                  start=(b == 0), stop=(b == BLOCKS - 1))
                        if b1 == BLOCKS:
                            mm.then_inc(chunk_out, 1)
                            if c:
                                fold_chunk(c - 1, before, (c - 1 + half * len(CHUNKS)) % 2)
                    c = len(CHUNKS) - 1
                    fold_chunk(c, before, (c + half * len(CHUNKS)) % 2)

                pe.sem_inc(fold_taken, 2)
                to_nodes(FEAT, 1)
                neighbour_sum(0, 1)
                pe.wait_ge(d_top_ready, 1)
                for b in range(BLOCKS):
                    n = rows_of(b)
                    mm = nc.tensor.matmul(ps[0:n, b * P:(b + 1) * P], top[:, b * P:b * P + n], ident[:],
                                          start=True, stop=True)
                    if b % 4 == 3 or b == BLOCKS - 1:
                        mm.then_inc(d_top_out, 1)
                for at, w in CHUNKS:
                    pe.wait_ge(diag1_ready, -(-(at + w) // P))
                    nc.tensor.matmul(ps[:, at:at + w], ones[:], diag1[:, at:at + w], start=True, stop=True)\
                      .then_inc(row1_out, 1)
                for c, (at, w) in enumerate(CHUNKS):
                    pe.wait_ge(row1_copied, c + 1)
                    pe.wait_ge(diag2_ready, -(-(at + w) // P))
                    nc.tensor.matmul(ps[:, at:at + w], ones[:], diag2[:, at:at + w], start=True, stop=True)\
                      .then_inc(row2_out, 1)
                pe.wait_ge(row2_copied, len(CHUNKS))
                for nth, buf, b, at, w in exp_pieces():
                    pe.wait_ge(soft_ready, nth + 1)
                    for c in range(0, w, BANK):
                        cw = min(BANK, w - c)
                        mm = nc.tensor.matmul(ps[0:FEAT + 1, at + c:at + c + cw], agg[:, b, :],
                                              exps[:, buf, 1, c:c + cw], start=(b == 0), stop=(b == BLOCKS - 1))
                    mm.then_inc(soft_used, 1)
                to_nodes(FEAT + 1, 2)
                with pe.Fori(0, STEPS // 2) as s:
                    neighbour_sum(s * (2 * len(CHUNKS)) + len(CHUNKS), 0)
                    neighbour_sum(s * (2 * len(CHUNKS)) + 2 * len(CHUNKS), 1)

            def run_general():
                for c in range(FEAT * FEAT // BANK):
                    mm = nc.tensor.matmul(ps[0:RELS, c * BANK:(c + 1) * BANK], wc[:], wb[:, c * BANK:(c + 1) * BANK],
                                          start=True, stop=True)
                mm.then_inc(relations_out, 1)
                pe.sem_inc(tile_done, 1)

                def edge_sums(p, tile):
                    cols = SUM_COLS[p]
                    for c, w in CHUNKS:
                        nc.tensor.matmul(ps[0:cols, c:c + w], zeros[:, 0:cols], zeros[:, 0:w], start=True, stop=False)
                    with pe.Fori(0, TILES) as t:
                        pe.wait_ge(tile_ready, t + tile + 1)
                        for c, w in CHUNKS:
                            mm = nc.tensor.matmul(ps[0:cols, c:c + w], val[:, 0:cols], hot[:, c:c + w],
                                                  start=False, stop=False)
                        mm.then_inc(tile_done, 1)
                    for c, w in CHUNKS:
                        mm = nc.tensor.matmul(ps[0:cols, c:c + w], zeros[:, 0:cols], zeros[:, 0:w], start=False, stop=True)
                    mm.then_inc(sums_out, 1)

                def to_nodes(p, nth):
                    pe.wait_ge(sums_copied, nth)
                    cols = SUM_COLS[p]
                    for b in range(BLOCKS):
                        mm = nc.tensor.matmul(ps_block(b, cols, rows_of(b)), aggT[0:cols, b * P:b * P + rows_of(b)],
                                              ident[0:cols, 0:cols], start=True, stop=True)
                    mm.then_inc(nodes_out, 1)

                def top_to_nodes(nth):
                    pe.wait_ge(top_ready, nth)
                    for b in range(BLOCKS):
                        n = rows_of(b)
                        mm = nc.tensor.matmul(ps[0:n, b * P:(b + 1) * P], top_g[:, b * P:b * P + n], ident[:],
                                              start=True, stop=True)
                    mm.then_inc(top_out, 1)

                for p in range(P_PROP):
                    pe.wait_ge(table_ready[p], 1)
                    if p != P_MAX:
                        edge_sums(p, (nth_sum[p] - 1) * TILES)
                        to_nodes(p, nth_sum[p])
                    if p == P_REL:
                        top_to_nodes(1)
                        pe.wait_ge(last_in, 16 * 2 * BLOCKS)
                        pe.wait_ge(top_copied, 1)
                        for b in range(BLOCKS):
                            mm = nc.tensor.matmul(ps[0:FEAT, b * P:(b + 1) * P], last_row[:, b, 0:FEAT], ident[:],
                                                  start=True, stop=True)
                        mm.then_inc(lastT_out, 1)
                        pe.wait_ge(lastT_ready, 1)
                        for b in range(BLOCKS):
                            mm = nc.tensor.matmul(ps_block(b, FEAT), lastT[:, b * P:(b + 1) * P], sl[:],
                                                  start=True, stop=True)
                        mm.then_inc(current_out, 1)
                    if p == P_MAX:
                        top_to_nodes(2)
                with pe.Fori(0, STEPS) as s:
                    pe.wait_ge(table_ready[P_PROP], s + 1)
                    edge_sums(P_PROP, s * TILES + (nth_sum[P_PROP] - 1) * TILES)
                    to_nodes(P_PROP, s + nth_sum[P_PROP])

            either(pe, run_sweep, run_dense, run_general)

        @block.scalar
        def _(act):
            a = nc.scalar

            act.wait_ge(inputs_loaded, 16 * LOADS)
            a.copy(rows[:, :, 0:FEAT], x[:])
            for nth, c in enumerate(range(0, NODES_PAD, BANK)):
                w = min(BANK, NODES_PAD - c)
                act.wait_ge(xT_out, nth + 1)
                a.copy(xT[0:FEAT, c:c + w], ps[0:FEAT, c:c + w]).then_inc(xT_ready, 1)
            for nth, b in enumerate(range(0, BLOCKS, PER_BANK)):
                e = min(b + PER_BANK, BLOCKS)
                act.wait_ge(projected, nth + 1)
                last_rows = a.copy(rows[:, b:e, FEAT:ROW], ps_blocks(FEAT, b, e))
                last_dst = a.copy(dst_rows[:, b:e, :], ps_blocks(ROW, b, e)[:, :, FEAT:ROW])
            last_rows.then_inc(rows_made, 1)
            last_dst.then_inc(dst_rows_made, 1)

            def run_sweep():
                for s, n in ((side_hotT_copied, 1), (adj_copied, 2), (per_edge_copied, 1), (sumsT_copied, 2),
                             (moved_copied, 1), (adj_moved, 2), (row_hot_ready, 1)):
                    act.sem_inc(s, n)

                def make_rows(i, u):
                    s, turn, h = u % UNROLL, i + u // UNROLL, u % 2
                    if s % PART == 0:
                        act.wait_ge(decoded, turn * 2 + (s // PART + 1))
                    act.wait_ge(pairs_used, i * UNROLL + (u + 1))
                    for k in range(ROWS_BY_SCALAR):
                        last = a.activation(row_hot[:, h, k, :], row_no[:], ACT.Square, bias=row_f[:, s, k:k + 1],
                                            scale=-1.0)
                    last.then_inc(row_distances, 1)
                    act.wait_ge(row_distances, i * UNROLL + (u + 1))
                    hot_rows = row_hot[:, h, 0:ROWS_BY_SCALAR].rearrange("p k v -> p (k v)")
                    a.activation(hot_rows, hot_rows, ACT.Relu, bias=1.0, scale=-1.0).then_inc(row_hot_ready, 1)

                def copy_side(i, u):
                    act.wait_ge(side_hotT_out, i * UNROLL + (u + 1))
                    act.wait_ge(per_edge_out, i * UNROLL + (u + UNROLL - 1))
                    a.copy(side_hotT[:, u % 2, :], ps[0:SIDE, TURNED:TURNED + WINDOW]).then_inc(side_hotT_copied, 1)

                def copy_per_edge(i, u):
                    act.wait_ge(per_edge_out, i * UNROLL + (u + UNROLL + 1))
                    act.wait_ge(mixed_ready, i * UNROLL + max(u, 1))
                    a.copy(per_edge[:, u % 2].rearrange("p k c -> p (k c)"),
                           ps[:, FETCHED:FETCHED + SLOTS * REL_COLS]).then_inc(per_edge_copied, 1)

                def copy_adj(i, u):
                    s, turn = u % UNROLL, i + u // UNROLL
                    if s % PART == 0:
                        act.wait_ge(adj_moved, turn * 2 + (s // PART + 1))
                    act.wait_ge(pairs_used, i * UNROLL + (u + 3))
                    act.wait_ge(adj_copied, i * UNROLL + (u + 1))
                    act.sem_inc(scalar_turns, 1)
                    at = COUNTS + u % 2 * BANK
                    a.activation(squares[:, u % 2, :], ps[:, at:at + PAIRS], ACT.Square,
                                 accum_out=square_sums[:, bass.ds(i * UNROLL + u, 1)])
                    d0 = s % PART * GROUP
                    a.activation(turn_adj[:, s // PART, :, d0:d0 + GROUP],
                                 ps[:, at:at + PAIRS].rearrange("p (b d) -> p b d", d=GROUP), ACT.Copy,
                                 saturate=False).then_inc(adj_copied, 1)

                def copy_sums(i, u):
                    act.wait_ge(mixed_used, i * UNROLL + (u + UNROLL + 1))
                    if u % PART == 0:
                        act.wait_ge(moved_out, i * 2 + (u // PART + 1))
                    at = MIXED + u % 2 * BANK
                    a.copy(sumsT[:, u * GROUP:(u + 1) * GROUP, :].rearrange("p d m -> p (d m)"),
                           ps[:, at:at + GROUP * MIXES]).then_inc(sumsT_copied, 1)

                def move_adj(i, h):
                    act.wait_ge(adj_copied, i * UNROLL + (h * PART + PART + 2))
                    act.sem_inc(scalar_turns, 1)
                    a.activation(adj_bytes[:, :, bass.ds(i * (2 * SPAN) + h * SPAN, SPAN)], turn_bytes[:, h],
                                 ACT.Copy).then_inc(adj_moved, 1)

                def move_sums(i, h):
                    act.wait_ge(moved_out, i * 2 + (h + 3))
                    act.sem_inc(scalar_turns, 1)
                    a.copy(aggT_parts[0:FEAT, bass.ds(i * (2 * SPAN) + (h + 1) * SPAN, SPAN)],
                           ps[0:FEAT, MOVED:MOVED + SPAN])\
                     .then_inc(moved_copied, 1)

                make_rows(0, 0)
                copy_side(0, 0)
                make_rows(0, 1)
                copy_side(0, 1)
                copy_per_edge(0, 0)
                copy_adj(0, 0)
                with act.Fori(0, TURNS) as i:
                    for u in range(UNROLL):
                        act.wait_ge(score_ready, i * UNROLL + (UNROLL + u + 1))
                        a.activation(weight_e[:, u, :], score[:, u, :], ACT.Tanh, scale=1.0 / sqrt(FEAT))\
                         .then_inc(weight_ready, 1)
                        copy_per_edge(i, u + 1)
                        copy_side(i, u + 2)
                        make_rows(i, u + 2)
                        if u % PART == PART - 1:
                            move_adj(i, u // PART)
                        copy_adj(i, u + 1)
                        copy_sums(i, u)
                        if u % PART == MIX_STEPS + 1:
                            move_sums(i, u // PART - 1)
                move_sums(TURNS, -1)

            def run_dense():
                def root(nth):
                    act.wait_ge(d_root_in, nth)
                    a.activation(stat[:, 2, :], stat[:, 1, :], ACT.Sqrt, bias=eps[:], scale=1.0 / FEAT)\
                     .then_inc(d_root_out, 1)

                def copy_chunks(before, first=False, half=0):
                    for c, (at, w) in enumerate(CHUNKS):
                        act.wait_ge(chunk_out, before + (c + 1))
                        if not (first and c < 2):
                            act.wait_ge(fold_out, before + (c - 1))
                        a.copy(chunkT[:, (c + half * len(CHUNKS)) % 2, 0:w],
                               ps[0:3 * FEAT + 1, c % 4 * BANK:c % 4 * BANK + w]).then_inc(chunk_copied, 1)

                root(1)
                copy_chunks(0, True, 1)
                root(2)
                for b in range(BLOCKS):
                    a.activation(counted, adj[:, b, 0:NODES], ACT.Copy, accum_out=src_count[:, b:b + 1])\
                     .then_inc(degree_out, 1)
                    act.wait_ge(degree_out, b + 1)
                act.wait_ge(level_ready, 1)
                for b in range(BLOCKS):
                    a.activation(diag1[:, b * P:(b + 1) * P], ident[:], ACT.Copy, scale=level[:, b:b + 1])\
                     .then_inc(diag1_ready, 1)
                for c, (at, w) in enumerate(CHUNKS):
                    act.wait_ge(row1_out, c + 1)
                    a.copy(row1[:, at:at + w], ps[:, at:at + w]).then_inc(row1_copied, 1)
                act.wait_ge(row2_copied, len(CHUNKS))
                for nth, buf, b, at, w in exp_pieces():
                    if nth >= EXP_BUFFERS:
                        act.wait_ge(soft_used, nth - EXP_BUFFERS + 1)
                    a.activation(exps[:, buf, 0, 0:w], row1[:, at:at + w], ACT.Exp, bias=s_src[:, b:b + 1])
                    a.activation(exps[:, buf, 1, 0:w], row2[:, at:at + w], ACT.Exp, bias=s_src_small[:, b:b + 1])\
                     .then_inc(exps_ready, 1)
                root(3)
                act.wait_ge(d_root_in, 4)
                a.activation(src_norm[:], src_norm[:], ACT.Sqrt)
                a.activation(dst_norm[:], dst_norm[:], ACT.Sqrt).then_inc(d_root_out, 1)
                with act.Fori(0, STEPS // 2) as s:
                    copy_chunks(s * (2 * len(CHUNKS)) + len(CHUNKS), half=0)
                    copy_chunks(s * (2 * len(CHUNKS)) + 2 * len(CHUNKS), half=1)
                root(5)

            def run_general():
                with act.Fori(0, TILES) as t:
                    act.wait_ge(score_out, t + 1)
                    nc.scalar.activation(score_g[:, 1:2], score_g[:, 0:1], ACT.Tanh, scale=1.0 / sqrt(FEAT))\
                       .then_inc(weight_out, 1)
                for n in (1, 2):
                    act.wait_ge(root_in, n)
                    nc.scalar.activation(stat[:, 2, :], stat[:, 1, :], ACT.Sqrt, bias=eps[:], scale=1.0 / FEAT)\
                       .then_inc(root_out, 1)
                with act.Fori(0, TILES) as t:
                    act.wait_ge(score_out, t + (TILES + 1))
                    nc.scalar.activation(score_g[:, 1:2], score_g[:, 0:1], ACT.Exp).then_inc(weight_out, 1)
                act.wait_ge(root_in, 3)
                nc.scalar.activation(stat[:, 2, :], stat[:, 1, :], ACT.Sqrt, bias=eps[:], scale=1.0 / FEAT)\
                   .then_inc(root_out, 1)
                act.wait_ge(root_in, 4)
                nc.scalar.activation(src_norm[:], src_norm[:], ACT.Sqrt).then_inc(root_out, 1)
                nc.scalar.activation(dst_norm[:], dst_norm[:], ACT.Sqrt).then_inc(root_out, 1)
                act.wait_ge(root_in, 5)
                nc.scalar.activation(stat[:, 2, :], stat[:, 1, :], ACT.Sqrt, bias=eps[:], scale=1.0 / FEAT)\
                   .then_inc(root_out, 1)

            either(act, run_sweep, run_dense, run_general)

        @block.vector
        def _(dve):
            v = nc.vector
            chain = Chain(dve, vector_steps)
            link = chain.link

            def spread(per_node, cols):
                return per_node.unsqueeze(2).to_broadcast([P, BLOCKS, cols])

            def norm_start(link):
                link(v.tensor_reduce(stat[:, 0, :], x[:], AX.X, ALU.add))
                link(v.tensor_scalar(stat[:, 0, :], stat[:, 0, :], -1.0 / FEAT, None, ALU.mult))
                link(v.tensor_tensor(x[:], x[:], spread(stat[:, 0, :], FEAT), ALU.add))
                link(v.tensor_tensor(work[:], x[:], x[:], ALU.mult))
                link(v.tensor_reduce(stat[:, 1, :], work[:], AX.X, ALU.add))

            def norm_end(link):
                link(v.reciprocal(stat[:, 3, :], stat[:, 2, :]))
                link(v.tensor_tensor(x[:], x[:], spread(stat[:, 3, :], FEAT), ALU.mult))

            def split(link, whole, rest, to):
                link(v.tensor_copy(to[0], whole))
                link(v.tensor_tensor(rest, whole, to[0], ALU.subtract))
                link(v.tensor_copy(to[1], rest))
                link(v.tensor_tensor(to[2], rest, to[1], ALU.subtract))

            v.memset(rel_side[:], 0.0).then_inc(cleared, 1)
            for tile, value in ((agg, 0.0), (eps, EPS), (stat, 0.0), (ones, 1.0), (flag_parts, 0.0)):
                link(v.memset(tile[:], value))
            link(v.memset(xT[FEAT:FEAT + 1, :], 1.0))
            dve.sem_inc(cleared, 1)
            dve.wait_ge(inputs_loaded, 16 * LOADS)
            dve.wait_ge(constants_made, CONSTANTS)
            link(v.tensor_tensor(unsorted, checked[:, :, 1], checked[:, :, 3], ALU.is_gt))
            link(v.tensor_reduce(runs_below[:, WINDOWS:WINDOWS + 1], unsorted, AX.X, ALU.add))
            link(v.tensor_copy(run_last, checked.rearrange("p (r e) c -> p r (e c)", e=RUN)
                               [:, :, (RUN - 1) * EDGE_COLS + 1]))
            n = [ROWS_CHECKED, WINDOWS, RUNS]
            link(v.tensor_tensor(below, run_last.unsqueeze(1).to_broadcast(n),
                                 first_dst[0:ROWS_CHECKED, :].unsqueeze(2).to_broadcast(n), ALU.is_lt))
            link(v.tensor_reduce(runs_below[:, 0:WINDOWS], below, AX.X, ALU.add))
            dve.sem_inc(runs_counted, 1)
            dve.wait_ge(dst_rows_made, 1)
            rest = split_rest.rearrange("p (b f) -> p b f", b=BLOCKS)
            split(link, dst_rows[:], rest, [q_parts[:, :, j, :] for j in range(3)])
            dve.sem_inc(parts_split, 1)
            dve.wait_ge(side_loaded, 32)
            split(link, rel_side[:], split_rest[0:DST_AT, 0:REL_COLS], [rel_parts[:, j, :] for j in range(3)])
            dve.wait_ge(runs_summed, 1)
            link(v.tensor_copy(found[:, 0:WINDOWS + 1], ps[0:1, RUNS_AT:RUNS_AT + WINDOWS + 1]))
            link(v.tensor_scalar(window_at[0:1, 0:WINDOWS], found[:, 0:WINDOWS], float(RUN), None, ALU.mult))
            link(v.tensor_tensor(flag_parts[0:1, 1:2], found[:, 1:2], found[:, 0:1], ALU.subtract))
            span = unsorted[0:1, 0:GROUPS]
            link(v.tensor_tensor(span, found[:, 1:GROUPS + 1], found[:, 0:GROUPS], ALU.subtract))
            link(v.tensor_reduce(flag_parts[0:1, 1:2], span, AX.X, ALU.max))
            link(v.tensor_scalar(flag_parts[0:1, 1:2], flag_parts[0:1, 1:2], WINDOW / RUN - 1.0, None, ALU.is_gt))
            link(v.tensor_tensor(flag_parts[0:1, 2:3], flag_parts[0:1, 1:2], found[:, WINDOWS:WINDOWS + 1], ALU.max))
            link(v.tensor_scalar(flag_parts[0:1, 2:3], flag_parts[0:1, 2:3], 1.0, None, ALU.min))
            link(v.tensor_copy(flags[0:1, 0:1], flag_parts[0:1, 2:3]))
            link(v.tensor_copy(flags[0:1, 1:2], flag_parts[0:1, 2:3]))
            dve.wait_ge(parts_stored, 32)
            dve.wait_ge(rows_stored, 16)
            dve.sem_inc(flag_ready, 1)

            def run_sweep():
                chain = Chain(dve, sweep_steps)
                link, step = chain.link, chain.step
                link(v.memset(side, 0.0))
                link(v.tensor_copy(side[0:DST_AT], rel_parts.unsqueeze(1).to_broadcast([DST_AT, UNROLL, 3, REL_COLS])))
                dve.sem_inc(cleared, 1)
                link(v.memset(square_sums, 0.0))
                link(v.memset(sumsT[:, SPAN:2 * SPAN, :], 0.0))
                dve.sem_inc(score_ready, UNROLL)
                dve.sem_inc(mixed_ready, 1)

                def decode(i, h):
                    own = slice(h * PART, (h + 1) * PART)
                    for u in range(h * PART, (h + 1) * PART):
                        dve.wait_ge(window_in[u], i * 16 + 16)
                    src, dst, rel, after = [window[:, own, :, c] for c in range(EDGE_COLS)]
                    off, hot, pair = dst_off[:, own, :], inside, pair_of[:, own, :]
                    step(v.tensor_scalar(block_of, src, 7, None, ALU.logical_shift_right))
                    step(v.tensor_scalar(row_of, src, P - 1, None, ALU.bitwise_and))
                    step(v.tensor_copy(rel_f[:, own, :], rel))
                    step(v.tensor_tensor(coeff[:, own, :, BASES], dst, after, ALU.not_equal))
                    step(v.tensor_tensor(off, dst, first_dst[:, bass.ds(i * UNROLL + h * PART, PART)].unsqueeze(2)
                                         .to_broadcast([P, PART, SLOTS]), ALU.subtract))
                    chain.wait()
                    step(v.tensor_copy(row_f[:, own, :], row_of))
                    step(v.tensor_scalar(hot, off, 0.0, None, ALU.is_ge))
                    chain.wait()
                    step(v.scalar_tensor_tensor(out=hot, in0=off, scalar=float(GROUP), in1=hot,
                                                op0=ALU.is_lt, op1=ALU.mult))
                    step(v.scalar_tensor_tensor(out=pair, in0=block_of, scalar=float(GROUP), in1=off,
                                                op0=ALU.mult, op1=ALU.add))
                    chain.wait()
                    step(v.scalar_tensor_tensor(out=pair, in0=pair, scalar=1.0, in1=hot, op0=ALU.add, op1=ALU.mult))
                    step(v.scalar_tensor_tensor(out=off, in0=off, scalar=1.0, in1=hot, op0=ALU.add, op1=ALU.mult))
                    chain.wait()
                    n = [P, PART * SLOTS, GROUP]
                    link(v.tensor_tensor(side_hot[:, own, :, DST_AT:SIDE].rearrange("p u k d -> p (u k) d"),
                                         dst_no[:].unsqueeze(1).to_broadcast(n),
                                         off.rearrange("p u k -> p (u k)").unsqueeze(2).to_broadcast(n), ALU.is_equal))
                    dve.sem_inc(decoded, 1)

                def make_side(i, u):
                    s = u % UNROLL
                    n = [P, SLOTS, DST_AT]
                    v.tensor_tensor(side_hot[:, s, :, 0:DST_AT], row_no[:, 0:DST_AT].unsqueeze(1).to_broadcast(n),
                                    rel_f[:, s, :].unsqueeze(2).to_broadcast(n), ALU.is_equal)\
                     .then_inc(side_hot_ready, 1)

                def make_pairs(i, u):
                    s, h = u % UNROLL, u % 2
                    dve.wait_ge(pairs_used, i * UNROLL + (u + 1))
                    for k in range(SLOTS):
                        if k >= ROWS_BY_SCALAR:
                            v.tensor_scalar(row_hot[:, h, k, :], row_no[:], row_f[:, s, k:k + 1], None, ALU.is_equal)
                        last = v.tensor_scalar(pair_hot[:, h, k, :], pair_no[:], pair_of[:, s, k:k + 1], None,
                                               ALU.is_equal)
                    last.then_inc(pairs_ready, 1)

                def score_edges(i, u):
                    dve.wait_ge(per_edge_copied, i * UNROLL + (u + 2))
                    dve.wait_ge(gathered[u], i * (16 * SLOTS) + 16 * SLOTS)
                    link(v.tensor_tensor(product, per_edge[:, u % 2, :, 0:FEAT], xp[:, u % PART, :, FEAT:ROW], ALU.mult))
                    v.tensor_reduce(score[:, u, :], product, AX.X, ALU.add).then_inc(score_ready, 1)

                def make_mixed(i, u):
                    dve.wait_ge(weight_ready, i * UNROLL + (u + 1))
                    n = [P, SLOTS, BASES]
                    link(v.scalar_tensor_tensor(out=coeff[:, u, :, 0:BASES],
                                                in0=weight_e[:, u, :].unsqueeze(2).to_broadcast(n), scalar=0.0,
                                                in1=per_edge[:, u % 2, :, FEAT:REL_COLS], op0=ALU.max, op1=ALU.mult))
                    dve.wait_ge(mixed_used, i * UNROLL + (u + UNROLL - 1))
                    n = [P, SLOTS, GROUP, MIXES]
                    v.tensor_tensor(mixed[:, u % 2], side_hot[:, u, :, DST_AT:SIDE].unsqueeze(3).to_broadcast(n),
                                    coeff[:, u].unsqueeze(2).to_broadcast(n), ALU.mult).then_inc(mixed_ready, 1)

                DECODE_STEPS = 12
                decode(0, 0)
                make_side(0, 0)
                make_side(0, 1)
                make_pairs(0, 0)
                with dve.Fori(0, TURNS) as i:
                    chain.enter(i, TURNS, 2 * DECODE_STEPS + 2 * UNROLL)
                    for u in range(UNROLL):
                        score_edges(i, u)
                        if u + AHEAD == PART:
                            dve.wait_ge(mixed_ready, i * UNROLL + 1)
                            dve.wait_ge(row_hot_ready, i * UNROLL + 1)
                            decode(i, 1)
                        if u + AHEAD == UNROLL:
                            dve.wait_ge(mixed_ready, i * UNROLL + (PART + 1))
                            dve.wait_ge(row_hot_ready, i * UNROLL + (PART + 1))
                            decode(i + 1, 0)
                        make_side(i, u + 2)
                        make_pairs(i, u + 1)
                        make_mixed(i, u)
                    chain.leave()
                dve.wait_ge(moved_copied, 2 * TURNS + 2)
                link(v.tensor_reduce(flag_parts[:, 1:2], square_sums, AX.X, ALU.max))
                link(v.tensor_scalar(flag_parts[:, 0:1], flag_parts[:, 1:2], float(ADJ_MAX ** 2), None, ALU.is_gt))
                dve.sem_inc(flags_counted, 1)
                dve.wait_ge(flags_summed, 1)
                link(v.tensor_scalar(flag_parts[0:1, 3:4], ps[0:1, 0:1], 1.0, None, ALU.min))
                link(v.tensor_copy(flags[0:1, 1:2], flag_parts[0:1, 3:4]))

            def run_dense():
                chain = Chain(dve, dense_steps)
                link = chain.link

                def layer_norm(nth):
                    norm_start(link)
                    dve.sem_inc(d_root_in, 1)
                    dve.wait_ge(d_root_out, nth)
                    norm_end(link)

                def to_agg(cols, nth):
                    dve.wait_ge(layer_nodes, nth)
                    for b in range(0, BLOCKS - 1, PER_BANK):
                        link(v.tensor_copy(agg[:, b:b + PER_BANK, 0:cols], ps_blocks(cols, b, b + PER_BANK)))
                    n = rows_of(BLOCKS - 1)
                    link(v.tensor_copy(agg[0:n, BLOCKS - 1:BLOCKS, 0:cols], ps_blocks(cols, BLOCKS - 1, BLOCKS, n)))

                def chunk_blocks(c):
                    b0 = CHUNKS[c][0] // P
                    return b0, min(b0 + 4, BLOCKS), P if c + 1 < len(CHUNKS) else rows_of(BLOCKS - 1)

                def folded(c, parity, cols):
                    b0, b1, n = chunk_blocks(c)
                    at = (4 + parity) * BANK
                    return ps[0:n, at:at + (b1 - b0) * ROW].rearrange("p (b c) -> p b c", c=ROW)[:, :, 0:cols]

                def split_nodes(half, b0, b1, n, whole, rest):
                    split(link, whole, rest, [parts[0:n, half, b0:b1, j * FEAT:(j + 1) * FEAT] for j in range(3)])
                    dve.sem_inc(parts_ready, 1)

                dve.sem_inc(layer_copied, len(CHUNKS))
                link(v.memset(parts, 0.0))
                link(v.memset(parts[:, :, :, 3 * FEAT:3 * FEAT + 1], 1.0))
                link(v.memset(fold, 0.0))
                for q in range(0, 3 * FEAT, FEAT):
                    link(v.tensor_copy(fold[q:q + FEAT, 0:FEAT], ident[q:q + FEAT, q:q + FEAT]))
                link(v.memset(fold[3 * FEAT:3 * FEAT + 1, FEAT:FEAT + 1], 1.0))
                to_agg(FEAT, 1)
                link(v.tensor_scalar(work[:], agg[:, :, 0:FEAT], 0.0, None, ALU.max))
                link(v.tensor_tensor(x[:], x[:], work[:], ALU.add))
                layer_norm(1)

                for c in range(len(CHUNKS)):
                    b0, b1, _ = chunk_blocks(c)
                    split_nodes(1, b0, b1, P, x[:, b0:b1, :], work[:, b0:b1, :])
                for c in range(len(CHUNKS)):
                    b0, b1, n = chunk_blocks(c)
                    dve.wait_ge(fold_out, c + 1)
                    link(v.tensor_copy(agg[0:n, b0:b1, :], folded(c, (c + len(CHUNKS)) % 2, FEAT + 1)))
                    dve.sem_inc(fold_taken, 1)
                link(v.tensor_scalar(dst_norm[:], agg[:, :, FEAT], 1.0, None, ALU.max))
                link(v.tensor_tensor(x[:], x[:], agg[:, :, 0:FEAT], ALU.add))
                layer_norm(2)

                def own_scores(half, to):
                    w = attn[:, half * FEAT:(half + 1) * FEAT].unsqueeze(1).to_broadcast([P, BLOCKS, FEAT])
                    link(v.tensor_tensor(work[:], x[:], w, ALU.mult))
                    link(v.tensor_reduce(to, work[:], AX.X, ALU.add))

                own_scores(0, s_src)
                link(v.tensor_reduce(spread_of[:, 0:1], s_src, AX.X, ALU.max, apply_absolute_value=True))
                dve.sem_inc(range_in, 1)
                dve.wait_ge(range_out, 1)
                link(v.tensor_scalar(spread_of[:, 2:3], spread_of[:, 1:2], 1e-30, 4.0, ALU.max, ALU.mult))
                link(v.reciprocal(spread_of[:, 3:4], spread_of[:, 2:3]))
                link(v.tensor_scalar(s_max, s_src, spread_of[:, 3:4], 0.75, ALU.mult, ALU.add))
                link(v.tensor_scalar(top, adj[:, 0, 0:NODES], s_max[:, 0:1], None, ALU.min))
                for b in range(1, BLOCKS):
                    link(v.scalar_tensor_tensor(out=top, in0=adj[:, b, 0:NODES], scalar=s_max[:, b:b + 1], in1=top,
                                                op0=ALU.min, op1=ALU.max))
                dve.sem_inc(d_top_ready, 1)
                own_scores(1, s_dst)
                link(v.tensor_scalar(s_src_small, s_src, SLOPE, None, ALU.mult))
                link(v.tensor_copy(agg[:, :, 0:FEAT], x[:]))
                link(v.memset(agg[:, :, FEAT:FEAT + 1], 1.0))
                for c in range(len(CHUNKS)):
                    b0, b1, n = chunk_blocks(c)
                    dve.wait_ge(d_top_out, c + 1)
                    link(v.tensor_reduce(s_max[0:n, b0:b1], ps[0:n, b0 * P:b1 * P].rearrange("p (b c) -> p b c", c=P),
                                         AX.X, ALU.max))
                link(v.tensor_scalar(s_max, s_max, -0.75, spread_of[:, 2:3], ALU.add, ALU.mult))
                link(v.tensor_tensor(s_max, s_max, s_dst, ALU.add))
                link(v.scalar_tensor_tensor(out=s_max, in0=s_max, scalar=SLOPE, in1=s_max, op0=ALU.mult, op1=ALU.max))
                link(v.tensor_tensor(level, s_dst, s_max, ALU.subtract))
                dve.sem_inc(level_ready, 1)
                link(v.scalar_tensor_tensor(out=s_dst, in0=s_dst, scalar=SLOPE, in1=s_max, op0=ALU.mult,
                                            op1=ALU.subtract))
                for b in range(BLOCKS):
                    v.tensor_scalar(diag2[:, b * P:(b + 1) * P], ident[:], s_dst[:, b:b + 1], None, ALU.mult)\
                     .then_inc(diag2_ready, 1)
                for c, (at, w) in enumerate(CHUNKS):
                    dve.wait_ge(row2_out, c + 1)
                    v.tensor_copy(row2[:, at:at + w], ps[:, at:at + w]).then_inc(row2_copied, 1)
                def mask(nth, buf, b, at, w):
                    dve.wait_ge(larger_ready, nth + 1)
                    v.scalar_tensor_tensor(out=exps[:, buf, 1, 0:w], in0=exps[:, buf, 0, 0:w], scalar=1.0,
                                           in1=adj[:, b, at:at + w], op0=ALU.min, op1=ALU.mult)\
                     .then_inc(soft_ready, 1)

                before = None
                for piece in exp_pieces():
                    nth, buf, b, at, w = piece
                    dve.wait_ge(exps_ready, nth + 1)
                    v.tensor_tensor(exps[:, buf, 0, 0:w], exps[:, buf, 0, 0:w], exps[:, buf, 1, 0:w], ALU.max)\
                     .then_inc(larger_ready, 1)
                    if before:
                        mask(*before)
                    before = piece
                mask(*before)
                dve.wait_ge(soft_used, len(PIECES) * BLOCKS)
                for at, w in CHUNKS:
                    v.tensor_copy(aggT[:, at:at + w], ps[0:FEAT + 1, at:at + w]).then_inc(layer_copied, 1)
                to_agg(FEAT + 1, 2)
                link(v.tensor_scalar(stat[:, 0, :], agg[:, :, FEAT], 1e-30, None, ALU.max))
                link(v.reciprocal(stat[:, 1, :], stat[:, 0, :]))
                link(v.tensor_tensor(work[:], agg[:, :, 0:FEAT], spread(stat[:, 1, :], FEAT), ALU.mult))
                link(v.tensor_tensor(x[:], x[:], work[:], ALU.add))
                layer_norm(3)

                dve.wait_ge(degree_out, BLOCKS)
                link(v.tensor_scalar(src_norm[:], src_count, 1.0, None, ALU.max))
                dve.sem_inc(d_root_in, 1)
                dve.wait_ge(d_root_out, 4)
                link(v.reciprocal(stat[:, 0, :], src_norm[:]))
                link(v.tensor_copy(src_norm[:], stat[:, 0, :]))
                link(v.reciprocal(stat[:, 0, :], dst_norm[:]))
                link(v.tensor_scalar(dst_norm[:], stat[:, 0, :], 1.0 - ALPHA, None, ALU.mult))
                link(v.tensor_scalar(x0[:], x[:], ALPHA, None, ALU.mult))
                link(v.tensor_tensor(work[:], x[:], spread(src_norm[:], FEAT), ALU.mult))
                for c in range(len(CHUNKS)):
                    b0, b1, _ = chunk_blocks(c)
                    split_nodes(0, b0, b1, P, work[:, b0:b1, :], fresh[:, 0, 0:b1 - b0, :])

                def propagate(before, half):
                    for c in range(len(CHUNKS)):
                        b0, b1, n = chunk_blocks(c)
                        per_node = [n, b1 - b0, FEAT]
                        new, scaled, rest = work[0:n, b0:b1, :], fresh[0:n, 0, 0:b1 - b0, :], fresh[0:n, 1, 0:b1 - b0, :]
                        dve.wait_ge(fold_out, before + (c + 1))
                        link(v.tensor_tensor(new, folded(c, (c + half * len(CHUNKS)) % 2, FEAT),
                                             dst_norm[0:n, b0:b1].unsqueeze(2).to_broadcast(per_node), ALU.mult))
                        dve.sem_inc(fold_taken, 1)
                        link(v.tensor_tensor(new, new, x0[0:n, b0:b1, :], ALU.add))
                        link(v.tensor_tensor(scaled, new, src_norm[0:n, b0:b1].unsqueeze(2).to_broadcast(per_node),
                                             ALU.mult))
                        split_nodes(1 - half, b0, b1, n, scaled, rest)

                with dve.Fori(0, STEPS // 2) as s:
                    chain.enter(s, STEPS // 2, 2 * 7 * len(CHUNKS))
                    propagate(s * (2 * len(CHUNKS)) + len(CHUNKS), 0)
                    propagate(s * (2 * len(CHUNKS)) + 2 * len(CHUNKS), 1)
                    chain.leave()
                link(v.tensor_tensor(x[:], x[:], work[:], ALU.add))
                layer_norm(5)
                dve.sem_inc(result_ready, 1)

            def run_general():
                chain = Chain(dve, general_steps)
                link = chain.link

                def layer_norm(_, roots):
                    norm_start(link)
                    dve.sem_inc(root_in, 1)
                    dve.wait_ge(root_out, roots)
                    norm_end(link)

                def sums_to_nodes(p, nth):
                    cols = SUM_COLS[p]
                    dve.wait_ge(sums_out, nth)
                    for c, w in CHUNKS:
                        link(v.tensor_copy(aggT[0:cols, c:c + w], ps[0:cols, c:c + w]))
                    dve.sem_inc(sums_copied, 1)
                    dve.wait_ge(nodes_out, nth)
                    for b in range(0, BLOCKS, PER_BANK):
                        e = min(b + PER_BANK, BLOCKS - 1)
                        if e > b:
                            link(v.tensor_copy(agg[:, b:e, 0:cols], ps_blocks(cols, b, e)))
                    n = rows_of(BLOCKS - 1)
                    link(v.tensor_copy(agg[0:n, BLOCKS - 1:BLOCKS, 0:cols], ps_blocks(cols, BLOCKS - 1, BLOCKS, n)))

                def top_to_nodes(nth):
                    dve.sem_inc(top_ready, 1)
                    dve.wait_ge(top_out, nth)
                    for b in range(BLOCKS):
                        n = rows_of(b)
                        link(v.tensor_reduce(stat[0:n, 3, b:b + 1], ps[0:n, b * P:(b + 1) * P], AX.X, ALU.max))
                    dve.sem_inc(top_copied, 1)

                def one_hot():
                    link(v.tensor_copy(score_g[:, 2:3], edge[:, 1:2]))
                    link(v.tensor_scalar(hot[:], node_no[:], score_g[:, 2:3], None, ALU.is_equal))

                link(v.memset(zeros, 0.0))
                link(v.memset(val, 1.0))
                link(v.memset(top_g, 0.0))
                link(v.memset(stat[:], 0.0))
                link(v.memset(agg[:], 0.0))
                dve.wait_ge(general_made, 2)
                dve.wait_ge(embedding_in, 16)
                dve.wait_ge(relations_out, 1)
                for c in range(0, FEAT * FEAT, BANK):
                    link(v.tensor_copy(rel_rows[:, FEAT + c:FEAT + c + BANK], ps[0:RELS, c:c + BANK]))
                dve.sem_inc(table_ready[P_REL], 1)

                with dve.Fori(0, TILES) as t:
                    chain.enter(t, TILES, 12)
                    dve.wait_ge(rows_in[P_REL], t * 48 + 48)
                    link(v.tensor_tensor(prod_g[:, 0, :], dst_row[:], rel_row[:, 0:FEAT], ALU.add))
                    link(v.tensor_tensor(prod_g[:, 0, :], prod_g[:, 0, :], src_row[:, FEAT:ROW], ALU.mult))
                    link(v.tensor_reduce(score_g[:, 3:4], prod_g[:, 0, :], AX.X, ALU.add))
                    link(v.tensor_scalar(score_g[:, 0:1], score_g[:, 3:4], 0.0, None, ALU.max))
                    dve.sem_inc(score_out, 1)
                    link(v.tensor_tensor(prod_g[:], rel_row[:, FEAT:].rearrange("p (i o) -> p o i", o=FEAT),
                                         src_row[:, 0:FEAT].unsqueeze(1).to_broadcast([P, FEAT, FEAT]), ALU.mult))
                    link(v.tensor_reduce(val[:, 0:FEAT], prod_g[:], AX.X, ALU.add))
                    link(v.tensor_scalar(edge_no[:], edge_no[:], float(P), None, ALU.add))
                    one_hot()
                    link(v.scalar_tensor_tensor(out=top_g[:], in0=hot[:], scalar=edge_no[:], in1=top_g[:],
                                                op0=ALU.mult, op1=ALU.max))
                    dve.wait_ge(weight_out, t + 1)
                    link(v.tensor_scalar(val[:, 0:FEAT], val[:, 0:FEAT], score_g[:, 1:2], None, ALU.mult))
                    link(v.tensor_copy(score_g[:, 3:4], score_g[:, 1:2]))
                    dve.sem_inc(tile_ready, 1)
                    chain.leave()
                sums_to_nodes(P_REL, nth_sum[P_REL])
                top_to_nodes(1)
                link(v.tensor_scalar(stat[:, 0, :], stat[:, 3, :], 0.0, None, ALU.is_gt))
                link(v.tensor_scalar(stat[:, 3, :], stat[:, 3, :], -1.0, 0.0, ALU.add, ALU.max))
                link(v.tensor_copy(last_no[:], stat[:, 3, :]))
                dve.sem_inc(last_ready, 1)
                dve.wait_ge(last_in, 16 * BLOCKS)
                link(v.tensor_copy(last_src[:].unsqueeze(2), last_edge[:, :, 0:1]))
                dve.sem_inc(last_ready, 1)
                dve.wait_ge(lastT_out, 1)
                for c in range(0, NODES_PAD, BANK):
                    w = min(BANK, NODES_PAD - c)
                    link(v.tensor_copy(lastT[:, c:c + w], ps[0:FEAT, c:c + w]))
                dve.sem_inc(lastT_ready, 1)
                dve.wait_ge(current_out, 1)
                for b in range(0, BLOCKS, PER_BANK):
                    e = min(b + PER_BANK, BLOCKS)
                    link(v.tensor_tensor(work[:, b:e, :], agg[:, b:e, 0:FEAT], ps_blocks(FEAT, b, e), ALU.add))
                link(v.tensor_scalar(work[:], work[:], 0.0, None, ALU.max))
                link(v.tensor_tensor(work[:], work[:], spread(stat[:, 0, :], FEAT), ALU.mult))
                link(v.tensor_tensor(x[:], x[:], work[:], ALU.add))
                layer_norm(1, 1)
                link(v.tensor_copy(rows[:, :, 0:FEAT], x[:]))
                dve.sem_inc(table_ready[P_SUM], 1)

                def value_tiles(p):
                    with dve.Fori(0, TILES) as t:
                        chain.enter(t, TILES, 3)
                        dve.wait_ge(rows_in[p], t * 16 + 16)
                        link(v.tensor_copy(val[:, 0:FEAT], src_row[:, 0:FEAT]))
                        one_hot()
                        dve.sem_inc(tile_ready, 1)
                        chain.leave()

                value_tiles(P_SUM)
                sums_to_nodes(P_SUM, nth_sum[P_SUM])
                link(v.tensor_scalar(dst_norm[:], agg[:, :, FEAT:FEAT + 1].rearrange("p b c -> p (b c)"), 1.0, None,
                                     ALU.max))
                link(v.tensor_tensor(x[:], x[:], agg[:, :, 0:FEAT], ALU.add))
                layer_norm(2, 2)

                link(v.tensor_copy(rows[:, :, 0:FEAT], x[:]))
                for half, to in ((0, rows[:, :, FEAT:FEAT + 1]), (1, dst_rows[:, :, 0:1])):
                    w = attn[:, half * FEAT:(half + 1) * FEAT].unsqueeze(1).to_broadcast([P, BLOCKS, FEAT])
                    link(v.tensor_tensor(work[:], x[:], w, ALU.mult))
                    link(v.tensor_reduce(to.rearrange("p b c -> p (b c)"), work[:], AX.X, ALU.add))
                link(v.memset(top_g[:], -FAR))
                dve.sem_inc(table_ready[P_MAX], 1)

                def edge_score():
                    link(v.tensor_tensor(score_g[:, 0:1], src_row[:, FEAT:FEAT + 1], dst_row[:, 0:1], ALU.add))
                    link(v.scalar_tensor_tensor(out=score_g[:, 3:4], in0=score_g[:, 0:1], scalar=SLOPE,
                                                in1=score_g[:, 0:1], op0=ALU.mult, op1=ALU.max))

                with dve.Fori(0, TILES) as t:
                    chain.enter(t, TILES, 6)
                    dve.wait_ge(rows_in[P_MAX], t * 32 + 32)
                    edge_score()
                    one_hot()
                    link(v.tensor_scalar(hot[:], hot[:], FAR, -FAR, ALU.mult, ALU.add))
                    link(v.scalar_tensor_tensor(out=top_g[:], in0=hot[:], scalar=score_g[:, 3:4], in1=top_g[:],
                                                op0=ALU.add, op1=ALU.max))
                    dve.sem_inc(tile_done, 1)
                    chain.leave()
                top_to_nodes(2)
                link(v.tensor_copy(dst_rows[:, :, 1:2], stat[:, 3, :].unsqueeze(2)))
                dve.sem_inc(table_ready[P_SOFT], 1)
                with dve.Fori(0, TILES) as t:
                    chain.enter(t, TILES, 7)
                    dve.wait_ge(rows_in[P_SOFT], t * 32 + 32)
                    edge_score()
                    link(v.tensor_tensor(score_g[:, 0:1], score_g[:, 3:4], dst_row[:, 1:2], ALU.subtract))
                    dve.sem_inc(score_out, 1)
                    one_hot()
                    dve.wait_ge(weight_out, t + (TILES + 1))
                    link(v.tensor_scalar(val[:, 0:FEAT], src_row[:, 0:FEAT], score_g[:, 1:2], None, ALU.mult))
                    link(v.tensor_copy(val[:, FEAT:FEAT + 1], score_g[:, 1:2]))
                    dve.sem_inc(tile_ready, 1)
                    chain.leave()
                sums_to_nodes(P_SOFT, nth_sum[P_SOFT])
                link(v.tensor_scalar(stat[:, 0, :], agg[:, :, FEAT:FEAT + 1].rearrange("p b c -> p (b c)"), 1e-30, None,
                                     ALU.max))
                link(v.reciprocal(stat[:, 1, :], stat[:, 0, :]))
                link(v.tensor_tensor(work[:], agg[:, :, 0:FEAT], spread(stat[:, 1, :], FEAT), ALU.mult))
                link(v.tensor_tensor(x[:], x[:], work[:], ALU.add))
                layer_norm(3, 3)
                link(v.memset(val[:], 1.0))
                dve.sem_inc(table_ready[P_OUTDEG], 1)

                with dve.Fori(0, TILES) as t:
                    chain.enter(t, TILES, 2)
                    dve.wait_ge(edge_in, t * 16 + (16 * serial[P_OUTDEG] + 16))
                    link(v.tensor_copy(score_g[:, 2:3], edge[:, 0:1]))
                    link(v.tensor_scalar(hot[:], node_no[:], score_g[:, 2:3], None, ALU.is_equal))
                    dve.sem_inc(tile_ready, 1)
                    chain.leave()
                sums_to_nodes(P_OUTDEG, nth_sum[P_OUTDEG])
                link(v.tensor_scalar(src_norm[:], agg[:, :, 0:1].rearrange("p b c -> p (b c)"), 1.0, None, ALU.max))
                dve.sem_inc(root_in, 1)
                dve.wait_ge(root_out, 5)
                link(v.reciprocal(stat[:, 0, :], src_norm[:]))
                link(v.tensor_copy(src_norm[:], stat[:, 0, :]))
                link(v.reciprocal(stat[:, 0, :], dst_norm[:]))
                link(v.tensor_scalar(dst_norm[:], stat[:, 0, :], 1.0 - ALPHA, None, ALU.mult))
                link(v.tensor_scalar(x0[:], x[:], ALPHA, None, ALU.mult))
                link(v.tensor_copy(work[:], x[:]))
                link(v.tensor_tensor(rows[:, :, 0:FEAT], work[:], spread(src_norm[:], FEAT), ALU.mult))
                dve.sem_inc(table_ready[P_PROP], 1)
                PER_STEP = 3 * TILES + len(CHUNKS) + 4 + 3
                with dve.Fori(0, STEPS) as s:
                    chain.enter(s, STEPS, PER_STEP)
                    dve.wait_ge(rows_in_cleared, s + 1)
                    dve.sem_inc(vector_turns, 1)
                    value_tiles(P_PROP)
                    sums_to_nodes(P_PROP, s + nth_sum[P_PROP])
                    link(v.tensor_tensor(work[:], agg[:, :, 0:FEAT], spread(dst_norm[:], FEAT), ALU.mult))
                    link(v.tensor_tensor(work[:], work[:], x0[:], ALU.add))
                    link(v.tensor_tensor(rows[:, :, 0:FEAT], work[:], spread(src_norm[:], FEAT), ALU.mult))
                    dve.sem_inc(table_ready[P_PROP], 1)
                    chain.leave()
                link(v.tensor_tensor(x[:], x[:], work[:], ALU.add))
                layer_norm(5, 6)
                dve.sem_inc(result_ready, 1)
            with dve.If(dve.value_load(flags[0:1, 0:1], min_val=0, max_val=1) == 0):
                run_sweep()
            dve.sem_inc(flag_ready, 1)
            with dve.If(dve.value_load(flags[0:1, 1:2], min_val=0, max_val=1) == 0):
                run_dense()
            with dve.Else():
                run_general()


def kernel(**inputs):
    import numpy as np
    import concourse.bacc as bacc
    from concourse.bass_utils import run_bass_kernel_spmd

    x = np.asarray(inputs["x"])
    x_pad = np.zeros((NODES_PAD, FEAT), x.dtype)
    x_pad[:NODES] = x
    edges = np.zeros((EDGES_PAD, EDGE_COLS), np.int32)
    edges[EDGES:, 0:2] = NOWHERE
    for c, name in enumerate(("src", "dst", "edge_type_86")):
        edges[:EDGES, c] = np.asarray(inputs[name])
    edges[:-1, 3] = edges[1:, 1]
    edges[-1, 3] = NOWHERE

    def with_bias(w, b):
        return np.concatenate([np.asarray(inputs[w]).T, np.asarray(inputs[b])[None]], 0)

    arrays = {
        "x_pad": x_pad, "edges": edges,
        "weight": np.asarray(inputs["L0_gnn_weight"]).reshape(BASES, FEAT * FEAT),
        "w_comp": np.asarray(inputs["L0_gnn_w_comp"]),
        "w_comp_t": np.asarray(inputs["L0_gnn_w_comp"]).T,
        "self_loop": np.asarray(inputs["L0_gnn_self_loop_weight"]),
        "a1_t": with_bias("L0_gnn_A1_w", "L0_gnn_A1_b"), "a2_t": with_bias("L0_gnn_A2_w", "L0_gnn_A2_b"),
        "rel_emb": np.asarray(inputs["L0_gnn_rel_emb"]),
        "attn_w": np.asarray(inputs["L2_gnn_attn_w"])[None],
    }
    arrays = {k: np.ascontiguousarray(a) for k, a in arrays.items()}
    nc = bacc.Bacc("TRN2", target_bir_lowering=False, num_devices=1)
    aps = {k: nc.dram_tensor(k, a.shape, mybir.dt.from_np(a.dtype), kind="ExternalInput").ap()
           for k, a in arrays.items()}
    out = nc.dram_tensor("out", [NODES_PAD, FEAT], F32, kind="ExternalOutput").ap()
    gnn(nc, out=out, **aps)
    r = run_bass_kernel_spmd(nc, [arrays], core_ids=[0])
    return r.results[0]["out"][:NODES]
```
